# Optimizing a Trainium2 kernel written in Bass

```python
import numpy as np
import jax
import jax.numpy as jnp

def _softmax(x, axis=-1):
    return jax.nn.softmax(x, axis=axis)

def _gelu(x):
    return jax.nn.gelu(x, approximate=True)

def _silu(x):
    return jax.nn.silu(x)

def _sigmoid(x):
    return jax.nn.sigmoid(x)

def _layernorm(x, axis=-1, eps=1e-05):
    m = jnp.mean(x, axis=axis, keepdims=True)
    v = jnp.var(x, axis=axis, keepdims=True)
    return (x - m) / jnp.sqrt(v + eps)

def _scatter_add(tgt, idx, src, axis=0):
    return tgt.at[idx].add(src)

def _segment_sum(src, seg, n):
    return jax.ops.segment_sum(src, seg, n)
kernel_name = 'mk_adaln_attn_ffn_d2_seqx_r8_d90096'

def setup_inputs(seed: int=0):
    np.random.seed(seed)
    _w = jnp.asarray

    def _rec_inputs():
        import jax
        import jax.numpy as jnp
        _rk = jax.random.key(seed)
        x = -0.0003929 + 0.9999 * jax.random.normal(jax.random.fold_in(_rk, 1), (128, 32, 512), jnp.float32)
        _lenS = 32 - jax.random.randint(jax.random.fold_in(_rk, 7), (128,), 0, max(1, 32 // 4) + 1, jnp.int32)
        _lenS2 = 32 - jax.random.randint(jax.random.fold_in(_rk, 8), (128,), 0, max(1, 32 // 4) + 1, jnp.int32)
        cond_512 = 0.00782532 + 1.00527 * jax.random.normal(jax.random.fold_in(_rk, 11), (128, 64), jnp.float32)
        return (x, cond_512)
    x, cond_512 = _rec_inputs()

    def _L0_cond_setup():
        import jax, jax.numpy as jnp
        from jax import lax
        import numpy as np
        CIN, COUT, K, STYLE_DIM = (32, 32, 3, 64)
        N_LAYERS = 4
        TYPES = ('same', 'upsample', 'same', 'downsample')
        SCALE = 1.0 / float(np.sqrt(CIN * K ** 2))
        EPS = 1e-08
        _BK = np.array([1.0, 3.0, 3.0, 1.0], dtype=np.float32)
        BLUR_K = _BK / _BK.sum()

        def _blur(x, kern, pad):
            B, C, _ = x.shape
            xp = jnp.pad(x, ((0, 0), (0, 0), (pad[0], pad[1])))
            w = jnp.broadcast_to(kern.astype(x.dtype)[None, None, :], (C, 1, kern.shape[0]))
            return lax.conv_general_dilated(xp, w, (1,), 'VALID', feature_group_count=C, dimension_numbers=('NCH', 'OIH', 'NCH'))

        def _conv_same(x, w):
            p = (K - 1) // 2
            return lax.conv_general_dilated(x[None], w, (1,), [(p, p)], dimension_numbers=('NCH', 'OIH', 'NCH'))[0]

        def _conv_down(x, w):
            return lax.conv_general_dilated(x[None], w, (2,), 'VALID', dimension_numbers=('NCH', 'OIH', 'NCH'))[0]

        def _conv_up(x, w_t):
            return lax.conv_transpose(x[None], w_t, (2,), 'VALID', dimension_numbers=('NCH', 'IOH', 'NCH'), transpose_kernel=True)[0]

        def _layer(x, style, w, b, mw, mb, typ):
            s = style @ mw.T + mb
            weight = SCALE * w * s[:, None, :, None]
            demod = lax.rsqrt(jnp.sum(weight * weight, axis=(2, 3)) + EPS)
            weight = weight * demod[:, :, None, None]
            blur_k = jnp.asarray(BLUR_K)
            if typ == 'same':
                out = jax.vmap(_conv_same)(x, weight) + b[None, :, None]
            elif typ == 'upsample':
                out = jax.vmap(_conv_up)(x, weight.transpose(0, 2, 1, 3)) + b[None, :, None]
                out = _blur(out, 2.0 * blur_k, (1, 1))
            elif typ == 'downsample':
                xb = _blur(x, blur_k, (2, 2))
                out = jax.vmap(_conv_down)(xb, weight) + b[None, :, None]
            else:
                raise NotImplementedError(typ)
            return out
        key = jax.random.key(seed)
        ks = jax.random.split(key, 6)
        B, L = (16, 512)
        return {'x': jax.random.normal(ks[0], (B, CIN, L), dtype=jnp.float32), 'style': jax.random.normal(ks[1], (B, STYLE_DIM), dtype=jnp.float32), 'weights': jax.random.normal(ks[2], (N_LAYERS, COUT, CIN, K), dtype=jnp.float32), 'biases': jax.random.normal(ks[3], (N_LAYERS, COUT), dtype=jnp.float32) * 0.1, 'mod_w': jax.random.normal(ks[4], (N_LAYERS, CIN, STYLE_DIM), dtype=jnp.float32) / np.sqrt(STYLE_DIM), 'mod_b': 1.0 + 0.1 * jax.random.normal(ks[5], (N_LAYERS, CIN), dtype=jnp.float32)}
    _L0_cond_all = _L0_cond_setup()
    _L0_cond_in = {k: v for k, v in _L0_cond_all.items() if k in ('weights', 'biases', 'mod_w', 'mod_b')}
    del _L0_cond_all

    def _L0_attn_setup():
        import jax, jax.numpy as jnp
        import numpy as np
        HIDDEN = 512
        NUM_HEADS = 32
        HEAD_DIM = HIDDEN // NUM_HEADS

        def _fp8_roundtrip(x):
            return x.astype(jnp.float8_e4m3fn).astype(jnp.float32)
        key = jax.random.key(seed)
        ks = jax.random.split(key, 10)
        B, S = (2, 512)
        hidden_states = jax.random.normal(ks[0], (B, S, HIDDEN), dtype=jnp.float32)
        scale = 0.02

        def lin(kw, kb):
            w = jax.random.normal(kw, (HIDDEN, HIDDEN), dtype=jnp.float32) * scale
            b = jax.random.normal(kb, (HIDDEN,), dtype=jnp.float32) * scale
            return (w, b)
        wq, bq = lin(ks[1], ks[2])
        wk, bk = lin(ks[3], ks[4])
        wv, bv = lin(ks[5], ks[6])
        wl, bl = lin(ks[7], ks[8])
        wq, bq = (_fp8_roundtrip(wq), _fp8_roundtrip(bq))
        wk, bk = (_fp8_roundtrip(wk), _fp8_roundtrip(bk))
        wv, bv = (_fp8_roundtrip(wv), _fp8_roundtrip(bv))
        return {'hidden_states': hidden_states, 'wq': wq, 'bq': bq, 'wk': wk, 'bk': bk, 'wv': wv, 'bv': bv, 'wl': wl, 'bl': bl}
    _L0_attn_all = _L0_attn_setup()
    _L0_attn_in = {k: v for k, v in _L0_attn_all.items() if k in ('wq', 'bq', 'wk', 'bk', 'wv', 'bv', 'wl', 'bl')}
    del _L0_attn_all

    def _L0_cond2_setup():
        import jax, jax.numpy as jnp
        from jax import lax
        import numpy as np
        CIN, COUT, K, STYLE_DIM = (32, 32, 3, 64)
        N_LAYERS = 4
        TYPES = ('same', 'upsample', 'same', 'downsample')
        SCALE = 1.0 / float(np.sqrt(CIN * K ** 2))
        EPS = 1e-08
        _BK = np.array([1.0, 3.0, 3.0, 1.0], dtype=np.float32)
        BLUR_K = _BK / _BK.sum()

        def _blur(x, kern, pad):
            B, C, _ = x.shape
            xp = jnp.pad(x, ((0, 0), (0, 0), (pad[0], pad[1])))
            w = jnp.broadcast_to(kern.astype(x.dtype)[None, None, :], (C, 1, kern.shape[0]))
            return lax.conv_general_dilated(xp, w, (1,), 'VALID', feature_group_count=C, dimension_numbers=('NCH', 'OIH', 'NCH'))

        def _conv_same(x, w):
            p = (K - 1) // 2
            return lax.conv_general_dilated(x[None], w, (1,), [(p, p)], dimension_numbers=('NCH', 'OIH', 'NCH'))[0]

        def _conv_down(x, w):
            return lax.conv_general_dilated(x[None], w, (2,), 'VALID', dimension_numbers=('NCH', 'OIH', 'NCH'))[0]

        def _conv_up(x, w_t):
            return lax.conv_transpose(x[None], w_t, (2,), 'VALID', dimension_numbers=('NCH', 'IOH', 'NCH'), transpose_kernel=True)[0]

        def _layer(x, style, w, b, mw, mb, typ):
            s = style @ mw.T + mb
            weight = SCALE * w * s[:, None, :, None]
            demod = lax.rsqrt(jnp.sum(weight * weight, axis=(2, 3)) + EPS)
            weight = weight * demod[:, :, None, None]
            blur_k = jnp.asarray(BLUR_K)
            if typ == 'same':
                out = jax.vmap(_conv_same)(x, weight) + b[None, :, None]
            elif typ == 'upsample':
                out = jax.vmap(_conv_up)(x, weight.transpose(0, 2, 1, 3)) + b[None, :, None]
                out = _blur(out, 2.0 * blur_k, (1, 1))
            elif typ == 'downsample':
                xb = _blur(x, blur_k, (2, 2))
                out = jax.vmap(_conv_down)(xb, weight) + b[None, :, None]
            else:
                raise NotImplementedError(typ)
            return out
        key = jax.random.key(seed)
        ks = jax.random.split(key, 6)
        B, L = (16, 512)
        return {'x': jax.random.normal(ks[0], (B, CIN, L), dtype=jnp.float32), 'style': jax.random.normal(ks[1], (B, STYLE_DIM), dtype=jnp.float32), 'weights': jax.random.normal(ks[2], (N_LAYERS, COUT, CIN, K), dtype=jnp.float32), 'biases': jax.random.normal(ks[3], (N_LAYERS, COUT), dtype=jnp.float32) * 0.1, 'mod_w': jax.random.normal(ks[4], (N_LAYERS, CIN, STYLE_DIM), dtype=jnp.float32) / np.sqrt(STYLE_DIM), 'mod_b': 1.0 + 0.1 * jax.random.normal(ks[5], (N_LAYERS, CIN), dtype=jnp.float32)}
    _L0_cond2_all = _L0_cond2_setup()
    _L0_cond2_in = {k: v for k, v in _L0_cond2_all.items() if k in ('weights', 'biases', 'mod_w', 'mod_b')}
    del _L0_cond2_all

    def _L0_ffn_setup():
        import jax, jax.numpy as jnp
        import numpy as np
        B, S, D, O, E, R = (4, 256, 512, 512, 8, 16)
        SCALING = 32.0 / 16.0
        MAX_THRESHOLD = 0.125
        key = jax.random.key(seed)
        ks = jax.random.split(key, 8)
        return {'x': jax.random.normal(ks[0], (B, S, D), jnp.float32), 'W_base': jax.random.normal(ks[1], (O, D), jnp.float32) * (1.0 / np.sqrt(D)), 'b_base': jax.random.normal(ks[2], (O,), jnp.float32) * 0.02, 'W_gate': jax.random.normal(ks[3], (E, D), jnp.float32) * (1.0 / np.sqrt(D)), 'W_thr': jax.random.normal(ks[4], (D,), jnp.float32) * (1.0 / np.sqrt(D)), 'b_thr': jax.random.normal(ks[5], (1,), jnp.float32) * 0.02, 'A_w': jax.random.normal(ks[6], (E, R, D), jnp.float32) * (1.0 / np.sqrt(D)), 'B_w': jax.random.normal(ks[7], (E, O, R), jnp.float32) * (1.0 / np.sqrt(R))}
    _L0_ffn_all = _L0_ffn_setup()
    _L0_ffn_in = {k: v for k, v in _L0_ffn_all.items() if k in ('W_base', 'b_base', 'W_gate', 'W_thr', 'b_thr', 'A_w', 'B_w')}
    del _L0_ffn_all

    def _L1_cond_setup():
        import jax, jax.numpy as jnp
        from jax import lax
        import numpy as np
        CIN, COUT, K, STYLE_DIM = (32, 32, 3, 64)
        N_LAYERS = 4
        TYPES = ('same', 'upsample', 'same', 'downsample')
        SCALE = 1.0 / float(np.sqrt(CIN * K ** 2))
        EPS = 1e-08
        _BK = np.array([1.0, 3.0, 3.0, 1.0], dtype=np.float32)
        BLUR_K = _BK / _BK.sum()

        def _blur(x, kern, pad):
            B, C, _ = x.shape
            xp = jnp.pad(x, ((0, 0), (0, 0), (pad[0], pad[1])))
            w = jnp.broadcast_to(kern.astype(x.dtype)[None, None, :], (C, 1, kern.shape[0]))
            return lax.conv_general_dilated(xp, w, (1,), 'VALID', feature_group_count=C, dimension_numbers=('NCH', 'OIH', 'NCH'))

        def _conv_same(x, w):
            p = (K - 1) // 2
            return lax.conv_general_dilated(x[None], w, (1,), [(p, p)], dimension_numbers=('NCH', 'OIH', 'NCH'))[0]

        def _conv_down(x, w):
            return lax.conv_general_dilated(x[None], w, (2,), 'VALID', dimension_numbers=('NCH', 'OIH', 'NCH'))[0]

        def _conv_up(x, w_t):
            return lax.conv_transpose(x[None], w_t, (2,), 'VALID', dimension_numbers=('NCH', 'IOH', 'NCH'), transpose_kernel=True)[0]

        def _layer(x, style, w, b, mw, mb, typ):
            s = style @ mw.T + mb
            weight = SCALE * w * s[:, None, :, None]
            demod = lax.rsqrt(jnp.sum(weight * weight, axis=(2, 3)) + EPS)
            weight = weight * demod[:, :, None, None]
            blur_k = jnp.asarray(BLUR_K)
            if typ == 'same':
                out = jax.vmap(_conv_same)(x, weight) + b[None, :, None]
            elif typ == 'upsample':
                out = jax.vmap(_conv_up)(x, weight.transpose(0, 2, 1, 3)) + b[None, :, None]
                out = _blur(out, 2.0 * blur_k, (1, 1))
            elif typ == 'downsample':
                xb = _blur(x, blur_k, (2, 2))
                out = jax.vmap(_conv_down)(xb, weight) + b[None, :, None]
            else:
                raise NotImplementedError(typ)
            return out
        key = jax.random.key(seed)
        ks = jax.random.split(key, 6)
        B, L = (16, 512)
        return {'x': jax.random.normal(ks[0], (B, CIN, L), dtype=jnp.float32), 'style': jax.random.normal(ks[1], (B, STYLE_DIM), dtype=jnp.float32), 'weights': jax.random.normal(ks[2], (N_LAYERS, COUT, CIN, K), dtype=jnp.float32), 'biases': jax.random.normal(ks[3], (N_LAYERS, COUT), dtype=jnp.float32) * 0.1, 'mod_w': jax.random.normal(ks[4], (N_LAYERS, CIN, STYLE_DIM), dtype=jnp.float32) / np.sqrt(STYLE_DIM), 'mod_b': 1.0 + 0.1 * jax.random.normal(ks[5], (N_LAYERS, CIN), dtype=jnp.float32)}
    _L1_cond_all = _L1_cond_setup()
    _L1_cond_in = {k: v for k, v in _L1_cond_all.items() if k in ('weights', 'biases', 'mod_w', 'mod_b')}
    del _L1_cond_all

    def _L1_attn_setup():
        import jax, jax.numpy as jnp
        import numpy as np
        B, S, D = (1, 256, 512)
        H = 32
        Q_RANK, KV_RANK = (192, 64)
        NOPE, ROPE, VD = (128, 64, 128)
        QD = NOPE + ROPE
        EPS = 1e-06
        THETA = 10000.0

        def _rmsnorm(x, w):
            return x * jax.lax.rsqrt(jnp.mean(x * x, axis=-1, keepdims=True) + EPS) * w

        def _rotate_half(x):
            h = x.shape[-1] // 2
            return jnp.concatenate([-x[..., h:], x[..., :h]], axis=-1)

        def _apply_rope(x, cos, sin):
            xp = jnp.concatenate([x[..., 0::2], x[..., 1::2]], axis=-1)
            return xp * cos + _rotate_half(xp) * sin

        def _mla_forward(hidden_states, Wq_a, q_a_ln_w, Wq_b, Wkv_a, kv_a_ln_w, Wkv_b, Wo):
            b, s, _ = hidden_states.shape
            q = _rmsnorm(hidden_states @ Wq_a, q_a_ln_w) @ Wq_b
            q = q.reshape(b, s, H, QD).transpose(0, 2, 1, 3)
            q_nope, q_pe = (q[..., :NOPE], q[..., NOPE:])
            ckv = hidden_states @ Wkv_a
            compressed, k_pe = (ckv[..., :KV_RANK], ckv[..., KV_RANK:])
            kv = _rmsnorm(compressed, kv_a_ln_w) @ Wkv_b
            kv = kv.reshape(b, s, H, NOPE + VD).transpose(0, 2, 1, 3)
            k_nope, v = (kv[..., :NOPE], kv[..., NOPE:])
            k_pe = k_pe[:, None, :, :]
            inv_freq = 1.0 / THETA ** (jnp.arange(0, ROPE, 2, dtype=jnp.float32) / ROPE)
            freqs = jnp.outer(jnp.arange(s, dtype=jnp.float32), inv_freq)
            emb = jnp.concatenate([freqs, freqs], axis=-1)
            cos = jnp.cos(emb)[None, None].astype(hidden_states.dtype)
            sin = jnp.sin(emb)[None, None].astype(hidden_states.dtype)
            q_pe = _apply_rope(q_pe, cos, sin)
            k_pe = _apply_rope(k_pe, cos, sin)
            qf = jnp.concatenate([q_nope, q_pe], axis=-1)
            kf = jnp.concatenate([k_nope, jnp.broadcast_to(k_pe, (b, H, s, ROPE))], axis=-1)
            scale = QD ** (-0.5)
            scores = jnp.einsum('bhqd,bhkd->bhqk', qf, kf) * scale
            causal = jnp.tril(jnp.ones((s, s), dtype=bool))
            scores = jnp.where(causal, scores, jnp.finfo(scores.dtype).min)
            probs = jax.nn.softmax(scores, axis=-1)
            o = jnp.einsum('bhqk,bhkd->bhqd', probs, v)
            o = o.transpose(0, 2, 1, 3).reshape(b, s, H * VD)
            return o @ Wo
        key = jax.random.key(seed)
        ks = jax.random.split(key, 8)
        std = 0.02
        return {'hidden_states': jax.random.normal(ks[0], (B, S, D), jnp.float32), 'Wq_a': jax.random.normal(ks[1], (D, Q_RANK), jnp.float32) * std, 'q_a_ln_w': jnp.ones((Q_RANK,), jnp.float32), 'Wq_b': jax.random.normal(ks[2], (Q_RANK, H * QD), jnp.float32) * std, 'Wkv_a': jax.random.normal(ks[3], (D, KV_RANK + ROPE), jnp.float32) * std, 'kv_a_ln_w': jnp.ones((KV_RANK,), jnp.float32), 'Wkv_b': jax.random.normal(ks[4], (KV_RANK, H * (NOPE + VD)), jnp.float32) * std, 'Wo': jax.random.normal(ks[5], (H * VD, D), jnp.float32) * std}
    _L1_attn_all = _L1_attn_setup()
    _L1_attn_in = {k: v for k, v in _L1_attn_all.items() if k in ('Wq_a', 'q_a_ln_w', 'Wq_b', 'Wkv_a', 'kv_a_ln_w', 'Wkv_b', 'Wo')}
    del _L1_attn_all

    def _L1_cond2_setup():
        import jax, jax.numpy as jnp
        from jax import lax
        import numpy as np
        CIN, COUT, K, STYLE_DIM = (32, 32, 3, 64)
        N_LAYERS = 4
        TYPES = ('same', 'upsample', 'same', 'downsample')
        SCALE = 1.0 / float(np.sqrt(CIN * K ** 2))
        EPS = 1e-08
        _BK = np.array([1.0, 3.0, 3.0, 1.0], dtype=np.float32)
        BLUR_K = _BK / _BK.sum()

        def _blur(x, kern, pad):
            B, C, _ = x.shape
            xp = jnp.pad(x, ((0, 0), (0, 0), (pad[0], pad[1])))
            w = jnp.broadcast_to(kern.astype(x.dtype)[None, None, :], (C, 1, kern.shape[0]))
            return lax.conv_general_dilated(xp, w, (1,), 'VALID', feature_group_count=C, dimension_numbers=('NCH', 'OIH', 'NCH'))

        def _conv_same(x, w):
            p = (K - 1) // 2
            return lax.conv_general_dilated(x[None], w, (1,), [(p, p)], dimension_numbers=('NCH', 'OIH', 'NCH'))[0]

        def _conv_down(x, w):
            return lax.conv_general_dilated(x[None], w, (2,), 'VALID', dimension_numbers=('NCH', 'OIH', 'NCH'))[0]

        def _conv_up(x, w_t):
            return lax.conv_transpose(x[None], w_t, (2,), 'VALID', dimension_numbers=('NCH', 'IOH', 'NCH'), transpose_kernel=True)[0]

        def _layer(x, style, w, b, mw, mb, typ):
            s = style @ mw.T + mb
            weight = SCALE * w * s[:, None, :, None]
            demod = lax.rsqrt(jnp.sum(weight * weight, axis=(2, 3)) + EPS)
            weight = weight * demod[:, :, None, None]
            blur_k = jnp.asarray(BLUR_K)
            if typ == 'same':
                out = jax.vmap(_conv_same)(x, weight) + b[None, :, None]
            elif typ == 'upsample':
                out = jax.vmap(_conv_up)(x, weight.transpose(0, 2, 1, 3)) + b[None, :, None]
                out = _blur(out, 2.0 * blur_k, (1, 1))
            elif typ == 'downsample':
                xb = _blur(x, blur_k, (2, 2))
                out = jax.vmap(_conv_down)(xb, weight) + b[None, :, None]
            else:
                raise NotImplementedError(typ)
            return out
        key = jax.random.key(seed)
        ks = jax.random.split(key, 6)
        B, L = (16, 512)
        return {'x': jax.random.normal(ks[0], (B, CIN, L), dtype=jnp.float32), 'style': jax.random.normal(ks[1], (B, STYLE_DIM), dtype=jnp.float32), 'weights': jax.random.normal(ks[2], (N_LAYERS, COUT, CIN, K), dtype=jnp.float32), 'biases': jax.random.normal(ks[3], (N_LAYERS, COUT), dtype=jnp.float32) * 0.1, 'mod_w': jax.random.normal(ks[4], (N_LAYERS, CIN, STYLE_DIM), dtype=jnp.float32) / np.sqrt(STYLE_DIM), 'mod_b': 1.0 + 0.1 * jax.random.normal(ks[5], (N_LAYERS, CIN), dtype=jnp.float32)}
    _L1_cond2_all = _L1_cond2_setup()
    _L1_cond2_in = {k: v for k, v in _L1_cond2_all.items() if k in ('weights', 'biases', 'mod_w', 'mod_b')}
    del _L1_cond2_all

    def _L1_ffn_setup():
        import jax, jax.numpy as jnp
        import numpy as np
        import math
        D = 512
        TOKENS = (4, 256)
        P = 0.8

        def conn_dense(kernel, x):
            w = jnp.where(kernel, jnp.asarray(1.0, x.dtype), jnp.asarray(-1.0, x.dtype))
            return x @ w

        def ei_dense(x, kernel, scale, p):
            in_dim = x.shape[-1]
            ne = round(in_dim * p)
            x_exc = x[..., :ne]
            x_inh = x[..., ne:]
            xx = jnp.concatenate([x_exc, -p / (1.0 - p) * x_inh], axis=-1)
            return scale * conn_dense(kernel, xx)
        key = jax.random.key(seed)
        ks = jax.random.split(key, 4)
        x = jax.random.normal(ks[0], (*TOKENS, D), dtype=jnp.float32)
        k0 = jax.random.bernoulli(ks[1], 0.5, (D, D))
        k1 = jax.random.bernoulli(ks[2], 0.5, (D, D))
        k2 = jax.random.bernoulli(ks[3], 0.5, (D, D))
        s = jnp.asarray(1.0 / math.sqrt(D), dtype=jnp.float32)
        return {'x': x, 'k0': k0, 's0': s, 'k1': k1, 's1': s, 'k2': k2, 's2': s}
    _L1_ffn_all = _L1_ffn_setup()
    _L1_ffn_in = {k: v for k, v in _L1_ffn_all.items() if k in ('k0', 's0', 'k1', 's1', 'k2', 's2')}
    del _L1_ffn_all
    return {'x': x, 'cond_512': cond_512, 'L0_cond_weights': _L0_cond_in['weights'], 'L0_cond_biases': _L0_cond_in['biases'], 'L0_cond_mod_w': _L0_cond_in['mod_w'], 'L0_cond_mod_b': _L0_cond_in['mod_b'], 'L0_attn_wq': _L0_attn_in['wq'], 'L0_attn_bq': _L0_attn_in['bq'], 'L0_attn_wk': _L0_attn_in['wk'], 'L0_attn_bk': _L0_attn_in['bk'], 'L0_attn_wv': _L0_attn_in['wv'], 'L0_attn_bv': _L0_attn_in['bv'], 'L0_attn_wl': _L0_attn_in['wl'], 'L0_attn_bl': _L0_attn_in['bl'], 'L0_cond2_weights': _L0_cond2_in['weights'], 'L0_cond2_biases': _L0_cond2_in['biases'], 'L0_cond2_mod_w': _L0_cond2_in['mod_w'], 'L0_cond2_mod_b': _L0_cond2_in['mod_b'], 'L0_ffn_W_base': _L0_ffn_in['W_base'], 'L0_ffn_b_base': _L0_ffn_in['b_base'], 'L0_ffn_W_gate': _L0_ffn_in['W_gate'], 'L0_ffn_W_thr': _L0_ffn_in['W_thr'], 'L0_ffn_b_thr': _L0_ffn_in['b_thr'], 'L0_ffn_A_w': _L0_ffn_in['A_w'], 'L0_ffn_B_w': _L0_ffn_in['B_w'], 'L1_cond_weights': _L1_cond_in['weights'], 'L1_cond_biases': _L1_cond_in['biases'], 'L1_cond_mod_w': _L1_cond_in['mod_w'], 'L1_cond_mod_b': _L1_cond_in['mod_b'], 'L1_attn_Wq_a': _L1_attn_in['Wq_a'], 'L1_attn_q_a_ln_w': _L1_attn_in['q_a_ln_w'], 'L1_attn_Wq_b': _L1_attn_in['Wq_b'], 'L1_attn_Wkv_a': _L1_attn_in['Wkv_a'], 'L1_attn_kv_a_ln_w': _L1_attn_in['kv_a_ln_w'], 'L1_attn_Wkv_b': _L1_attn_in['Wkv_b'], 'L1_attn_Wo': _L1_attn_in['Wo'], 'L1_cond2_weights': _L1_cond2_in['weights'], 'L1_cond2_biases': _L1_cond2_in['biases'], 'L1_cond2_mod_w': _L1_cond2_in['mod_w'], 'L1_cond2_mod_b': _L1_cond2_in['mod_b'], 'L1_ffn_k0': _L1_ffn_in['k0'], 'L1_ffn_s0': _L1_ffn_in['s0'], 'L1_ffn_k1': _L1_ffn_in['k1'], 'L1_ffn_s1': _L1_ffn_in['s1'], 'L1_ffn_k2': _L1_ffn_in['k2'], 'L1_ffn_s2': _L1_ffn_in['s2']}

def reference(x, cond_512, L0_cond_weights, L0_cond_biases, L0_cond_mod_w, L0_cond_mod_b, L0_attn_wq, L0_attn_bq, L0_attn_wk, L0_attn_bk, L0_attn_wv, L0_attn_bv, L0_attn_wl, L0_attn_bl, L0_cond2_weights, L0_cond2_biases, L0_cond2_mod_w, L0_cond2_mod_b, L0_ffn_W_base, L0_ffn_b_base, L0_ffn_W_gate, L0_ffn_W_thr, L0_ffn_b_thr, L0_ffn_A_w, L0_ffn_B_w, L1_cond_weights, L1_cond_biases, L1_cond_mod_w, L1_cond_mod_b, L1_attn_Wq_a, L1_attn_q_a_ln_w, L1_attn_Wq_b, L1_attn_Wkv_a, L1_attn_kv_a_ln_w, L1_attn_Wkv_b, L1_attn_Wo, L1_cond2_weights, L1_cond2_biases, L1_cond2_mod_w, L1_cond2_mod_b, L1_ffn_k0, L1_ffn_s0, L1_ffn_k1, L1_ffn_s1, L1_ffn_k2, L1_ffn_s2):
    import jax
    import jax.numpy as jnp

    def _L0_cond_ref(x, style, weights, biases, mod_w, mod_b):
        import jax, jax.numpy as jnp
        from jax import lax
        import numpy as np
        CIN, COUT, K, STYLE_DIM = (32, 32, 3, 64)
        N_LAYERS = 4
        TYPES = ('same', 'upsample', 'same', 'downsample')
        SCALE = 1.0 / float(np.sqrt(CIN * K ** 2))
        EPS = 1e-08
        _BK = np.array([1.0, 3.0, 3.0, 1.0], dtype=np.float32)
        BLUR_K = _BK / _BK.sum()

        def _blur(x, kern, pad):
            B, C, _ = x.shape
            xp = jnp.pad(x, ((0, 0), (0, 0), (pad[0], pad[1])))
            w = jnp.broadcast_to(kern.astype(x.dtype)[None, None, :], (C, 1, kern.shape[0]))
            return lax.conv_general_dilated(xp, w, (1,), 'VALID', feature_group_count=C, dimension_numbers=('NCH', 'OIH', 'NCH'))

        def _conv_same(x, w):
            p = (K - 1) // 2
            return lax.conv_general_dilated(x[None], w, (1,), [(p, p)], dimension_numbers=('NCH', 'OIH', 'NCH'))[0]

        def _conv_down(x, w):
            return lax.conv_general_dilated(x[None], w, (2,), 'VALID', dimension_numbers=('NCH', 'OIH', 'NCH'))[0]

        def _conv_up(x, w_t):
            return lax.conv_transpose(x[None], w_t, (2,), 'VALID', dimension_numbers=('NCH', 'IOH', 'NCH'), transpose_kernel=True)[0]

        def _layer(x, style, w, b, mw, mb, typ):
            s = style @ mw.T + mb
            weight = SCALE * w * s[:, None, :, None]
            demod = lax.rsqrt(jnp.sum(weight * weight, axis=(2, 3)) + EPS)
            weight = weight * demod[:, :, None, None]
            blur_k = jnp.asarray(BLUR_K)
            if typ == 'same':
                out = jax.vmap(_conv_same)(x, weight) + b[None, :, None]
            elif typ == 'upsample':
                out = jax.vmap(_conv_up)(x, weight.transpose(0, 2, 1, 3)) + b[None, :, None]
                out = _blur(out, 2.0 * blur_k, (1, 1))
            elif typ == 'downsample':
                xb = _blur(x, blur_k, (2, 2))
                out = jax.vmap(_conv_down)(xb, weight) + b[None, :, None]
            else:
                raise NotImplementedError(typ)
            return out
        out = x
        for i, typ in enumerate(TYPES):
            out = _layer(out, style, weights[i], biases[i], mod_w[i], mod_b[i], typ)
        return out

    def _L0_attn_ref(hidden_states, wq, bq, wk, bk, wv, bv, wl, bl):
        import jax, jax.numpy as jnp
        import numpy as np
        HIDDEN = 512
        NUM_HEADS = 32
        HEAD_DIM = HIDDEN // NUM_HEADS

        def _fp8_roundtrip(x):
            return x.astype(jnp.float8_e4m3fn).astype(jnp.float32)
        B, S, E = hidden_states.shape
        H, D = (NUM_HEADS, HEAD_DIM)
        q = (hidden_states @ wq.T + bq).reshape(B, S, H, D)
        k = (hidden_states @ wk.T + bk).reshape(B, S, H, D)
        v = (hidden_states @ wv.T + bv).reshape(B, S, H, D)
        latent = hidden_states @ wl.T + bl
        scores = jnp.einsum('bshd,bstd->bsht', q, k) / np.sqrt(D).astype(np.float32)
        probs = jax.nn.softmax(scores, axis=-1)
        context = jnp.einsum('bsht,bstd->bshd', probs, v).reshape(B, S, E)
        return context

    def _L0_cond2_ref(x, style, weights, biases, mod_w, mod_b):
        import jax, jax.numpy as jnp
        from jax import lax
        import numpy as np
        CIN, COUT, K, STYLE_DIM = (32, 32, 3, 64)
        N_LAYERS = 4
        TYPES = ('same', 'upsample', 'same', 'downsample')
        SCALE = 1.0 / float(np.sqrt(CIN * K ** 2))
        EPS = 1e-08
        _BK = np.array([1.0, 3.0, 3.0, 1.0], dtype=np.float32)
        BLUR_K = _BK / _BK.sum()

        def _blur(x, kern, pad):
            B, C, _ = x.shape
            xp = jnp.pad(x, ((0, 0), (0, 0), (pad[0], pad[1])))
            w = jnp.broadcast_to(kern.astype(x.dtype)[None, None, :], (C, 1, kern.shape[0]))
            return lax.conv_general_dilated(xp, w, (1,), 'VALID', feature_group_count=C, dimension_numbers=('NCH', 'OIH', 'NCH'))

        def _conv_same(x, w):
            p = (K - 1) // 2
            return lax.conv_general_dilated(x[None], w, (1,), [(p, p)], dimension_numbers=('NCH', 'OIH', 'NCH'))[0]

        def _conv_down(x, w):
            return lax.conv_general_dilated(x[None], w, (2,), 'VALID', dimension_numbers=('NCH', 'OIH', 'NCH'))[0]

        def _conv_up(x, w_t):
            return lax.conv_transpose(x[None], w_t, (2,), 'VALID', dimension_numbers=('NCH', 'IOH', 'NCH'), transpose_kernel=True)[0]

        def _layer(x, style, w, b, mw, mb, typ):
            s = style @ mw.T + mb
            weight = SCALE * w * s[:, None, :, None]
            demod = lax.rsqrt(jnp.sum(weight * weight, axis=(2, 3)) + EPS)
            weight = weight * demod[:, :, None, None]
            blur_k = jnp.asarray(BLUR_K)
            if typ == 'same':
                out = jax.vmap(_conv_same)(x, weight) + b[None, :, None]
            elif typ == 'upsample':
                out = jax.vmap(_conv_up)(x, weight.transpose(0, 2, 1, 3)) + b[None, :, None]
                out = _blur(out, 2.0 * blur_k, (1, 1))
            elif typ == 'downsample':
                xb = _blur(x, blur_k, (2, 2))
                out = jax.vmap(_conv_down)(xb, weight) + b[None, :, None]
            else:
                raise NotImplementedError(typ)
            return out
        out = x
        for i, typ in enumerate(TYPES):
            out = _layer(out, style, weights[i], biases[i], mod_w[i], mod_b[i], typ)
        return out

    def _L0_ffn_ref(x, W_base, b_base, W_gate, W_thr, b_thr, A_w, B_w):
        import jax, jax.numpy as jnp
        import numpy as np
        B, S, D, O, E, R = (4, 256, 512, 512, 8, 16)
        SCALING = 32.0 / 16.0
        MAX_THRESHOLD = 0.125
        base = jnp.einsum('bsd,od->bso', x, W_base) + b_base
        xf = x.reshape(-1, D)
        gate = jax.nn.softmax(xf @ W_gate.T, axis=-1)
        thr = jax.nn.sigmoid(xf @ W_thr + b_thr[0]) * MAX_THRESHOLD
        adapted = gate - thr[:, None]
        selected = (adapted >= 0).astype(x.dtype)
        w = adapted * selected
        wsum = jnp.sum(w, axis=-1, keepdims=True)
        wsum = jnp.where(wsum == 0, jnp.ones_like(wsum), wsum)
        w = w / wsum
        h = jnp.einsum('nd,erd->ner', xf, A_w)
        moe = jnp.einsum('ner,ne,eor->no', h, w, B_w) * SCALING
        return base + moe.reshape(base.shape)

    def _L1_cond_ref(x, style, weights, biases, mod_w, mod_b):
        import jax, jax.numpy as jnp
        from jax import lax
        import numpy as np
        CIN, COUT, K, STYLE_DIM = (32, 32, 3, 64)
        N_LAYERS = 4
        TYPES = ('same', 'upsample', 'same', 'downsample')
        SCALE = 1.0 / float(np.sqrt(CIN * K ** 2))
        EPS = 1e-08
        _BK = np.array([1.0, 3.0, 3.0, 1.0], dtype=np.float32)
        BLUR_K = _BK / _BK.sum()

        def _blur(x, kern, pad):
            B, C, _ = x.shape
            xp = jnp.pad(x, ((0, 0), (0, 0), (pad[0], pad[1])))
            w = jnp.broadcast_to(kern.astype(x.dtype)[None, None, :], (C, 1, kern.shape[0]))
            return lax.conv_general_dilated(xp, w, (1,), 'VALID', feature_group_count=C, dimension_numbers=('NCH', 'OIH', 'NCH'))

        def _conv_same(x, w):
            p = (K - 1) // 2
            return lax.conv_general_dilated(x[None], w, (1,), [(p, p)], dimension_numbers=('NCH', 'OIH', 'NCH'))[0]

        def _conv_down(x, w):
            return lax.conv_general_dilated(x[None], w, (2,), 'VALID', dimension_numbers=('NCH', 'OIH', 'NCH'))[0]

        def _conv_up(x, w_t):
            return lax.conv_transpose(x[None], w_t, (2,), 'VALID', dimension_numbers=('NCH', 'IOH', 'NCH'), transpose_kernel=True)[0]

        def _layer(x, style, w, b, mw, mb, typ):
            s = style @ mw.T + mb
            weight = SCALE * w * s[:, None, :, None]
            demod = lax.rsqrt(jnp.sum(weight * weight, axis=(2, 3)) + EPS)
            weight = weight * demod[:, :, None, None]
            blur_k = jnp.asarray(BLUR_K)
            if typ == 'same':
                out = jax.vmap(_conv_same)(x, weight) + b[None, :, None]
            elif typ == 'upsample':
                out = jax.vmap(_conv_up)(x, weight.transpose(0, 2, 1, 3)) + b[None, :, None]
                out = _blur(out, 2.0 * blur_k, (1, 1))
            elif typ == 'downsample':
                xb = _blur(x, blur_k, (2, 2))
                out = jax.vmap(_conv_down)(xb, weight) + b[None, :, None]
            else:
                raise NotImplementedError(typ)
            return out
        out = x
        for i, typ in enumerate(TYPES):
            out = _layer(out, style, weights[i], biases[i], mod_w[i], mod_b[i], typ)
        return out

    def _L1_attn_ref(hidden_states, Wq_a, q_a_ln_w, Wq_b, Wkv_a, kv_a_ln_w, Wkv_b, Wo):
        import jax, jax.numpy as jnp
        import numpy as np
        B, S, D = (1, 256, 512)
        H = 32
        Q_RANK, KV_RANK = (192, 64)
        NOPE, ROPE, VD = (128, 64, 128)
        QD = NOPE + ROPE
        EPS = 1e-06
        THETA = 10000.0

        def _rmsnorm(x, w):
            return x * jax.lax.rsqrt(jnp.mean(x * x, axis=-1, keepdims=True) + EPS) * w

        def _rotate_half(x):
            h = x.shape[-1] // 2
            return jnp.concatenate([-x[..., h:], x[..., :h]], axis=-1)

        def _apply_rope(x, cos, sin):
            xp = jnp.concatenate([x[..., 0::2], x[..., 1::2]], axis=-1)
            return xp * cos + _rotate_half(xp) * sin

        def _mla_forward(hidden_states, Wq_a, q_a_ln_w, Wq_b, Wkv_a, kv_a_ln_w, Wkv_b, Wo):
            b, s, _ = hidden_states.shape
            q = _rmsnorm(hidden_states @ Wq_a, q_a_ln_w) @ Wq_b
            q = q.reshape(b, s, H, QD).transpose(0, 2, 1, 3)
            q_nope, q_pe = (q[..., :NOPE], q[..., NOPE:])
            ckv = hidden_states @ Wkv_a
            compressed, k_pe = (ckv[..., :KV_RANK], ckv[..., KV_RANK:])
            kv = _rmsnorm(compressed, kv_a_ln_w) @ Wkv_b
            kv = kv.reshape(b, s, H, NOPE + VD).transpose(0, 2, 1, 3)
            k_nope, v = (kv[..., :NOPE], kv[..., NOPE:])
            k_pe = k_pe[:, None, :, :]
            inv_freq = 1.0 / THETA ** (jnp.arange(0, ROPE, 2, dtype=jnp.float32) / ROPE)
            freqs = jnp.outer(jnp.arange(s, dtype=jnp.float32), inv_freq)
            emb = jnp.concatenate([freqs, freqs], axis=-1)
            cos = jnp.cos(emb)[None, None].astype(hidden_states.dtype)
            sin = jnp.sin(emb)[None, None].astype(hidden_states.dtype)
            q_pe = _apply_rope(q_pe, cos, sin)
            k_pe = _apply_rope(k_pe, cos, sin)
            qf = jnp.concatenate([q_nope, q_pe], axis=-1)
            kf = jnp.concatenate([k_nope, jnp.broadcast_to(k_pe, (b, H, s, ROPE))], axis=-1)
            scale = QD ** (-0.5)
            scores = jnp.einsum('bhqd,bhkd->bhqk', qf, kf) * scale
            causal = jnp.tril(jnp.ones((s, s), dtype=bool))
            scores = jnp.where(causal, scores, jnp.finfo(scores.dtype).min)
            probs = jax.nn.softmax(scores, axis=-1)
            o = jnp.einsum('bhqk,bhkd->bhqd', probs, v)
            o = o.transpose(0, 2, 1, 3).reshape(b, s, H * VD)
            return o @ Wo
        return _mla_forward(hidden_states, Wq_a, q_a_ln_w, Wq_b, Wkv_a, kv_a_ln_w, Wkv_b, Wo)

    def _L1_cond2_ref(x, style, weights, biases, mod_w, mod_b):
        import jax, jax.numpy as jnp
        from jax import lax
        import numpy as np
        CIN, COUT, K, STYLE_DIM = (32, 32, 3, 64)
        N_LAYERS = 4
        TYPES = ('same', 'upsample', 'same', 'downsample')
        SCALE = 1.0 / float(np.sqrt(CIN * K ** 2))
        EPS = 1e-08
        _BK = np.array([1.0, 3.0, 3.0, 1.0], dtype=np.float32)
        BLUR_K = _BK / _BK.sum()

        def _blur(x, kern, pad):
            B, C, _ = x.shape
            xp = jnp.pad(x, ((0, 0), (0, 0), (pad[0], pad[1])))
            w = jnp.broadcast_to(kern.astype(x.dtype)[None, None, :], (C, 1, kern.shape[0]))
            return lax.conv_general_dilated(xp, w, (1,), 'VALID', feature_group_count=C, dimension_numbers=('NCH', 'OIH', 'NCH'))

        def _conv_same(x, w):
            p = (K - 1) // 2
            return lax.conv_general_dilated(x[None], w, (1,), [(p, p)], dimension_numbers=('NCH', 'OIH', 'NCH'))[0]

        def _conv_down(x, w):
            return lax.conv_general_dilated(x[None], w, (2,), 'VALID', dimension_numbers=('NCH', 'OIH', 'NCH'))[0]

        def _conv_up(x, w_t):
            return lax.conv_transpose(x[None], w_t, (2,), 'VALID', dimension_numbers=('NCH', 'IOH', 'NCH'), transpose_kernel=True)[0]

        def _layer(x, style, w, b, mw, mb, typ):
            s = style @ mw.T + mb
            weight = SCALE * w * s[:, None, :, None]
            demod = lax.rsqrt(jnp.sum(weight * weight, axis=(2, 3)) + EPS)
            weight = weight * demod[:, :, None, None]
            blur_k = jnp.asarray(BLUR_K)
            if typ == 'same':
                out = jax.vmap(_conv_same)(x, weight) + b[None, :, None]
            elif typ == 'upsample':
                out = jax.vmap(_conv_up)(x, weight.transpose(0, 2, 1, 3)) + b[None, :, None]
                out = _blur(out, 2.0 * blur_k, (1, 1))
            elif typ == 'downsample':
                xb = _blur(x, blur_k, (2, 2))
                out = jax.vmap(_conv_down)(xb, weight) + b[None, :, None]
            else:
                raise NotImplementedError(typ)
            return out
        out = x
        for i, typ in enumerate(TYPES):
            out = _layer(out, style, weights[i], biases[i], mod_w[i], mod_b[i], typ)
        return out

    def _L1_ffn_ref(x, k0, s0, k1, s1, k2, s2):
        import jax, jax.numpy as jnp
        import numpy as np
        import math
        D = 512
        TOKENS = (4, 256)
        P = 0.8

        def conn_dense(kernel, x):
            w = jnp.where(kernel, jnp.asarray(1.0, x.dtype), jnp.asarray(-1.0, x.dtype))
            return x @ w

        def ei_dense(x, kernel, scale, p):
            in_dim = x.shape[-1]
            ne = round(in_dim * p)
            x_exc = x[..., :ne]
            x_inh = x[..., ne:]
            xx = jnp.concatenate([x_exc, -p / (1.0 - p) * x_inh], axis=-1)
            return scale * conn_dense(kernel, xx)
        h = s0 * conn_dense(k0, x)
        h = jax.nn.relu(h) * 2.0
        h = ei_dense(h, k1, s1, P)
        h = jax.nn.relu(h) * 2.0
        return ei_dense(h, k2, s2, P)
    x = x + _L0_attn_ref(_L0_cond_ref(x, cond_512, L0_cond_weights, L0_cond_biases, L0_cond_mod_w, L0_cond_mod_b), L0_attn_wq, L0_attn_bq, L0_attn_wk, L0_attn_bk, L0_attn_wv, L0_attn_bv, L0_attn_wl, L0_attn_bl)
    x = x + _L0_ffn_ref(_L0_cond2_ref(x, cond_512, L0_cond2_weights, L0_cond2_biases, L0_cond2_mod_w, L0_cond2_mod_b), L0_ffn_W_base, L0_ffn_b_base, L0_ffn_W_gate, L0_ffn_W_thr, L0_ffn_b_thr, L0_ffn_A_w, L0_ffn_B_w)
    x = x + _L1_attn_ref(_L1_cond_ref(x, cond_512, L1_cond_weights, L1_cond_biases, L1_cond_mod_w, L1_cond_mod_b), L1_attn_Wq_a, L1_attn_q_a_ln_w, L1_attn_Wq_b, L1_attn_Wkv_a, L1_attn_kv_a_ln_w, L1_attn_Wkv_b, L1_attn_Wo)
    x = x + _L1_ffn_ref(_L1_cond2_ref(x, cond_512, L1_cond2_weights, L1_cond2_biases, L1_cond2_mod_w, L1_cond2_mod_b), L1_ffn_k0, L1_ffn_s0, L1_ffn_k1, L1_ffn_s1, L1_ffn_k2, L1_ffn_s2)
    return x

_drawn_inputs = setup_inputs


def setup_inputs(seed=0):
    import zlib

    import numpy as np

    out = dict(_drawn_inputs(seed))
    spreads = {'L1_attn_q_a_ln_w': (1.0, 0.6), 'L1_attn_kv_a_ln_w': (1.0, 0.6)}
    factors = {'L0_cond_biases': 2.717,
     'L0_cond_mod_b': 5.491,
     'L0_attn_wq': 4.036,
     'L0_attn_bq': 8.0,
     'L0_attn_wk': 3.642,
     'L0_attn_bk': 8.0,
     'L0_attn_bv': 8.0,
     'L0_ffn_b_base': 4.767,
     'L1_cond_biases': 4.482,
     'L1_cond_mod_b': 6.157,
     'L1_attn_Wq_a': 8.0,
     'L1_attn_Wq_b': 8.0}
    for name, (base, spread) in spreads.items():
        noise = np.random.default_rng([zlib.crc32(name.encode()), seed]).standard_normal(out[name].shape)
        drawn = base * np.exp(spread * noise) if base else spread * noise
        out[name] = jnp.asarray(drawn.astype(out[name].dtype))
    for name, factor in factors.items():
        out[name] = (out[name] * factor).astype(out[name].dtype)
    return out
```

```python
from contextlib import ExitStack

import numpy as np
import concourse.bass as bass
from concourse import mybir

F32 = mybir.dt.float32
U8 = mybir.dt.uint8
ALU = mybir.AluOpType
ACT = mybir.ActivationFunctionType
AX = mybir.AxisListType

P = 128
D = 512
S = 32
GB = P // S
KC = D // P
STYLE = 64
LAYERS, TAPS = 4, 3
CONDS = 4
CONV_SCALE = 1.0 / float(np.sqrt(S * TAPS ** 2))
CONV_EPS = 1e-8
UP = 2 * D
NCOEF = 9

H = 32
HD = 16
QR, CR, RO = 192, 64, 64
NOPE, VD = 128, 128
RMS_EPS = 1e-6
MLA_SCALE = float(NOPE + RO) ** -0.5
MASKED = -1e30

EX, RK = 8, 16
AG = EX * RK + EX + 1
MAX_THRESHOLD = 0.125
LORA_SCALE = 2.0
EXC = round(D * 0.8)
INH = -4.0


class Named:
    pass


def is_first(count):
    return isinstance(count, int) and count == 0


def steps(eng, groups, base, body):
    assert groups % 2 == 0 and groups >= 6
    first = 1 if base else 2
    body(0, 0, 0, True, False)
    for t in range(1, 2 * first):
        body(t, t // 2, t % 2, True, True)
    with eng.Fori(first, groups // 2) as i:
        body(2 * i, i, 0, True, True)
        body(2 * i + 1, i, 1, True, True)
    body(groups, groups // 2, 0, False, True)


def block_half(h, par):
    return h if par else h - 1



def conv_load(sp, k, t, n, par):
    if not is_first(n):
        sp.wait_ge(k.prescaled, n - 1)
    sp.dma_start(k.xin[:, par, :], k.src[bass.ds(t * P, P), :]).then_inc(k.x_loaded[par], 16)


def conv_coef(dve, nc, k, t, n, par):
    if not is_first(n):
        dve.wait_ge(k.y_ready, n - 1)
    nc.vector.tensor_scalar(k.coef[:, par, :],
                            k.table[:, k.cond, bass.ds(t, 1), :].rearrange("p a c -> p (a c)"),
                            1.0, None, ALU.mult).then_inc(k.coef_ready, 1)


def conv_act(act, nc, k, slot, n, nh, par):
    coef = k.coef[:, par, :]
    if slot == "C0":
        act.wait_ge(k.x_loaded[par], 16 * nh + 16)
        act.wait_ge(k.coef_ready, n + 1)
        act.wait_ge(k.conv1_done, n)
        nc.scalar.activation(k.x1[:, 1:1 + D], k.xin[:, par, :], ACT.Copy,
                             scale=coef[:, 0:1]).then_inc(k.prescaled, 1)
    if slot == "C1":
        act.wait_ge(k.conv1_done, n + 1)
        act.wait_ge(k.conv2_done, 3 * n)
        nc.scalar.activation(k.x2[:, 1:1 + D], k.pc[:, 0, :], ACT.Identity,
                             bias=coef[:, 2:3], scale=coef[:, 1:2]).then_inc(k.x2_ready, 1)
    if slot == "C2":
        act.wait_ge(k.blur1_done, 3 * n)
        for m, (src, lo, cnt) in enumerate(((1, 1, D), (2, 2, D), (0, UP + 1, 1))):
            act.wait_ge(k.conv2_done, 3 * n + m + 1)
            nc.scalar.activation(k.y2[:, lo:lo + 2 * cnt - 1:2], k.pc[:, src, 0:cnt], ACT.Identity,
                                 bias=coef[:, 4:5], scale=coef[:, 3:4]).then_inc(k.y2_ready, 1)
    if slot == "C3":
        act.wait_ge(k.blur2_done, 3 * n)
        for m in range(2):
            act.wait_ge(k.conv3_done, 2 * n + m + 1)
            nc.scalar.activation(k.y3[:, 2 + m * D:2 + (m + 1) * D], k.pc[:, 1 + m, :],
                                 ACT.Identity, bias=coef[:, 6:7],
                                 scale=coef[:, 5:6]).then_inc(k.y3_ready, 1)
    if slot == "C4":
        act.wait_ge(k.conv4_done, n + 1)
        if not is_first(n):
            act.wait_ge(k.y_turned, n - 1)
        nc.scalar.activation(k.y[:, par, :], k.pc[:, 0, :], ACT.Identity,
                             bias=coef[:, 8:9], scale=coef[:, 7:8]).then_inc(k.y_ready, 1)


def conv_vector(dve, nc, k, slot, n):
    if slot == "C2":
        dve.wait_ge(k.y2_ready, 3 * n + 3)
        nc.vector.tensor_tensor(k.blur_a[:, 0:UP + 2], k.y2[:, 0:UP + 2], k.y2[:, 1:UP + 3],
                                ALU.add).then_inc(k.blur1_done, 1)
        dve.wait_ge(k.blur1_done, 3 * n + 1)
        nc.vector.tensor_tensor(k.blur_b[:, 0:UP + 1], k.blur_a[:, 0:UP + 1],
                                k.blur_a[:, 1:UP + 2], ALU.add).then_inc(k.blur1_done, 1)
        dve.wait_ge(k.blur1_done, 3 * n + 2)
        dve.wait_ge(k.conv3_done, 2 * n)
        nc.vector.tensor_tensor(k.x3[:, 1:1 + UP], k.blur_b[:, 0:UP], k.blur_b[:, 1:UP + 1],
                                ALU.add).then_inc(k.blur1_done, 1)
    if slot == "C3":
        dve.wait_ge(k.y3_ready, 2 * n + 2)
        nc.vector.tensor_tensor(k.blur_a[:, 0:UP + 3], k.y3[:, 0:UP + 3], k.y3[:, 1:UP + 4],
                                ALU.add).then_inc(k.blur2_done, 1)
        dve.wait_ge(k.blur2_done, 3 * n + 1)
        nc.vector.tensor_tensor(k.blur_b[:, 0:UP + 2], k.blur_a[:, 0:UP + 2],
                                k.blur_a[:, 1:UP + 3], ALU.add).then_inc(k.blur2_done, 1)
        dve.wait_ge(k.blur2_done, 3 * n + 2)
        dve.wait_ge(k.conv4_done, n)
        nc.vector.tensor_tensor(k.x4[:, 0:UP + 1], k.blur_b[:, 0:UP + 1], k.blur_b[:, 1:UP + 2],
                                ALU.add).then_inc(k.blur2_done, 1)


def conv_tensor(pe, nc, k, slot, n):
    def weights(layer, tap):
        return k.convw[:, k.cond, layer * TAPS + tap, :]

    if slot == "C1":
        pe.wait_ge(k.prescaled, n + 1)
        pe.wait_ge(k.y_ready, n)
        for tap in range(TAPS):
            mm = nc.tensor.matmul(k.pc[:, 0, :], weights(0, tap), k.x1[:, tap:tap + D],
                                  start=(tap == 0), stop=(tap == TAPS - 1))
        mm.then_inc(k.conv1_done, 1)
    if slot == "C2":
        pe.wait_ge(k.x2_ready, n + 1)
        pe.wait_ge(k.y3_ready, 2 * n)
        nc.tensor.matmul(k.pc[:, 1, :], weights(1, 0), k.x2[:, 1:1 + D], start=True, stop=False)
        nc.tensor.matmul(k.pc[:, 1, :], weights(1, 2), k.x2[:, 0:D], start=False,
                         stop=True).then_inc(k.conv2_done, 1)
        nc.tensor.matmul(k.pc[:, 2, :], weights(1, 1), k.x2[:, 1:1 + D], start=True,
                         stop=True).then_inc(k.conv2_done, 1)
        nc.tensor.matmul(k.pc[:, 0, 0:1], weights(1, 2), k.x2[:, D:D + 1], start=True,
                         stop=True).then_inc(k.conv2_done, 1)
    if slot == "C3":
        pe.wait_ge(k.blur1_done, 3 * n + 3)
        for m in range(2):
            for tap in range(TAPS):
                mm = nc.tensor.matmul(k.pc[:, 1 + m, :], weights(2, tap),
                                      k.x3[:, m * D + tap:m * D + tap + D],
                                      start=(tap == 0), stop=(tap == TAPS - 1))
            mm.then_inc(k.conv3_done, 1)
    if slot == "C4":
        pe.wait_ge(k.blur2_done, 3 * n + 3)
        for tap in range(TAPS):
            mm = nc.tensor.matmul(k.pc[:, 0, :], weights(3, tap), k.x4[:, tap:tap + UP - 1:2],
                                  start=(tap == 0), stop=(tap == TAPS - 1))
        mm.then_inc(k.conv4_done, 1)



def residual_load(sp, k, g, n, par):
    if not is_first(n):
        sp.wait_ge(k.out_ready, n - 1)
    sp.dma_start(k.xres[:, par, :], k.src[bass.ds(g * P, P), :]).then_inc(k.res_loaded[par], 16)


def store(sp, k, g, n, par):
    sp.wait_ge(k.out_ready, n + 1)
    sp.dma_start(k.dst[bass.ds(g * P, P), :], k.xout[:, par, :]).then_inc(k.stored[par], 16)


def turn_y(pe, nc, k, n, par):
    pe.wait_ge(k.y_ready, n + 1)
    pe.wait_ge(k.out_ready, n)
    for c in range(KC):
        mm = nc.tensor.transpose(k.pb[:, 4, c * P:(c + 1) * P], k.y[:, par, c * P:(c + 1) * P],
                                 k.ident[:, :])
    mm.then_inc(k.y_turned, 1)


def copy_yT(dve, nc, k, n):
    dve.wait_ge(k.y_turned, n + 1)
    nc.vector.tensor_copy(k.yT[:, :, :].rearrange("p c t -> p (c t)"),
                          k.pb[:, 4, :]).then_inc(k.yT_ready, 1)


def dense(nc, out, xT, w, cols=D, last=True):
    for c in range(KC):
        mm = nc.tensor.matmul(out, xT[:, c, :], w[:, c, 0:cols], start=(c == 0),
                              stop=last and c == KC - 1)
    return mm



def conv_tiles(nc, ctx, k, tag):
    def sb(name, shape):
        return ctx.enter_context(nc.sbuf_tensor(f"{name}_{tag}", shape, F32))

    k.xin = sb("xin", [P, 2, D])
    k.coef = sb("coef", [P, 2, NCOEF])
    k.x1 = sb("x1", [P, D + 2])
    k.x2 = sb("x2", [P, D + 2])
    k.y2 = sb("y2", [P, UP + 3])
    k.x3 = sb("x3", [P, UP + 2])
    k.y3 = sb("y3", [P, UP + 4])
    k.x4 = sb("x4", [P, UP + 2])
    k.blur_a = sb("blur_a", [P, UP + 4])
    k.blur_b = sb("blur_b", [P, UP + 4])
    k.y = sb("y", [P, 2, D])
    k.yT = sb("yT", [P, KC, P])
    k.xres = sb("xres", [P, 2, D])
    k.xout = sb("xout", [P, 2, D])


def zero_edges(nc, k):
    last = None
    for tile, cols in ((k.x1, (0, D + 1)), (k.x2, (0, D + 1)), (k.y2, (0, UP + 2)),
                       (k.x3, (0, UP + 1)), (k.y3, (0, 1, UP + 2, UP + 3))):
        for c in cols:
            last = nc.vector.memset(tile[:, c:c + 1], 0.0)
            last.then_inc(k.edges_zero, 1)
    return 12


def prepare(nc, k, d, groups):
    with ExitStack() as ctx:
        def sb(name, shape):
            return ctx.enter_context(nc.sbuf_tensor(name, shape, F32))

        NL = CONDS * LAYERS
        demw = sb("demw", [P, NL, TAPS, S])
        styT = sb("styT", [STYLE, groups * GB])
        modT = sb("modT", [STYLE, NL, S])
        modb = sb("modb", [P, NL])
        bias = sb("bias", [P, NL])
        demsq = sb("demsq", [P, NL, S])
        sty = sb("sty", [P, CONDS, LAYERS, groups])
        stysq = sb("stysq", [P, NL, groups])
        dem = sb("dem", [P, CONDS, LAYERS, groups])
        eps = sb("eps", [P, 1])
        ps = ctx.enter_context(nc.psum_tensor("ps_prep", [P, 5, 512], F32))
        NB = min(NL, 512 // groups)
        assert NB == NL
        s = Named()
        s.zeroed = ctx.enter_context(nc.semaphore("zeroed"))
        s.wloaded = ctx.enter_context(nc.semaphore("wloaded"))
        s.dloaded = ctx.enter_context(nc.semaphore("dloaded"))
        s.ident_ready = ctx.enter_context(nc.semaphore("ident_ready"))
        s.sty_done = ctx.enter_context(nc.semaphore("sty_done"))
        s.sty_ready = ctx.enter_context(nc.semaphore("sty_ready"))
        s.sq_done = ctx.enter_context(nc.semaphore("sq_done"))
        s.dem_done = ctx.enter_context(nc.semaphore("dem_done"))
        s.dem_root = ctx.enter_context(nc.semaphore("dem_root"))
        s.tab_done = ctx.enter_context(nc.semaphore("tab_done"))
        with nc.Block() as block:
            @block.sync
            def _(sp):
                for b in range(GB):
                    rows = slice(b * S, (b + 1) * S)
                    sp.dma_start(demw[rows, :, :, :], d["demod_w"]).then_inc(s.dloaded, 16)
                    sp.dma_start(modb[rows, :], d["mod_b"]).then_inc(s.dloaded, 16)
                    sp.dma_start(bias[rows, :], d["conv_b"]).then_inc(s.dloaded, 16)
                sp.dma_start(styT[:, :], d["style_t"]).then_inc(s.dloaded, 16)
                sp.dma_start(modT[:, :, :], d["mod_wt"]).then_inc(s.dloaded, 16)
                sp.wait_ge(s.zeroed, CONDS)
                for b in range(GB):
                    rows = slice(b * S, (b + 1) * S)
                    for c in range(CONDS):
                        sp.dma_start(k.convw[rows, c, :, rows], d["conv_w"][:, c, :, :]
                                     ).then_inc(s.wloaded, 16)
                sp.wait_ge(s.wloaded, 16 * GB * CONDS)

            @block.gpsimd
            def _(pool):
                for c in range(CONDS):
                    nc.gpsimd.memset(k.convw[:, c, :, :], 0.0).then_inc(s.zeroed, 1)
                nc.gpsimd.memset(k.ident[:, :], 0.0).then_inc(s.ident_ready, 1)
                pool.wait_ge(s.ident_ready, 1)
                nc.gpsimd.affine_select(out=k.ident[:, :], in_=k.ident[:, :],
                                        compare_op=ALU.not_equal, fill=1.0, base=0,
                                        pattern=[[-1, P]], channel_multiplier=1
                                        ).then_inc(s.ident_ready, 1)

            loads = 16 * (3 * GB + 2)

            @block.tensor
            def _(pe):
                pe.wait_ge(s.dloaded, loads)
                for b in range(GB):
                    for l in range(NL):
                        mm = nc.tensor.matmul(ps[b * S:(b + 1) * S, 4, l * groups:(l + 1) * groups],
                                              modT[:, l, :], styT[:, b:GB * groups:GB],
                                              start=True, stop=True)
                mm.then_inc(s.sty_done, 1)
                pe.wait_ge(s.sty_ready, 2)
                pe.wait_ge(s.sq_done, 3)
                for b in range(GB):
                    rows = slice(b * S, (b + 1) * S)
                    for l in range(NL):
                        mm = nc.tensor.matmul(ps[rows, b, l * groups:(l + 1) * groups],
                                              demsq[rows, l, :], stysq[rows, l, :],
                                              start=True, stop=True)
                mm.then_inc(s.dem_done, 1)

            @block.scalar
            def _(act):
                act.wait_ge(s.sq_done, 4)
                act.wait_ge(s.dem_done, 1)
                for b in range(GB):
                    rows = slice(b * S, (b + 1) * S)
                    nc.scalar.activation(dem[rows, :, :, :].rearrange("p c l g -> p (c l g)"),
                                         ps[rows, b, 0:NL * groups], ACT.Sqrt,
                                         bias=eps[rows, :], scale=CONV_SCALE ** 2
                                         ).then_inc(s.dem_root, 1)

            @block.vector
            def _(dve):
                dve.wait_ge(s.dloaded, loads)
                sq = demw[:, :, :, :].rearrange("p l t o -> p (l t o)")
                nc.vector.tensor_tensor(sq, sq, sq, ALU.mult).then_inc(s.sq_done, 1)
                dve.wait_ge(s.sq_done, 1)
                nc.vector.tensor_tensor(demsq[:, :, :], demw[:, :, 0, :], demw[:, :, 1, :],
                                        ALU.add).then_inc(s.sq_done, 1)
                dve.wait_ge(s.sq_done, 2)
                nc.vector.tensor_tensor(demsq[:, :, :], demsq[:, :, :], demw[:, :, 2, :],
                                        ALU.add).then_inc(s.sq_done, 1)
                nc.vector.memset(eps[:, :], CONV_EPS).then_inc(s.sq_done, 1)
                dve.wait_ge(s.sty_done, 1)
                styf = sty[:, :, :, :].rearrange("p c l g -> p (c l) g")
                nc.vector.tensor_tensor(
                    styf, ps[:, 4, 0:NL * groups].rearrange("p (l g) -> p l g", l=NL),
                    modb[:, :].unsqueeze(2).broadcast_to([P, NL, groups]),
                    ALU.add).then_inc(s.sty_ready, 1)
                dve.wait_ge(s.sty_ready, 1)
                nc.vector.tensor_tensor(stysq[:, :, :], styf, styf, ALU.mult
                                        ).then_inc(s.sty_ready, 1)
                dve.wait_ge(s.dem_root, GB)
                dall = dem[:, :, :, :].rearrange("p c l g -> p (c l g)")
                nc.vector.reciprocal(dall, dall).then_inc(s.tab_done, 1)
                dve.wait_ge(s.tab_done, 1)
                nc.vector.tensor_scalar(dall, dall, CONV_SCALE, None, ALU.mult
                                        ).then_inc(s.tab_done, 1)
                dve.wait_ge(s.tab_done, 2)
                tab = [k.table[:, :, :, j] for j in range(NCOEF)]
                bl = [bias[:, l:CONDS * LAYERS:LAYERS].unsqueeze(2).broadcast_to([P, CONDS, groups])
                      for l in range(LAYERS)]
                st = [sty[:, :, l, :] for l in range(LAYERS)]
                dm = [dem[:, :, l, :] for l in range(LAYERS)]
                nc.vector.tensor_copy(tab[0], st[0]).then_inc(s.tab_done, 1)
                nc.vector.tensor_tensor(tab[1], dm[0], dm[1], ALU.mult).then_inc(s.tab_done, 1)
                nc.vector.tensor_tensor(tab[2], bl[0], dm[1], ALU.mult).then_inc(s.tab_done, 1)
                nc.vector.scalar_tensor_tensor(out=tab[3], in0=st[1], scalar=0.25, in1=st[2],
                                               op0=ALU.mult, op1=ALU.mult).then_inc(s.tab_done, 1)
                nc.vector.scalar_tensor_tensor(out=tab[4], in0=st[2], scalar=0.25, in1=bl[1],
                                               op0=ALU.mult, op1=ALU.mult).then_inc(s.tab_done, 1)
                nc.vector.scalar_tensor_tensor(out=tab[5], in0=dm[2], scalar=0.125, in1=st[3],
                                               op0=ALU.mult, op1=ALU.mult).then_inc(s.tab_done, 1)
                nc.vector.scalar_tensor_tensor(out=tab[6], in0=st[3], scalar=0.125, in1=bl[2],
                                               op0=ALU.mult, op1=ALU.mult).then_inc(s.tab_done, 1)
                nc.vector.tensor_copy(tab[7], dm[3]).then_inc(s.tab_done, 1)
                nc.vector.tensor_copy(tab[8], bl[3]).then_inc(s.tab_done, 1)
                dve.wait_ge(s.tab_done, 11)


def phase_attention(nc, k, d, groups, base):
    order = ("C0", "C1", "B0", "C2", "B1", "C3", "B2", "C4", "B3")
    with ExitStack() as ctx:
        def sb(name, shape):
            return ctx.enter_context(nc.sbuf_tensor(name, shape, F32))

        conv_tiles(nc, ctx, k, "a0")
        w = sb("wqkv", [P, 3, KC, D])
        bqkv = sb("bqkv", [P, 3, D])
        yTv = sb("yTv", [P, KC, P])
        qz = sb("qz", [P, 2, H // 2, 2, HD])
        kd = sb("kd", [P, H, 2, HD])
        v = sb("v", [P, H, HD])
        qT = sb("qT", [P, S, H])
        kT = sb("kT", [P, S, H])
        vT = sb("vT", [P, S, HD + 1])
        e = sb("e", [P, GB * 8, H])
        eT = sb("eT", [P, GB * 8, H])
        top = sb("top", [P, GB * 8])
        rs = sb("rs", [P, GB * 8])
        ctxh = sb("ctxh", [P, GB * 8, HD])
        ctxt = sb("ctxt", [P, H // 2, 2, HD])
        s = Named()
        s.wqkv_loaded = ctx.enter_context(nc.semaphore("wqkv_loaded"))
        s.fixed = ctx.enter_context(nc.semaphore("fixed"))
        s.yTv_ready = ctx.enter_context(nc.semaphore("yTv_ready"))
        s.proj_done = ctx.enter_context(nc.semaphore("proj_done"))
        s.qkv_ready = ctx.enter_context(nc.semaphore("qkv_ready"))
        s.qkvT_ready = ctx.enter_context(nc.semaphore("qkvT_ready"))
        s.scores_done = ctx.enter_context(nc.semaphore("scores_done"))
        s.max_done = ctx.enter_context(nc.semaphore("max_done"))
        s.e_ready = ctx.enter_context(nc.semaphore("e_ready"))
        s.exp_done = ctx.enter_context(nc.semaphore("exp_done"))
        s.eT_ready = ctx.enter_context(nc.semaphore("eT_ready"))
        s.pv_done = ctx.enter_context(nc.semaphore("pv_done"))
        s.ctx_ready = ctx.enter_context(nc.semaphore("ctx_ready"))
        C8 = 8
        scores = k.pb[:, 0:4, 0:C8 * H].rearrange("p b (n t) -> p b n t", n=C8)
        heads = k.pb[:, 0:4, 0:C8 * (HD + 1)].rearrange("p b (n d) -> p b n d", n=C8)

        with nc.Block() as block:
            @block.sync
            def _(sp):
                sp.dma_start(w[:, :, :, :], d["w_qkv"].rearrange("j (c p) n -> p j c n", p=P)
                             ).then_inc(s.wqkv_loaded, 16)
                for j in range(3):
                    sp.dma_start(bqkv[:, j, :], d["b_qkv"][j:j + 1, :].broadcast_to([P, D])
                                 ).then_inc(s.wqkv_loaded, 16)

                def step(t, h, par, conv, blk):
                    if conv:
                        conv_load(sp, k, t, base + t, par)
                    if blk:
                        residual_load(sp, k, t - 1, base + t - 1, 1 - par)
                        store(sp, k, t - 1, base + t - 1, 1 - par)
                steps(sp, groups, base, step)
                for par in range(2):
                    sp.wait_ge(k.stored[par], 8 * (base + groups))

            @block.gpsimd
            def _(pool):
                def step(t, h, par, conv, blk):
                    if blk:
                        n, bpar = base + t - 1, 1 - par
                        pool.wait_ge(s.ctx_ready, 3 * (t - 1) + 3)
                        nh = base // 2 + block_half(h, par)
                        pool.wait_ge(k.res_loaded[bpar], 16 * nh + 16)
                        pool.wait_ge(k.stored[bpar], 16 * nh)
                        nc.gpsimd.tensor_tensor(
                            k.xout[:, bpar, :], ctxt[:, :, :, :].rearrange("p c h d -> p (c h d)"),
                            k.xres[:, bpar, :], ALU.add).then_inc(k.out_ready, 1)
                steps(pool, groups, base, step)

            @block.scalar
            def _(act):
                act.wait_ge(k.edges_zero, 12 * (1 + k.cond))

                def step(t, h, par, conv, blk):
                    g = t - 1
                    for slot in order:
                        if conv and slot[0] == "C":
                            conv_act(act, nc, k, slot, base + t, base // 2 + h, par)
                        if blk and slot == "B1":
                            act.wait_ge(s.proj_done, 3 * g)
                            act.wait_ge(k.yT_ready, base + g + 1)
                            for c in range(KC):
                                nc.scalar.copy(
                                    yTv[:, c, :].rearrange("p (g q n) -> p g q n", q=GB, g=GB),
                                    k.yT[:, c, :].rearrange("p (q g n) -> p g q n", q=GB, g=GB)
                                    ).then_inc(s.yTv_ready, 1)
                        if blk and slot == "B2":
                            act.wait_ge(s.e_ready, g + 1)
                            nc.scalar.activation(e[:, :, :], e[:, :, :], ACT.Exp,
                                                 scale=float(HD) ** -0.5).then_inc(s.exp_done, 1)
                steps(act, groups, base, step)

            @block.tensor
            def _(pe):
                pe.wait_ge(s.wqkv_loaded, 64)

                def step(t, h, par, conv, blk):
                    g, n = t - 1, base + t - 1
                    for slot in order:
                        if conv and slot[0] == "C":
                            conv_tensor(pe, nc, k, slot, base + t)
                        if not blk:
                            continue
                        if slot == "B0":
                            turn_y(pe, nc, k, n, 1 - par)
                        if slot == "B1":
                            pe.wait_ge(k.yT_ready, n + 1)
                            pe.wait_ge(s.ctx_ready, 3 * g)
                            dense(nc, k.pb[:, 0, :], k.yT, w[:, 0, :, :]).then_inc(s.proj_done, 1)
                            dense(nc, k.pb[:, 1, :], k.yT, w[:, 1, :, :]).then_inc(s.proj_done, 1)
                            pe.wait_ge(s.yTv_ready, KC * (g + 1))
                            dense(nc, k.pb[:, 2, :], yTv, w[:, 2, :, :]).then_inc(s.proj_done, 1)
                        if slot == "B2":
                            pe.wait_ge(s.fixed, 2)
                            pe.wait_ge(s.qkvT_ready, 3 * g + 3)
                            pe.nop(nofuse=True)
                            for i in range(C8):
                                for q in range(GB):
                                    for c in range(GB):
                                        rows = slice(q * S, (q + 1) * S)
                                        mm = nc.tensor.matmul(
                                            k.pb[c * S:(c + 1) * S, q, i * H:(i + 1) * H],
                                            qT[rows, c * C8 + i, :], kT[rows, c * C8 + i, :],
                                            start=True, stop=True)
                            mm.then_inc(s.scores_done, 1)
                        if slot == "B3":
                            pe.wait_ge(s.fixed, 2)
                            pe.wait_ge(s.eT_ready, g + 1)
                            pe.nop(nofuse=True)
                            for i in range(C8):
                                for c in range(GB):
                                    for q in range(GB):
                                        rows = slice(c * S, (c + 1) * S)
                                        mm = nc.tensor.matmul(
                                            k.pb[q * S:(q + 1) * S, c,
                                                 i * (HD + 1):(i + 1) * (HD + 1)],
                                            eT[rows, q * C8 + i, :], vT[rows, q * C8 + i, :],
                                            start=True, stop=True)
                            mm.then_inc(s.pv_done, 1)
                steps(pe, groups, base, step)

            @block.vector
            def _(dve):
                zero_edges(nc, k)
                nc.vector.memset(qz[:, :, :, :, :].rearrange("p a c h d -> p (a c h d)"), 0.0
                                 ).then_inc(s.fixed, 1)
                nc.vector.memset(vT[:, :, HD:HD + 1], 1.0).then_inc(s.fixed, 1)
                dve.wait_ge(s.fixed, 2)
                dve.wait_ge(k.edges_zero, 12 * (1 + k.cond))
                dve.wait_ge(s.wqkv_loaded, 64)

                def step(t, h, par, conv, blk):
                    g, n = t - 1, base + t - 1
                    for slot in order:
                        if conv and slot == "C0":
                            conv_coef(dve, nc, k, t, base + t, par)
                        if conv and slot[0] == "C":
                            conv_vector(dve, nc, k, slot, base + t)
                        if not blk:
                            continue
                        if slot == "B0":
                            copy_yT(dve, nc, k, n)
                        if slot == "B1":
                            dve.wait_ge(s.proj_done, 3 * g + 1)
                            qp = k.pb[:, 0, :].rearrange("p (c h d) -> p c h d", h=2, d=HD)
                            qb = bqkv[:, 0, :].rearrange("p (c h d) -> p c h d", h=2, d=HD)
                            for h in range(2):
                                nc.vector.tensor_tensor(qz[:, h, :, h, :], qp[:, :, h, :],
                                                        qb[:, :, h, :], ALU.add
                                                        ).then_inc(s.qkv_ready, 1)
                            dve.wait_ge(s.proj_done, 3 * g + 2)
                            kp = k.pb[:, 1, :].rearrange("p (t d) -> p t d", d=HD)
                            kb = bqkv[:, 1, :].rearrange("p (t d) -> p t d", d=HD)
                            for h in range(2):
                                nc.vector.tensor_tensor(kd[:, :, h, :], kp, kb, ALU.add
                                                        ).then_inc(s.qkv_ready, 1)
                            dve.wait_ge(s.proj_done, 3 * g + 3)
                            nc.vector.tensor_tensor(v[:, :, :].rearrange("p t d -> p (t d)"),
                                                    k.pb[:, 2, :], bqkv[:, 2, :], ALU.add
                                                    ).then_inc(s.qkv_ready, 1)
                            dve.wait_ge(s.qkv_ready, 5 * g + 2)
                            nc.vector.transpose(qT[:, :, :].rearrange("p n m -> p m n"),
                                                qz[:, :, :, :, :].rearrange(
                                                    "p a c h d -> p (a c) (h d)")
                                                ).then_inc(s.qkvT_ready, 1)
                            dve.wait_ge(s.qkv_ready, 5 * g + 4)
                            nc.vector.transpose(kT[:, :, :].rearrange("p n m -> p m n"),
                                                kd[:, :, :, :].rearrange("p t h d -> p t (h d)")
                                                ).then_inc(s.qkvT_ready, 1)
                            dve.wait_ge(s.qkv_ready, 5 * g + 5)
                            nc.vector.transpose(vT[:, :, 0:HD].rearrange("p n d -> p d n"),
                                                v[:, :, :].rearrange("p t d -> p d t")
                                                ).then_inc(s.qkvT_ready, 1)
                        if slot == "B2":
                            dve.wait_ge(s.scores_done, g + 1)
                            top4 = top[:, :].rearrange("p (b n) -> p b n", b=GB)
                            nc.vector.tensor_reduce(top4, scores, AX.X, ALU.max
                                                    ).then_inc(s.max_done, 1)
                            dve.wait_ge(s.max_done, g + 1)
                            nc.vector.tensor_tensor(
                                e[:, :, :].rearrange("p (b n) t -> p b n t", b=GB), scores,
                                top4.unsqueeze(3).broadcast_to([P, GB, C8, H]),
                                ALU.subtract).then_inc(s.e_ready, 1)
                            dve.wait_ge(s.exp_done, g + 1)
                            nc.vector.transpose(eT[:, :, :], e[:, :, :]).then_inc(s.eT_ready, 1)
                        if slot == "B3":
                            dve.wait_ge(s.pv_done, g + 1)
                            rs4 = rs[:, :].rearrange("p (b n) -> p b n", b=GB)
                            nc.vector.reciprocal(rs4, heads[:, :, :, HD]).then_inc(s.ctx_ready, 1)
                            dve.wait_ge(s.ctx_ready, 3 * g + 1)
                            nc.vector.tensor_tensor(
                                ctxh[:, :, :].rearrange("p (b n) d -> p b n d", b=GB),
                                heads[:, :, :, 0:HD],
                                rs4.unsqueeze(3).broadcast_to([P, GB, C8, HD]),
                                ALU.mult).then_inc(s.ctx_ready, 1)
                            dve.wait_ge(s.ctx_ready, 3 * g + 2)
                            dve.wait_ge(k.out_ready, n)
                            nc.vector.transpose(
                                ctxt[:, :, :, :].rearrange("p c h d -> p d h c"),
                                ctxh[:, :, :].rearrange("p n d -> p d n")
                                ).then_inc(s.ctx_ready, 1)
                steps(dve, groups, base, step)


def phase_experts(nc, k, d, groups, base):
    order = ("C0", "C1", "B0", "C2", "B1", "C3", "B2", "B3", "C4")
    with ExitStack() as ctx:
        def sb(name, shape):
            return ctx.enter_context(nc.sbuf_tensor(name, shape, F32))

        conv_tiles(nc, ctx, k, "f0")
        wbase = sb("wbase", [P, KC, D])
        wag = sb("wag", [P, KC, AG])
        wb = sb("wb", [EX * RK, D])
        bbase = sb("bbase", [P, D])
        nbthr = sb("nbthr", [P, 1])
        gates = sb("gates", [P, EX])
        wts = sb("wts", [P, EX])
        sc = sb("sc", [P, 12])
        ntop, gsum, grec, ez, thr, wsum, wrec, empty = (sc[:, j:j + 1] for j in range(8))
        ag = sb("ag", [P, AG])
        hw = sb("hw", [P, EX, RK])
        hwT = sb("hwT", [EX * RK, P])
        xb = sb("xb", [P, D])
        s = Named()
        s.wf0_loaded = ctx.enter_context(nc.semaphore("wf0_loaded"))
        s.f0_fixed = ctx.enter_context(nc.semaphore("f0_fixed"))
        s.ag_done = ctx.enter_context(nc.semaphore("ag_done"))
        s.ag_ready = ctx.enter_context(nc.semaphore("ag_ready"))
        s.ntop_ready = ctx.enter_context(nc.semaphore("ntop_ready"))
        s.gate_exp = ctx.enter_context(nc.semaphore("gate_exp"))
        s.gate_steps = ctx.enter_context(nc.semaphore("gate_steps"))
        s.hw_turned = ctx.enter_context(nc.semaphore("hw_turned"))
        s.hwT_ready = ctx.enter_context(nc.semaphore("hwT_ready"))
        s.f0_done = ctx.enter_context(nc.semaphore("f0_done"))
        s.xb_ready = ctx.enter_context(nc.semaphore("xb_ready"))
        STEPS = 12

        with nc.Block() as block:
            @block.sync
            def _(sp):
                sp.dma_start(wbase[:, :, :], d["w_base"].rearrange("(c p) n -> p c n", p=P)
                             ).then_inc(s.wf0_loaded, 16)
                sp.dma_start(wag[:, :, :], d["w_ag"].rearrange("(c p) n -> p c n", p=P)
                             ).then_inc(s.wf0_loaded, 16)
                sp.dma_start(wb[:, :], d["w_b"]).then_inc(s.wf0_loaded, 16)
                sp.dma_start(bbase[:, :], d["b_base"].broadcast_to([P, D])
                             ).then_inc(s.wf0_loaded, 16)
                sp.dma_start(nbthr[:, :], d["b_thr"].broadcast_to([P, 1])
                             ).then_inc(s.wf0_loaded, 16)

                def step(t, h, par, conv, blk):
                    if conv:
                        conv_load(sp, k, t, base + t, par)
                    if blk:
                        residual_load(sp, k, t - 1, base + t - 1, 1 - par)
                        store(sp, k, t - 1, base + t - 1, 1 - par)
                steps(sp, groups, base, step)
                for par in range(2):
                    sp.wait_ge(k.stored[par], 8 * (base + groups))

            @block.gpsimd
            def _(pool):
                pool.wait_ge(s.wf0_loaded, 80)

                def step(t, h, par, conv, blk):
                    if blk:
                        n, nh, bpar = base + t - 1, base // 2 + block_half(h, par), 1 - par
                        pool.wait_ge(k.res_loaded[bpar], 16 * nh + 16)
                        pool.wait_ge(k.out_ready, n)
                        nc.gpsimd.tensor_tensor(xb[:, :], k.xres[:, bpar, :], bbase[:, :], ALU.add
                                                ).then_inc(s.xb_ready, 1)
                steps(pool, groups, base, step)

            @block.scalar
            def _(act):
                act.wait_ge(k.edges_zero, 12 * (1 + k.cond))
                act.wait_ge(s.f0_fixed, 1)

                def step(t, h, par, conv, blk):
                    g = t - 1
                    for slot in order:
                        if conv and slot[0] == "C":
                            conv_act(act, nc, k, slot, base + t, base // 2 + h, par)
                        if blk and slot == "B1":
                            act.wait_ge(s.ag_done, g + 1)
                            act.wait_ge(s.gate_steps, STEPS * g)
                            nc.scalar.copy(ag[:, :], k.pb[:, 1, 0:AG]).then_inc(s.ag_ready, 1)
                            act.wait_ge(s.ag_ready, g + 1)
                            nc.scalar.activation(ez, ag[:, AG - 1:AG], ACT.Exp,
                                                 bias=nbthr[:, :], scale=-1.0
                                                 ).then_inc(s.gate_exp, 1)
                            act.wait_ge(s.ntop_ready, 2 * g + 2)
                            nc.scalar.activation(gates[:, :], ag[:, EX * RK:AG - 1], ACT.Exp,
                                                 bias=ntop, accum_out=gsum).then_inc(s.gate_exp, 1)
                        if blk and slot == "B2":
                            act.wait_ge(s.hw_turned, g + 1)
                            nc.scalar.copy(hwT[:, :], k.pb[:, 2, 0:P]).then_inc(s.hwT_ready, 1)
                steps(act, groups, base, step)

            @block.tensor
            def _(pe):
                pe.wait_ge(s.wf0_loaded, 80)

                def step(t, h, par, conv, blk):
                    g, n = t - 1, base + t - 1
                    for slot in order:
                        if conv and slot[0] == "C":
                            conv_tensor(pe, nc, k, slot, base + t)
                        if not blk:
                            continue
                        if slot == "B0":
                            turn_y(pe, nc, k, n, 1 - par)
                        if slot == "B1":
                            pe.wait_ge(k.yT_ready, n + 1)
                            pe.wait_ge(s.gate_steps, STEPS * g)
                            dense(nc, k.pb[:, 1, 0:AG], k.yT, wag, AG).then_inc(s.ag_done, 1)
                            pe.wait_ge(k.out_ready, n)
                            dense(nc, k.pb[:, 0, :], k.yT, wbase, D, last=False)
                        if slot == "B2":
                            pe.wait_ge(s.gate_steps, STEPS * g + STEPS)
                            nc.tensor.transpose(k.pb[:, 2, 0:P],
                                                hw[:, :, :].rearrange("p e r -> p (e r)"),
                                                k.ident[:, :]).then_inc(s.hw_turned, 1)
                        if slot == "B3":
                            pe.wait_ge(s.hwT_ready, g + 1)
                            nc.tensor.matmul(k.pb[:, 0, :], hwT[:, :], wb[:, :], start=False,
                                             stop=True).then_inc(s.f0_done, 1)
                steps(pe, groups, base, step)

            @block.vector
            def _(dve):
                zero_edges(nc, k)
                dve.wait_ge(s.wf0_loaded, 80)
                nc.vector.tensor_scalar(nbthr[:, :], nbthr[:, :], -1.0, None, ALU.mult
                                        ).then_inc(s.f0_fixed, 1)
                dve.wait_ge(s.f0_fixed, 1)
                dve.wait_ge(k.edges_zero, 12 * (1 + k.cond))

                def step(t, h, par, conv, blk):
                    g, n, bpar = t - 1, base + t - 1, 1 - par
                    for slot in order:
                        if conv and slot == "C0":
                            conv_coef(dve, nc, k, t, base + t, par)
                        if conv and slot[0] == "C":
                            conv_vector(dve, nc, k, slot, base + t)
                        if not blk:
                            continue
                        if slot == "B0":
                            copy_yT(dve, nc, k, n)
                        if slot == "B1":
                            v = nc.vector
                            dve.wait_ge(s.ag_ready, g + 1)
                            v.tensor_reduce(ntop, ag[:, EX * RK:AG - 1], AX.X, ALU.max
                                            ).then_inc(s.ntop_ready, 1)
                            dve.wait_ge(s.ntop_ready, 2 * g + 1)
                            v.tensor_scalar(ntop, ntop, -1.0, None, ALU.mult
                                            ).then_inc(s.ntop_ready, 1)
                            dve.wait_ge(s.gate_exp, 2 * g + 1)
                            v.tensor_scalar(thr, ez, 1.0, None, ALU.add).then_inc(s.gate_steps, 1)
                            dve.wait_ge(s.gate_steps, STEPS * g + 1)
                            v.reciprocal(thr, thr).then_inc(s.gate_steps, 1)
                            dve.wait_ge(s.gate_steps, STEPS * g + 2)
                            v.tensor_scalar(thr, thr, MAX_THRESHOLD, None, ALU.mult
                                            ).then_inc(s.gate_steps, 1)
                            dve.wait_ge(s.gate_exp, 2 * g + 2)
                            v.reciprocal(grec, gsum).then_inc(s.gate_steps, 1)
                            dve.wait_ge(s.gate_steps, STEPS * g + 4)
                            v.tensor_scalar(wts[:, :], gates[:, :], grec, thr, ALU.mult,
                                            ALU.subtract).then_inc(s.gate_steps, 1)
                            dve.wait_ge(s.gate_steps, STEPS * g + 5)
                            v.tensor_scalar(wts[:, :], wts[:, :], 0.0, None, ALU.max
                                            ).then_inc(s.gate_steps, 1)
                            dve.wait_ge(s.gate_steps, STEPS * g + 6)
                            v.reduce_sum(wsum, wts[:, :], AX.X).then_inc(s.gate_steps, 1)
                            dve.wait_ge(s.gate_steps, STEPS * g + 7)
                            v.tensor_scalar(empty, wsum, 0.0, None, ALU.is_equal
                                            ).then_inc(s.gate_steps, 1)
                            dve.wait_ge(s.gate_steps, STEPS * g + 8)
                            v.tensor_tensor(wsum, wsum, empty, ALU.add).then_inc(s.gate_steps, 1)
                            dve.wait_ge(s.gate_steps, STEPS * g + 9)
                            v.reciprocal(wrec, wsum).then_inc(s.gate_steps, 1)
                            dve.wait_ge(s.gate_steps, STEPS * g + 10)
                            v.tensor_scalar(wts[:, :], wts[:, :], wrec, LORA_SCALE, ALU.mult,
                                            ALU.mult).then_inc(s.gate_steps, 1)
                            dve.wait_ge(s.gate_steps, STEPS * g + 11)
                            v.tensor_tensor(hw[:, :, :],
                                            ag[:, 0:EX * RK].rearrange("p (e r) -> p e r", e=EX),
                                            wts[:, :].unsqueeze(2).broadcast_to([P, EX, RK]),
                                            ALU.mult).then_inc(s.gate_steps, 1)
                        if slot == "B3":
                            dve.wait_ge(s.f0_done, g + 1)
                            dve.wait_ge(s.xb_ready, g + 1)
                            dve.wait_ge(k.stored[bpar], 16 * (base // 2 + block_half(h, par)))
                            nc.vector.tensor_tensor(k.xout[:, bpar, :], k.pb[:, 0, :], xb[:, :],
                                                    ALU.add).then_inc(k.out_ready, 1)
                steps(dve, groups, base, step)


def prepare_latent(nc, k, d, wq, wvo, kvln, masks):
    with ExitStack() as ctx:
        def sb(name, shape):
            return ctx.enter_context(nc.sbuf_tensor(name, shape, F32))

        wqn = sb("wqn", [NOPE, H, QR])
        wk = sb("wk", [NOPE, H, CR])
        wv = sb("wv", [VD, H, CR])
        wo = sb("wo", [VD, 2, H // 4, D])
        qln = sb("qln", [P, 2])
        s = Named()
        s.wqk_loaded = ctx.enter_context(nc.semaphore("wqk_loaded"))
        s.wv_loaded = ctx.enter_context(nc.semaphore("wv_loaded"))
        s.wpe_loaded = ctx.enter_context(nc.semaphore("wpe_loaded"))
        s.qk_done = ctx.enter_context(nc.semaphore("qk_done"))
        s.qk_ready = ctx.enter_context(nc.semaphore("qk_ready"))
        s.vo_done = ctx.enter_context(nc.semaphore("vo_done"))
        s.vo_ready = ctx.enter_context(nc.semaphore("vo_ready"))
        s.mask_done = ctx.enter_context(nc.semaphore("mask_done"))
        wo_loaded = [ctx.enter_context(nc.semaphore(f"wo_loaded_{b}")) for b in range(2)]
        HB = 512 // CR
        QH = H // 4
        chunks = ((0, P), (P, QR))
        banks = [k.pc[:, 0, :], k.pc[:, 1, :]]
        vbanks = [k.pb[:, 0, :], k.pb[:, 1, :]]
        with nc.Block() as block:
            @block.sync
            def _(sp):
                sp.dma_start(wqn[:, :, :], d["w_q_nope"]).then_inc(s.wqk_loaded, 16)
                sp.dma_start(wk[:, :, :], d["w_k"]).then_inc(s.wqk_loaded, 16)
                for c, (lo, hi) in enumerate(chunks):
                    sp.dma_start(wq[0:hi - lo, c, :, CR:], d["w_q_pe"][lo:hi, :, :]
                                 ).then_inc(s.wpe_loaded, 16)
                    sp.dma_start(qln[0:hi - lo, c:c + 1], d["q_ln"][lo:hi, :]
                                 ).then_inc(s.wpe_loaded, 16)
                sp.dma_start(kvln[:, :], d["kv_ln"].broadcast_to([P, CR])).then_inc(s.wpe_loaded, 16)
                sp.dma_start(wv[:, :, :], d["w_v"]).then_inc(s.wv_loaded, 16)
                for q in range(4):
                    if q >= 2:
                        sp.wait_ge(s.vo_done, (q - 1) * QH // 2)
                    sp.dma_start(wo[:, q % 2, :, :],
                                 d["w_o"][q * QH:(q + 1) * QH, :, :].rearrange("h v n -> v h n")
                                 ).then_inc(wo_loaded[q % 2], 16)

            @block.gpsimd
            def _(pool):
                nc.gpsimd.memset(masks[:, :], 0.0).then_inc(s.mask_done, 1)
                pool.wait_ge(s.mask_done, 1)
                for b in range(GB):
                    rows = slice(b * S, (b + 1) * S)
                    nc.gpsimd.affine_select(out=masks[rows, :], in_=masks[rows, :],
                                            compare_op=ALU.is_ge, fill=MASKED, base=0,
                                            pattern=[[-1, S]], channel_multiplier=1
                                            ).then_inc(s.mask_done, 1)

            @block.tensor
            def _(pe):
                pe.wait_ge(s.wqk_loaded, 32)
                for m in range(H // HB * 2):
                    hb, c = divmod(m, 2)
                    lo, hi = chunks[c]
                    if m >= 2:
                        pe.wait_ge(s.qk_ready, m - 1)
                    for j in range(HB):
                        mm = nc.tensor.matmul(banks[m % 2][0:hi - lo, j * CR:(j + 1) * CR],
                                              wqn[:, hb * HB + j, lo:hi], wk[:, hb * HB + j, :],
                                              start=True, stop=True)
                    mm.then_inc(s.qk_done, 1)
                pe.wait_ge(s.wv_loaded, 16)
                for m in range(H // 2):
                    q = 2 * m // QH
                    pe.wait_ge(wo_loaded[q % 2], 16 * (q // 2 + 1))
                    if m >= 2:
                        pe.wait_ge(s.vo_ready, m - 1)
                    for j in range(2):
                        mm = nc.tensor.matmul(vbanks[m % 2][j * CR:(j + 1) * CR, :],
                                              wv[:, 2 * m + j, :], wo[:, q % 2, (2 * m + j) % QH, :],
                                              start=True, stop=True)
                    mm.then_inc(s.vo_done, 1)

            @block.scalar
            def _(act):
                for m in range(H // 2):
                    act.wait_ge(s.vo_done, m + 1)
                    nc.scalar.copy(wvo[:, m, :], vbanks[m % 2]).then_inc(s.vo_ready, 1)

            @block.vector
            def _(dve):
                dve.wait_ge(s.wpe_loaded, 80)
                for m in range(H // HB * 2):
                    hb, c = divmod(m, 2)
                    rows = chunks[c][1] - chunks[c][0]
                    dve.wait_ge(s.qk_done, m + 1)
                    nc.vector.tensor_scalar(
                        wq[0:rows, c, hb * HB:(hb + 1) * HB, 0:CR],
                        banks[m % 2][0:rows, :].rearrange("p (h n) -> p h n", n=CR),
                        qln[0:rows, c:c + 1], None, ALU.mult).then_inc(s.qk_ready, 1)
                    nc.vector.tensor_scalar(
                        wq[0:rows, c, hb * HB:(hb + 1) * HB, CR:],
                        wq[0:rows, c, hb * HB:(hb + 1) * HB, CR:],
                        qln[0:rows, c:c + 1], None, ALU.mult)


def phase_latent(nc, k, d, groups, base):
    NB = 8
    order = ("C0", "C1", "B0", "B1", "C2", "B2", "Q0", "Q1", "Q2", "Q3", "C3", "Q4", "Q5", "Q6",
             "Q7", "B3", "C4", "B4", "B5")
    with ExitStack() as outer:
        def keep(name, shape):
            return outer.enter_context(nc.sbuf_tensor(name, shape, F32))

        wq = keep("wq", [P, 2, H, CR + RO])
        wvo = keep("wvo", [P, H // 2, D])
        kvln = keep("kvln", [P, CR])
        masks = keep("masks", [P, S])
        prepare_latent(nc, k, d, wq, wvo, kvln, masks)

        ctx = outer
        sb = keep
        conv_tiles(nc, ctx, k, "a1")
        wa = sb("wa", [P, KC, QR + CR + RO])
        cos = sb("cos", [P, RO])
        sin = sb("sin", [P, RO])
        a = sb("a", [P, QR + CR + RO])
        junk = sb("junk", [P, QR])
        ms = sb("ms", [P, 2])
        rms = sb("rms", [P, 2])
        qn = sb("qn", [P, QR])
        kf = sb("kf", [P, CR + RO])
        t1 = sb("t1", [P, RO])
        t2 = sb("t2", [P, RO])
        qnT = sb("qnT", [P, 2, P])
        kfT = sb("kfT", [P, P])
        qs = sb("qs", [P, 2, 4, CR + RO])
        r1 = sb("r1", [P, 4, RO])
        r2 = sb("r2", [P, 4, RO])
        qT = sb("mqT", [P, H, P])
        sc = sb("scores", [P, H, S])
        pr = sb("probs", [P, H, S])
        prT = sb("probsT", [P, H, S])
        top = sb("mtop", [P, H])
        den = sb("mden", [P, H])
        oT = sb("oT", [P, H // 2, GB, S])
        s = Named()
        s.wa_loaded = ctx.enter_context(nc.semaphore("wa_loaded"))
        s.eps_set = ctx.enter_context(nc.semaphore("eps_set"))
        s.a_done = ctx.enter_context(nc.semaphore("a_done"))
        s.a_ready = ctx.enter_context(nc.semaphore("a_ready"))
        s.ms_ready = ctx.enter_context(nc.semaphore("ms_ready"))
        s.root_ready = ctx.enter_context(nc.semaphore("root_ready"))
        s.norm_steps = ctx.enter_context(nc.semaphore("norm_steps"))
        s.kq_turned = ctx.enter_context(nc.semaphore("kq_turned"))
        s.kqT_ready = ctx.enter_context(nc.semaphore("kqT_ready"))
        s.q_done = ctx.enter_context(nc.semaphore("q_done"))
        s.q_copied = ctx.enter_context(nc.semaphore("q_copied"))
        s.rope_steps = ctx.enter_context(nc.semaphore("rope_steps"))
        s.q_turned = ctx.enter_context(nc.semaphore("q_turned"))
        s.qT_ready = ctx.enter_context(nc.semaphore("qT_ready"))
        s.sT_done = ctx.enter_context(nc.semaphore("sT_done"))
        s.s_ready = ctx.enter_context(nc.semaphore("s_ready"))
        s.masked = ctx.enter_context(nc.semaphore("masked"))
        s.soft_steps = ctx.enter_context(nc.semaphore("soft_steps"))
        s.p_exp = ctx.enter_context(nc.semaphore("p_exp"))
        s.p_ready = ctx.enter_context(nc.semaphore("p_ready"))
        s.prT_ready = ctx.enter_context(nc.semaphore("prT_ready"))
        s.pv2_done = ctx.enter_context(nc.semaphore("pv2_done"))
        s.oT_ready = ctx.enter_context(nc.semaphore("oT_ready"))
        s.a1_done = ctx.enter_context(nc.semaphore("a1_done"))
        eps = sb("rmseps", [P, 1])
        NS = 9
        half = RO // 2

        def rotated(x):
            return x[..., half:], x[..., 0:half]

        with nc.Block() as block:
            @block.sync
            def _(sp):
                sp.dma_start(wa[:, :, :], d["w_a"].rearrange("(c p) n -> p c n", p=P)
                             ).then_inc(s.wa_loaded, 16)
                sp.dma_start(cos[:, :], d["rope_cos"]).then_inc(s.wa_loaded, 16)
                sp.dma_start(sin[:, :], d["rope_sin"]).then_inc(s.wa_loaded, 16)

                def step(t, h, par, conv, blk):
                    if conv:
                        conv_load(sp, k, t, base + t, par)
                    if blk:
                        residual_load(sp, k, t - 1, base + t - 1, 1 - par)
                        store(sp, k, t - 1, base + t - 1, 1 - par)
                steps(sp, groups, base, step)
                for par in range(2):
                    sp.wait_ge(k.stored[par], 8 * (base + groups))

            @block.gpsimd
            def _(pool):
                def step(t, h, par, conv, blk):
                    g = t - 1
                    if blk:
                        pool.wait_ge(s.s_ready, g + 1)
                        nc.gpsimd.tensor_tensor(sc[:, :, :], sc[:, :, :],
                                                masks[:, :].unsqueeze(1).broadcast_to([P, H, S]),
                                                ALU.add).then_inc(s.masked, 1)
                        pool.wait_ge(s.soft_steps, 4 * g + 4)
                        nc.gpsimd.tensor_tensor(pr[:, :, :], pr[:, :, :],
                                                den[:, :].unsqueeze(2).broadcast_to([P, H, S]),
                                                ALU.mult).then_inc(s.p_ready, 1)
                steps(pool, groups, base, step)

            @block.scalar
            def _(act):
                act.wait_ge(k.edges_zero, 12 * (1 + k.cond))
                act.wait_ge(s.eps_set, 1)

                def step(t, h, par, conv, blk):
                    g, n = t - 1, base + t - 1
                    for slot in order:
                        if conv and slot[0] == "C":
                            conv_act(act, nc, k, slot, base + t, base // 2 + h, par)
                        if not blk:
                            continue
                        if slot == "B1":
                            act.wait_ge(s.a_done, g + 1)
                            act.wait_ge(s.norm_steps, NS * g)
                            nc.scalar.copy(a[:, :], k.pb[:, 0, 0:QR + CR + RO]
                                           ).then_inc(s.a_ready, 1)
                            act.wait_ge(s.ms_ready, 2 * g + 2)
                            for j, width in enumerate((QR, CR)):
                                nc.scalar.activation(rms[:, j:j + 1], ms[:, j:j + 1], ACT.Sqrt,
                                                     bias=eps[:, :], scale=1.0 / width
                                                     ).then_inc(s.root_ready, 1)
                        if slot == "B2":
                            act.wait_ge(s.kq_turned, 3 * g + 3)
                            nc.scalar.copy(qnT[:, 0, :], k.pb[:, 4, 0:P]).then_inc(s.kqT_ready, 1)
                            nc.scalar.copy(qnT[0:QR - P, 1, :], k.pb[0:QR - P, 4, P:2 * P]
                                           ).then_inc(s.kqT_ready, 1)
                            nc.scalar.copy(kfT[:, :], k.pb[:, 4, 2 * P:3 * P]
                                           ).then_inc(s.kqT_ready, 1)
                        if slot[0] == "Q":
                            j = int(slot[1])
                            act.wait_ge(s.q_done, NB * g + j + 1)
                            if j >= 2:
                                act.wait_ge(s.q_turned, NB * g + j - 1)
                            nc.scalar.copy(qs[:, j % 2, :, :],
                                           k.pb[:, j % 2, :].rearrange("p (h n) -> p h n", h=4)
                                           ).then_inc(s.q_copied, 1)
                            act.wait_ge(s.q_turned, NB * g + j + 1)
                            nc.scalar.copy(qT[:, 4 * j:4 * j + 4, :],
                                           k.pb[:, 2 + j % 2, :].rearrange("p (h n) -> p h n", h=4)
                                           ).then_inc(s.qT_ready, 1)
                        if slot == "B3":
                            act.wait_ge(s.soft_steps, 4 * g + 2)
                            nc.scalar.activation(pr[:, :, :], pr[:, :, :], ACT.Exp,
                                                 scale=MLA_SCALE).then_inc(s.p_exp, 1)
                        if slot == "B4":
                            for b in range(0, GB, 2):
                                act.wait_ge(s.pv2_done, GB * g + b + 1)
                                nc.scalar.copy(oT[:, :, b, :],
                                               k.pb[:, b, :].rearrange("p (h s) -> p h s", s=S)
                                               ).then_inc(s.oT_ready, 1)
                steps(act, groups, base, step)

            @block.tensor
            def _(pe):
                pe.wait_ge(s.wa_loaded, 48)

                def step(t, h, par, conv, blk):
                    g, n = t - 1, base + t - 1
                    for slot in order:
                        if conv and slot[0] == "C":
                            conv_tensor(pe, nc, k, slot, base + t)
                        if not blk:
                            continue
                        if slot == "B0":
                            turn_y(pe, nc, k, n, 1 - par)
                        if slot == "B1":
                            pe.wait_ge(k.yT_ready, n + 1)
                            pe.wait_ge(s.oT_ready, GB * g)
                            dense(nc, k.pb[:, 0, 0:QR + CR + RO], k.yT, wa, QR + CR + RO
                                  ).then_inc(s.a_done, 1)
                        if slot == "B2":
                            pe.wait_ge(s.norm_steps, NS * g + NS)
                            nc.tensor.transpose(k.pb[:, 4, 0:P], qn[:, 0:P], k.ident[:, :]
                                                ).then_inc(s.kq_turned, 1)
                            nc.tensor.transpose(k.pb[0:QR - P, 4, P:2 * P], qn[:, P:QR],
                                                k.ident[:, :]).then_inc(s.kq_turned, 1)
                            nc.tensor.transpose(k.pb[:, 4, 2 * P:3 * P], kf[:, :], k.ident[:, :]
                                                ).then_inc(s.kq_turned, 1)
                        if slot[0] == "Q":
                            j = int(slot[1])
                            if j == 0:
                                pe.wait_ge(s.kqT_ready, 3 * g + 3)
                            if j >= 2:
                                pe.wait_ge(s.q_copied, NB * g + j - 1)
                            for c, rows in enumerate((P, QR - P)):
                                mm = nc.tensor.matmul(
                                    k.pb[:, j % 2, :], qnT[0:rows, c, :],
                                    wq[0:rows, c, 4 * j:4 * j + 4, :].rearrange("p h n -> p (h n)"),
                                    start=(c == 0), stop=(c == 1))
                            mm.then_inc(s.q_done, 1)
                            for i in ([j - 1] if j else []) + ([j] if j == NB - 1 else []):
                                pe.wait_ge(s.rope_steps, 5 * (NB * g + i + 1))
                                if i >= 2:
                                    pe.wait_ge(s.qT_ready, NB * g + i - 1)
                                for m in range(4):
                                    mm = nc.tensor.transpose(
                                        k.pb[:, 2 + i % 2, m * P:(m + 1) * P], qs[:, i % 2, m, :],
                                        k.ident[:, :])
                                mm.then_inc(s.q_turned, 1)
                        if slot == "B3":
                            pe.wait_ge(s.qT_ready, NB * g + NB)
                            for m in range(2):
                                for b in range(GB):
                                    cols = slice(b * S, (b + 1) * S)
                                    mm = nc.tensor.matmul(
                                        k.pb[cols, m, :], kfT[:, cols],
                                        qT[:, m * H // 2:(m + 1) * H // 2, cols],
                                        start=True, stop=True)
                                mm.then_inc(s.sT_done, 1)
                        if slot == "B4":
                            pe.wait_ge(s.prT_ready, g + 1)
                            for b in range(GB):
                                rows = slice(b * S, (b + 1) * S)
                                for hh in range(2):
                                    mm = nc.tensor.matmul(
                                        k.pb[hh * CR:(hh + 1) * CR, b, :], kf[rows, 0:CR],
                                        prT[rows, hh:H:2, :], start=True, stop=True)
                                mm.then_inc(s.pv2_done, 1)
                        if slot == "B5":
                            pe.wait_ge(s.oT_ready, GB * g + GB)
                            for m in range(H // 2):
                                mm = nc.tensor.matmul(
                                    k.pb[:, 4, :], oT[:, m, :, :].rearrange("p b s -> p (b s)"),
                                    wvo[:, m, :], start=(m == 0), stop=(m == H // 2 - 1))
                            mm.then_inc(s.a1_done, 1)
                steps(pe, groups, base, step)

            @block.vector
            def _(dve):
                zero_edges(nc, k)
                nc.vector.memset(eps[:, :], RMS_EPS).then_inc(s.eps_set, 1)
                dve.wait_ge(s.wa_loaded, 48)
                dve.wait_ge(k.edges_zero, 12 * (1 + k.cond))

                def step(t, h, par, conv, blk):
                    g, n, bpar = t - 1, base + t - 1, 1 - par
                    v = nc.vector
                    for slot in order:
                        if conv and slot == "C0":
                            conv_coef(dve, nc, k, t, base + t, par)
                        if conv and slot[0] == "C":
                            conv_vector(dve, nc, k, slot, base + t)
                        if not blk:
                            continue
                        if slot == "B0":
                            copy_yT(dve, nc, k, n)
                        if slot == "B1":
                            dve.wait_ge(s.a_ready, g + 1)
                            dve.wait_ge(s.norm_steps, NS * g)
                            v.tensor_tensor_reduce(out=junk[:, :], in0=a[:, 0:QR], in1=a[:, 0:QR],
                                                   scale=1.0, scalar=0.0, op0=ALU.mult,
                                                   op1=ALU.add, accum_out=ms[:, 0:1]
                                                   ).then_inc(s.ms_ready, 1)
                            dve.wait_ge(s.ms_ready, 2 * g + 1)
                            v.tensor_tensor_reduce(out=junk[:, 0:CR], in0=a[:, QR:QR + CR],
                                                   in1=a[:, QR:QR + CR], scale=1.0, scalar=0.0,
                                                   op0=ALU.mult, op1=ALU.add,
                                                   accum_out=ms[:, 1:2]).then_inc(s.ms_ready, 1)
                            pe_ = a[:, QR + CR:]
                            v.tensor_tensor(t1[:, :], pe_, cos[:, :], ALU.mult
                                            ).then_inc(s.norm_steps, 1)
                            hi, lo = rotated(pe_)
                            v.tensor_tensor(t2[:, 0:half], hi, sin[:, 0:half], ALU.mult
                                            ).then_inc(s.norm_steps, 1)
                            v.tensor_tensor(t2[:, half:], lo, sin[:, half:], ALU.mult
                                            ).then_inc(s.norm_steps, 1)
                            dve.wait_ge(s.norm_steps, NS * g + 3)
                            v.tensor_tensor(kf[:, CR:], t1[:, :], t2[:, :], ALU.add
                                            ).then_inc(s.norm_steps, 1)
                            dve.wait_ge(s.root_ready, 2 * g + 2)
                            v.reciprocal(rms[:, :], rms[:, :]).then_inc(s.norm_steps, 1)
                            dve.wait_ge(s.norm_steps, NS * g + 5)
                            v.tensor_scalar(qn[:, :], a[:, 0:QR], rms[:, 0:1], None, ALU.mult
                                            ).then_inc(s.norm_steps, 1)
                            v.tensor_scalar(kf[:, 0:CR], a[:, QR:QR + CR], rms[:, 1:2], None,
                                            ALU.mult).then_inc(s.norm_steps, 1)
                            dve.wait_ge(s.norm_steps, NS * g + 7)
                            v.tensor_tensor(kf[:, 0:CR], kf[:, 0:CR], kvln[:, :], ALU.mult
                                            ).then_inc(s.norm_steps, 2)
                        if slot[0] == "Q":
                            j = int(slot[1])
                            dve.wait_ge(s.q_copied, NB * g + j + 1)
                            at = 5 * (NB * g + j)
                            pe_ = qs[:, j % 2, :, CR:]
                            c4 = cos[:, :].unsqueeze(1).broadcast_to([P, 4, RO])
                            v.tensor_tensor(r1[:, :, :], pe_, c4, ALU.mult
                                            ).then_inc(s.rope_steps, 1)
                            for lo in (0, half):
                                part = slice(lo, lo + half)
                                other = slice(half - lo, RO - lo)
                                v.tensor_tensor(
                                    r2[:, :, part], pe_[:, :, other],
                                    sin[:, part].unsqueeze(1).broadcast_to([P, 4, half]), ALU.mult
                                    ).then_inc(s.rope_steps, 1)
                            dve.wait_ge(s.rope_steps, at + 3)
                            v.tensor_tensor(qs[:, j % 2, :, CR:], r1[:, :, :], r2[:, :, :], ALU.add
                                            ).then_inc(s.rope_steps, 2)
                        if slot == "B3":
                            for m in range(2):
                                dve.wait_ge(s.sT_done, 2 * g + m + 1)
                                mm = v.transpose(sc[:, m * H // 2:(m + 1) * H // 2, :],
                                                 k.pb[:, m, :].rearrange("p (h s) -> p h s", s=S))
                            mm.then_inc(s.s_ready, 1)
                            dve.wait_ge(s.masked, g + 1)
                            v.tensor_reduce(top[:, :], sc[:, :, :], AX.X, ALU.max
                                            ).then_inc(s.soft_steps, 1)
                            dve.wait_ge(s.soft_steps, 4 * g + 1)
                            v.tensor_tensor(pr[:, :, :], sc[:, :, :],
                                            top[:, :].unsqueeze(2).broadcast_to([P, H, S]),
                                            ALU.subtract).then_inc(s.soft_steps, 1)
                            dve.wait_ge(s.p_exp, g + 1)
                            v.reduce_sum(den[:, :], pr[:, :, :], AX.X).then_inc(s.soft_steps, 1)
                            dve.wait_ge(s.soft_steps, 4 * g + 3)
                            v.reciprocal(den[:, :], den[:, :]).then_inc(s.soft_steps, 1)
                            dve.wait_ge(s.p_ready, g + 1)
                            v.transpose(prT[:, :, :], pr[:, :, :]).then_inc(s.prT_ready, 1)
                        if slot == "B4":
                            for b in range(1, GB, 2):
                                dve.wait_ge(s.pv2_done, GB * g + b + 1)
                                v.tensor_copy(oT[:, :, b, :],
                                              k.pb[:, b, :].rearrange("p (h s) -> p h s", s=S)
                                              ).then_inc(s.oT_ready, 1)
                        if slot == "B5":
                            dve.wait_ge(s.a1_done, g + 1)
                            nh = base // 2 + block_half(h, par)
                            dve.wait_ge(k.res_loaded[bpar], 16 * nh + 16)
                            dve.wait_ge(k.stored[bpar], 16 * nh)
                            v.tensor_tensor(k.xout[:, bpar, :], k.pb[:, 4, :], k.xres[:, bpar, :],
                                            ALU.add).then_inc(k.out_ready, 1)
                steps(dve, groups, base, step)


def phase_signs(nc, k, d, groups, base):
    order = ("C0", "C1", "B0", "C2", "B1", "C3", "B2", "B3", "C4", "B4", "B5")
    with ExitStack() as ctx:
        def sb(name, shape, dt=F32):
            return ctx.enter_context(nc.sbuf_tensor(name, shape, dt))

        conv_tiles(nc, ctx, k, "f1")
        raw = sb("raw", [P, 3, KC, D // 4], mybir.dt.int32)
        w = sb("wsign", [P, 3, KC, D])
        fac = sb("fac", [P, KC])
        two = sb("two", [P, KC])
        scales = sb("scales", [P, 3])
        hid = sb("hid", [P, D])
        hT = sb("hT", [P, KC, P])
        s = Named()
        s.signs_loaded = ctx.enter_context(nc.semaphore("signs_loaded"))
        s.fac_ready = ctx.enter_context(nc.semaphore("fac_ready"))
        s.w_ready = ctx.enter_context(nc.semaphore("w_ready"))
        s.dense_done = ctx.enter_context(nc.semaphore("dense_done"))
        s.hid_ready = ctx.enter_context(nc.semaphore("hid_ready"))
        s.hid_turned = ctx.enter_context(nc.semaphore("hid_turned"))
        s.hT_ready = ctx.enter_context(nc.semaphore("hT_ready"))
        NW = 2 + 3 * KC + 1

        with nc.Block() as block:
            @block.sync
            def _(sp):
                sp.dma_start(raw[:, :, :, :], d["k_signs"].rearrange("j (c p) n -> p j c n", p=P)
                             ).then_inc(s.signs_loaded, 16)
                sp.dma_start(scales[:, :], d["s_scales"].broadcast_to([P, 3])
                             ).then_inc(s.signs_loaded, 16)

                def step(t, h, par, conv, blk):
                    if conv:
                        conv_load(sp, k, t, base + t, par)
                    if blk:
                        residual_load(sp, k, t - 1, base + t - 1, 1 - par)
                        store(sp, k, t - 1, base + t - 1, 1 - par)
                steps(sp, groups, base, step)
                for par in range(2):
                    sp.wait_ge(k.stored[par], 8 * (base + groups))

            @block.gpsimd
            def _(pool):
                nc.gpsimd.memset(fac[:, :], 1.0).then_inc(s.fac_ready, 1)
                pool.wait_ge(s.fac_ready, 1)
                nc.gpsimd.affine_select(out=fac[:, :], in_=fac[:, :], compare_op=ALU.is_ge,
                                        fill=INH, base=EXC - 1, pattern=[[-P, KC]],
                                        channel_multiplier=-1).then_inc(s.fac_ready, 1)

            @block.scalar
            def _(act):
                act.wait_ge(k.edges_zero, 12 * (1 + k.cond))
                act.wait_ge(s.w_ready, NW)

                def step(t, h, par, conv, blk):
                    g = t - 1
                    for slot in order:
                        if conv and slot[0] == "C":
                            conv_act(act, nc, k, slot, base + t, base // 2 + h, par)
                        if blk and slot in ("B1", "B3"):
                            layer = 0 if slot == "B1" else 1
                            act.wait_ge(s.dense_done, 3 * g + layer + 1)
                            act.wait_ge(s.hid_turned, 2 * g + layer)
                            nc.scalar.activation(hid[:, :], k.pb[:, layer, :], ACT.Relu,
                                                 scale=scales[:, layer:layer + 1]
                                                 ).then_inc(s.hid_ready, 1)
                steps(act, groups, base, step)

            @block.tensor
            def _(pe):
                pe.wait_ge(s.w_ready, NW)

                def step(t, h, par, conv, blk):
                    g, n = t - 1, base + t - 1
                    for slot in order:
                        if conv and slot[0] == "C":
                            conv_tensor(pe, nc, k, slot, base + t)
                        if not blk:
                            continue
                        if slot == "B0":
                            turn_y(pe, nc, k, n, 1 - par)
                        if slot == "B1":
                            pe.wait_ge(k.yT_ready, n + 1)
                            dense(nc, k.pb[:, 0, :], k.yT, w[:, 0, :, :]).then_inc(s.dense_done, 1)
                        if slot in ("B2", "B4"):
                            layer = 0 if slot == "B2" else 1
                            pe.wait_ge(s.hid_ready, 2 * g + layer + 1)
                            for c in range(KC):
                                mm = nc.tensor.transpose(k.pb[:, 3, c * P:(c + 1) * P],
                                                         hid[:, c * P:(c + 1) * P], k.ident[:, :])
                            mm.then_inc(s.hid_turned, 1)
                        if slot in ("B3", "B5"):
                            layer = 1 if slot == "B3" else 2
                            pe.wait_ge(s.hT_ready, 2 * g + layer)
                            pe.wait_ge(k.out_ready, n)
                            dense(nc, k.pb[:, layer, :], hT, w[:, layer, :, :]
                                  ).then_inc(s.dense_done, 1)
                steps(pe, groups, base, step)

            @block.vector
            def _(dve):
                zero_edges(nc, k)
                dve.wait_ge(s.signs_loaded, 32)
                dve.wait_ge(s.fac_ready, 2)
                nc.vector.tensor_scalar(two[:, :], fac[:, :], 2.0, None, ALU.mult
                                        ).then_inc(s.w_ready, 1)
                nc.vector.tensor_scalar(scales[:, 0:2], scales[:, 0:2], 2.0, None, ALU.mult
                                        ).then_inc(s.w_ready, 1)
                dve.wait_ge(s.w_ready, 2)
                for j in range(3):
                    for c in range(KC):
                        signs = raw[:, j, c, :].bitcast(U8)
                        if j == 0:
                            nc.vector.tensor_scalar(w[:, j, c, :], signs, 2.0, -1.0, ALU.mult,
                                                    ALU.add).then_inc(s.w_ready, 1)
                        else:
                            nc.vector.tensor_scalar(w[:, j, c, :], signs, two[:, c:c + 1],
                                                    fac[:, c:c + 1], ALU.mult, ALU.subtract
                                                    ).then_inc(s.w_ready, 1)
                dve.wait_ge(k.edges_zero, 12 * (1 + k.cond))
                dve.wait_ge(s.w_ready, NW - 1)
                nc.vector.memset(two[:, :], 0.0).then_inc(s.w_ready, 1)

                def step(t, h, par, conv, blk):
                    g, n, bpar = t - 1, base + t - 1, 1 - par
                    for slot in order:
                        if conv and slot == "C0":
                            conv_coef(dve, nc, k, t, base + t, par)
                        if conv and slot[0] == "C":
                            conv_vector(dve, nc, k, slot, base + t)
                        if not blk:
                            continue
                        if slot == "B0":
                            copy_yT(dve, nc, k, n)
                        if slot in ("B2", "B4"):
                            layer = 0 if slot == "B2" else 1
                            dve.wait_ge(s.hid_turned, 2 * g + layer + 1)
                            dve.wait_ge(s.dense_done, 3 * g + layer + 1)
                            nc.vector.tensor_copy(hT[:, :, :].rearrange("p c t -> p (c t)"),
                                                  k.pb[:, 3, :]).then_inc(s.hT_ready, 1)
                        if slot == "B5":
                            dve.wait_ge(s.dense_done, 3 * g + 3)
                            nh = base // 2 + block_half(h, par)
                            dve.wait_ge(k.res_loaded[bpar], 16 * nh + 16)
                            dve.wait_ge(k.stored[bpar], 16 * nh)
                            nc.vector.scalar_tensor_tensor(
                                out=k.xout[:, bpar, :], in0=k.pb[:, 2, :], scalar=scales[:, 2:3],
                                in1=k.xres[:, bpar, :], op0=ALU.mult, op1=ALU.add
                                ).then_inc(k.out_ready, 1)
                steps(dve, groups, base, step)


PHASES = [phase_attention, phase_experts, phase_latent, phase_signs]


def program(nc, d, out, groups):
    with ExitStack() as ctx:
        k = Named()
        k.prescaled = ctx.enter_context(nc.semaphore("prescaled"))
        k.coef_ready = ctx.enter_context(nc.semaphore("coef_ready"))
        k.conv1_done = ctx.enter_context(nc.semaphore("conv1_done"))
        k.x2_ready = ctx.enter_context(nc.semaphore("x2_ready"))
        k.conv2_done = ctx.enter_context(nc.semaphore("conv2_done"))
        k.y2_ready = ctx.enter_context(nc.semaphore("y2_ready"))
        k.blur1_done = ctx.enter_context(nc.semaphore("blur1_done"))
        k.conv3_done = ctx.enter_context(nc.semaphore("conv3_done"))
        k.y3_ready = ctx.enter_context(nc.semaphore("y3_ready"))
        k.blur2_done = ctx.enter_context(nc.semaphore("blur2_done"))
        k.conv4_done = ctx.enter_context(nc.semaphore("conv4_done"))
        k.y_ready = ctx.enter_context(nc.semaphore("y_ready"))
        k.y_turned = ctx.enter_context(nc.semaphore("y_turned"))
        k.yT_ready = ctx.enter_context(nc.semaphore("yT_ready"))
        k.out_ready = ctx.enter_context(nc.semaphore("out_ready"))
        k.edges_zero = ctx.enter_context(nc.semaphore("edges_zero"))
        k.x_loaded, k.res_loaded, k.stored = (
            [ctx.enter_context(nc.semaphore(f"{name}_{par}")) for par in range(2)]
            for name in ("x_loaded", "res_loaded", "stored"))
        k.convw = ctx.enter_context(nc.sbuf_tensor("convw", [P, CONDS, LAYERS * TAPS, P], F32))
        k.table = ctx.enter_context(nc.sbuf_tensor("table", [P, CONDS, groups, NCOEF], F32))
        k.ident = ctx.enter_context(nc.sbuf_tensor("ident", [P, P], F32))
        prepare(nc, k, d, groups)
        k.pc = ctx.enter_context(nc.psum_tensor("pc", [P, 3, 512], F32))
        k.pb = ctx.enter_context(nc.psum_tensor("pb", [P, 5, 512], F32))
        k.src = d["x"]
        for n, phase in enumerate(PHASES):
            k.cond = n
            k.dst = out if n == len(PHASES) - 1 else \
                nc.dram_tensor(f"x_after_{n}", [groups * P, D], F32, kind="Internal").ap()
            phase(nc, k, d, groups, n * groups)
            k.src = k.dst


def kernel(**inputs):
    import concourse.bacc as bacc
    from concourse.bass_utils import run_bass_kernel_spmd

    a = {n: np.asarray(v) for n, v in inputs.items()}
    batches = a["x"].shape[0]
    conds = ("L0_cond", "L0_cond2", "L1_cond", "L1_cond2")
    cw = np.stack([a[c + "_weights"] for c in conds])
    lhs = np.stack([cw[:, l] if l == 1 else cw[:, l].transpose(0, 2, 1, 3)
                    for l in range(LAYERS)], 1)
    qb = a["L1_attn_Wq_b"].reshape(QR, H, NOPE + RO)
    kvb = a["L1_attn_Wkv_b"].reshape(CR, H, NOPE + VD)
    split = np.concatenate([np.arange(0, RO, 2), np.arange(1, RO, 2)])
    inv = np.float32(1.0) / np.float32(10000.0) ** (np.arange(0, RO, 2, dtype=np.float32) / RO)
    angle = np.outer(np.arange(S, dtype=np.float32), inv).astype(np.float32)
    cos, sin = np.cos(angle), np.sin(angle)
    host = {
        "x": a["x"].reshape(batches * S, D),
        "style_t": a["cond_512"].T,
        "conv_w": lhs.transpose(2, 0, 1, 4, 3).reshape(S, CONDS, LAYERS * TAPS, S),
        "demod_w": cw.transpose(3, 0, 1, 4, 2).reshape(S, CONDS * LAYERS, TAPS, S),
        "mod_wt": np.stack([a[c + "_mod_w"] for c in conds]).reshape(-1, S, STYLE).transpose(2, 0, 1),
        "mod_b": np.stack([a[c + "_mod_b"] for c in conds]).reshape(-1, S).T,
        "conv_b": np.stack([a[c + "_biases"] for c in conds]).reshape(-1, S).T,
        "w_qkv": np.stack([a["L0_attn_w" + j].T for j in "qkv"]),
        "b_qkv": np.stack([a["L0_attn_b" + j] for j in "qkv"]),
        "w_base": a["L0_ffn_W_base"].T,
        "b_base": a["L0_ffn_b_base"].reshape(1, D),
        "w_ag": np.concatenate([a["L0_ffn_A_w"].reshape(EX * RK, D), a["L0_ffn_W_gate"],
                                a["L0_ffn_W_thr"].reshape(1, D)]).T,
        "b_thr": a["L0_ffn_b_thr"].reshape(1, 1),
        "w_b": a["L0_ffn_B_w"].transpose(0, 2, 1).reshape(EX * RK, D),
        "w_a": np.concatenate([a["L1_attn_Wq_a"], a["L1_attn_Wkv_a"][:, :CR],
                               a["L1_attn_Wkv_a"][:, CR:][:, split]], 1),
        "q_ln": a["L1_attn_q_a_ln_w"].reshape(QR, 1),
        "kv_ln": a["L1_attn_kv_a_ln_w"].reshape(1, CR),
        "w_q_nope": qb[:, :, :NOPE].transpose(2, 1, 0),
        "w_q_pe": qb[:, :, NOPE:][:, :, split],
        "w_k": kvb[:, :, :NOPE].transpose(2, 1, 0),
        "w_v": kvb[:, :, NOPE:].transpose(2, 1, 0),
        "w_o": a["L1_attn_Wo"].reshape(H, VD, D),
        "rope_cos": np.tile(np.concatenate([cos, cos], 1), (GB, 1)),
        "rope_sin": np.tile(np.concatenate([-sin, sin], 1), (GB, 1)),
        "k_signs": np.stack([np.ascontiguousarray(a["L1_ffn_k" + j]).view(np.int32) for j in "012"]),
        "s_scales": np.stack([a["L1_ffn_s" + j] for j in "012"]).reshape(1, 3),
    }
    nc = bacc.Bacc("TRN2", target_bir_lowering=False, num_devices=1)
    arrays, dram = {}, {}
    for name, v in host.items():
        v = np.ascontiguousarray(v)
        arrays[name] = v
        dram[name] = nc.dram_tensor(name, v.shape, mybir.dt.from_np(v.dtype),
                                    kind="ExternalInput").ap()
    out = nc.dram_tensor("out", [batches * S, D], F32, kind="ExternalOutput").ap()
    program(nc, dram, out, batches // GB)
    r = run_bass_kernel_spmd(nc, [arrays], core_ids=[0])
    return r.results[0]["out"].reshape(batches, S, D)
```

```python
from contextlib import ExitStack

import numpy as np
import concourse.bass as bass
from concourse import mybir

F32 = mybir.dt.float32
U8 = mybir.dt.uint8
ALU = mybir.AluOpType
ACT = mybir.ActivationFunctionType
AX = mybir.AxisListType

P = 128
D = 512
S = 32
GB = P // S
KC = D // P
STYLE = 64
LAYERS, TAPS = 4, 3
CONDS = 4
CONV_SCALE = 1.0 / float(np.sqrt(S * TAPS ** 2))
CONV_EPS = 1e-8
UP = 2 * D
NCOEF = 9

H = 32
HD = 16
QR, CR, RO = 192, 64, 64
NOPE, VD = 128, 128
RMS_EPS = 1e-6
MLA_SCALE = float(NOPE + RO) ** -0.5
MASKED = -1e30

EX, RK = 8, 16
AG = EX * RK + EX + 1
MAX_THRESHOLD = 0.125
LORA_SCALE = 2.0
EXC = round(D * 0.8)
INH = -4.0


class Named:
    pass


def is_first(count):
    return isinstance(count, int) and count == 0


class Step:

    def __init__(self, t, half, par, groups, before):
        fixed = isinstance(t, int)
        self.conv_a = not fixed or t < groups
        self.conv_b = not fixed or 1 <= t <= groups
        self.blk = not fixed or 2 <= t <= groups + 1
        self.late = not fixed or 3 <= t
        self.t, self.half, self.par = t, half, par
        self.ga, self.gb, self.g, self.gl = t, t - 1, t - 2, t - 3
        self.na, self.nb, self.n, self.nl = (before + x for x in (t, t - 1, t - 2, t - 3))
        self.ma, self.m, self.ml = (before // 2 + x for x in (half, half - 1, half - 2 + par))
        self.pa, self.pb, self.p, self.pl = par, 1 - par, par, 1 - par

    def part(self, late):
        if late:
            return self.late, self.gl, self.nl, self.ml, self.pl
        return self.blk, self.g, self.n, self.m, self.p


def steps(eng, groups, base, body):
    first = 2 if base else 3
    assert groups % 2 == 0 and groups // 2 > first
    for t in range(2 * first):
        body(Step(t, t // 2, t % 2, groups, base))
    with eng.Fori(first, groups // 2) as i:
        body(Step(2 * i, i, 0, groups, base))
        body(Step(2 * i + 1, i, 1, groups, base))
    for t in range(groups, groups + 3):
        body(Step(t, t // 2, t % 2, groups, base))



def conv_load(sp, k, st):
    if not is_first(st.na):
        sp.wait_ge(k.prescaled, st.na - 1)
    sp.dma_start(k.xin[:, st.pa, :], k.src[bass.ds(st.ga * P, P), :]
                 ).then_inc(k.x_loaded[st.pa], 16)


def conv_act(act, nc, k, slot, st):
    n, coef = st.na, k.coef[:, st.pa, :]
    if slot == "C0" and st.conv_a:
        act.wait_ge(k.x_loaded[st.pa], 16 * st.ma + 16)
        act.wait_ge(k.coef_ready, n + 1)
        act.wait_ge(k.conv1_done, n)
        nc.scalar.activation(k.x1[:, 1:1 + D], k.xin[:, st.pa, :], ACT.Copy,
                             scale=coef[:, 0:1]).then_inc(k.prescaled, 1)
    if slot == "C1" and st.conv_a:
        act.wait_ge(k.conv1_done, n + 1)
        act.wait_ge(k.conv2_done, 3 * n)
        nc.scalar.activation(k.x2[:, 1:1 + D], k.pc[:, 0, :], ACT.Identity,
                             bias=coef[:, 2:3], scale=coef[:, 1:2]).then_inc(k.x2_ready, 1)
    if slot == "C2" and st.conv_a:
        act.wait_ge(k.blur1_done, 3 * n)
        for m, (src, lo, cnt) in enumerate(((1, 1, D), (2, 2, D), (0, UP + 1, 1))):
            act.wait_ge(k.conv2_done, 3 * n + m + 1)
            nc.scalar.activation(k.y2[:, lo:lo + 2 * cnt - 1:2], k.pc[:, src, 0:cnt], ACT.Identity,
                                 bias=coef[:, 4:5], scale=coef[:, 3:4]).then_inc(k.y2_ready, 1)
    n, coef = st.nb, k.coef[:, st.pb, :]
    if slot in ("C3a", "C3b") and st.conv_b:
        m = 0 if slot == "C3a" else 1
        act.wait_ge(k.blur2_done, 3 * n)
        act.wait_ge(k.conv3_done, 2 * n + m + 1)
        nc.scalar.activation(k.y3[:, 2 + m * D:2 + (m + 1) * D], k.pc[:, 1 + m, :],
                             ACT.Identity, bias=coef[:, 6:7],
                             scale=coef[:, 5:6]).then_inc(k.y3_ready, 1)
    if slot == "C4" and st.conv_b:
        act.wait_ge(k.conv4_done, n + 1)
        if not is_first(n):
            act.wait_ge(k.y_turned, n - 1)
        nc.scalar.activation(k.y[:, st.pb, :], k.pc[:, 0, :], ACT.Identity,
                             bias=coef[:, 8:9], scale=coef[:, 7:8]).then_inc(k.y_ready, 1)


def conv_vector(dve, nc, k, slot, st):
    n = st.na
    if slot == "C0" and st.conv_a:
        if not is_first(n):
            dve.wait_ge(k.y_ready, n - 1)
        nc.vector.tensor_scalar(k.coef[:, st.pa, :],
                                k.table[:, k.cond, bass.ds(st.ga, 1), :].rearrange(
                                    "p a c -> p (a c)"),
                                1.0, None, ALU.mult).then_inc(k.coef_ready, 1)
    if slot == "C2" and st.conv_a:
        dve.wait_ge(k.y2_ready, 3 * n + 3)
        nc.vector.tensor_tensor(k.blur_a[:, 0:UP + 2], k.y2[:, 0:UP + 2], k.y2[:, 1:UP + 3],
                                ALU.add).then_inc(k.blur1_done, 1)
        dve.wait_ge(k.blur1_done, 3 * n + 1)
        nc.vector.tensor_tensor(k.blur_b[:, 0:UP + 1], k.blur_a[:, 0:UP + 1],
                                k.blur_a[:, 1:UP + 2], ALU.add).then_inc(k.blur1_done, 1)
        dve.wait_ge(k.blur1_done, 3 * n + 2)
        dve.wait_ge(k.conv3_done, 2 * n)
        nc.vector.tensor_tensor(k.x3[:, 1:1 + UP], k.blur_b[:, 0:UP], k.blur_b[:, 1:UP + 1],
                                ALU.add).then_inc(k.blur1_done, 1)
    n = st.nb
    if slot == "C3b" and st.conv_b:
        dve.wait_ge(k.y3_ready, 2 * n + 2)
        nc.vector.tensor_tensor(k.blur_a[:, 0:UP + 3], k.y3[:, 0:UP + 3], k.y3[:, 1:UP + 4],
                                ALU.add).then_inc(k.blur2_done, 1)
        dve.wait_ge(k.blur2_done, 3 * n + 1)
        nc.vector.tensor_tensor(k.blur_b[:, 0:UP + 2], k.blur_a[:, 0:UP + 2],
                                k.blur_a[:, 1:UP + 3], ALU.add).then_inc(k.blur2_done, 1)
        dve.wait_ge(k.blur2_done, 3 * n + 2)
        dve.wait_ge(k.conv4_done, n)
        nc.vector.tensor_tensor(k.x4[:, 0:UP + 1], k.blur_b[:, 0:UP + 1], k.blur_b[:, 1:UP + 2],
                                ALU.add).then_inc(k.blur2_done, 1)


def conv_tensor(pe, nc, k, slot, st):
    def weights(layer, tap):
        return k.convw[:, k.cond, layer * TAPS + tap, :]

    n = st.na
    if slot == "C1" and st.conv_a:
        pe.wait_ge(k.prescaled, n + 1)
        if not is_first(n):
            pe.wait_ge(k.y_ready, n - 1)
        for tap in range(TAPS):
            mm = nc.tensor.matmul(k.pc[:, 0, :], weights(0, tap), k.x1[:, tap:tap + D],
                                  start=(tap == 0), stop=(tap == TAPS - 1))
        mm.then_inc(k.conv1_done, 1)
    if slot == "C2" and st.conv_a:
        pe.wait_ge(k.x2_ready, n + 1)
        pe.wait_ge(k.y3_ready, 2 * n)
        nc.tensor.matmul(k.pc[:, 1, :], weights(1, 0), k.x2[:, 1:1 + D], start=True, stop=False)
        nc.tensor.matmul(k.pc[:, 1, :], weights(1, 2), k.x2[:, 0:D], start=False,
                         stop=True).then_inc(k.conv2_done, 1)
        nc.tensor.matmul(k.pc[:, 2, :], weights(1, 1), k.x2[:, 1:1 + D], start=True,
                         stop=True).then_inc(k.conv2_done, 1)
        nc.tensor.matmul(k.pc[:, 0, 0:1], weights(1, 2), k.x2[:, D:D + 1], start=True,
                         stop=True).then_inc(k.conv2_done, 1)
    n = st.nb
    if slot in ("C3a", "C3b") and st.conv_b:
        m = 0 if slot == "C3a" else 1
        pe.wait_ge(k.blur1_done, 3 * n + 3)
        for tap in range(TAPS):
            mm = nc.tensor.matmul(k.pc[:, 1 + m, :], weights(2, tap),
                                  k.x3[:, m * D + tap:m * D + tap + D],
                                  start=(tap == 0), stop=(tap == TAPS - 1))
        mm.then_inc(k.conv3_done, 1)
    if slot == "C4" and st.conv_b:
        if st.conv_a:
            pe.wait_ge(k.y2_ready, 3 * n + 6)
        pe.wait_ge(k.blur2_done, 3 * n + 3)
        for tap in range(TAPS):
            mm = nc.tensor.matmul(k.pc[:, 0, :], weights(3, tap), k.x4[:, tap:tap + UP - 1:2],
                                  start=(tap == 0), stop=(tap == TAPS - 1))
        mm.then_inc(k.conv4_done, 1)



def residual_load(sp, k, g, n, par):
    if not is_first(n):
        sp.wait_ge(k.out_ready, n - 1)
    sp.dma_start(k.xres[:, par, :], k.src[bass.ds(g * P, P), :]).then_inc(k.res_loaded[par], 16)


def store(sp, k, g, n, par):
    sp.wait_ge(k.out_ready, n + 1)
    sp.dma_start(k.dst[bass.ds(g * P, P), :], k.xout[:, par, :]).then_inc(k.stored[par], 16)


def loads_and_stores(sp, k, groups, base, late):
    def step(st):
        if st.conv_a:
            conv_load(sp, k, st)
        if late and st.late:
            residual_load(sp, k, st.gl, st.nl, st.pl)
            store(sp, k, st.gl, st.nl, st.pl)
        if not late and st.blk:
            residual_load(sp, k, st.g, st.n, st.p)
            store(sp, k, st.g, st.n, st.p)
    steps(sp, groups, base, step)
    for par in range(2):
        sp.wait_ge(k.stored[par], 8 * (base + groups))


def turn_y(pe, nc, k, st):
    pe.wait_ge(k.y_ready, st.n + 1)
    for c in range(KC):
        mm = nc.tensor.transpose(k.pb[:, 4, c * P:(c + 1) * P], k.y[:, st.p, c * P:(c + 1) * P],
                                 k.ident[:, :])
    mm.then_inc(k.y_turned, 1)


def copy_yT(dve, nc, k, n):
    dve.wait_ge(k.y_turned, n + 1)
    nc.vector.tensor_copy(k.yT[:, :, :].rearrange("p c t -> p (c t)"),
                          k.pb[:, 4, :]).then_inc(k.yT_ready, 1)


def dense(nc, out, xT, w, cols=D, last=True):
    for c in range(KC):
        mm = nc.tensor.matmul(out, xT[:, c, :], w[:, c, 0:cols], start=(c == 0),
                              stop=last and c == KC - 1)
    return mm



def conv_tiles(nc, ctx, k, tag):
    def sb(name, shape):
        return ctx.enter_context(nc.sbuf_tensor(f"{name}_{tag}", shape, F32))

    k.xin = sb("xin", [P, 2, D])
    k.coef = sb("coef", [P, 2, NCOEF])
    k.x1 = sb("x1", [P, D + 2])
    k.x2 = sb("x2", [P, D + 2])
    k.y2 = sb("y2", [P, UP + 3])
    k.x3 = sb("x3", [P, UP + 2])
    k.y3 = sb("y3", [P, UP + 4])
    k.x4 = sb("x4", [P, UP + 2])
    k.blur_a = sb("blur_a", [P, UP + 4])
    k.blur_b = sb("blur_b", [P, UP + 4])
    k.y = sb("y", [P, 2, D])
    k.yT = sb("yT", [P, KC, P])
    k.xres = sb("xres", [P, 2, D])
    k.xout = sb("xout", [P, 2, D])


def zero_edges(nc, k):
    last = None
    for tile, cols in ((k.x1, (0, D + 1)), (k.x2, (0, D + 1)), (k.y2, (0, UP + 2)),
                       (k.x3, (0, UP + 1)), (k.y3, (0, 1, UP + 2, UP + 3))):
        for c in cols:
            last = nc.vector.memset(tile[:, c:c + 1], 0.0)
            last.then_inc(k.edges_zero, 1)
    return 12


def prepare(nc, k, d, groups):
    with ExitStack() as ctx:
        def sb(name, shape):
            return ctx.enter_context(nc.sbuf_tensor(name, shape, F32))

        NL = CONDS * LAYERS
        demw = sb("demw", [P, NL, TAPS, S])
        styT = sb("styT", [STYLE, groups * GB])
        modT = sb("modT", [STYLE, NL, S])
        modb = sb("modb", [P, NL])
        bias = sb("bias", [P, NL])
        demsq = sb("demsq", [P, NL, S])
        sty = sb("sty", [P, CONDS, LAYERS, groups])
        stysq = sb("stysq", [P, NL, groups])
        dem = sb("dem", [P, CONDS, LAYERS, groups])
        eps = sb("eps", [P, 1])
        ps = ctx.enter_context(nc.psum_tensor("ps_prep", [P, 5, 512], F32))
        NB = min(NL, 512 // groups)
        assert NB == NL
        s = Named()
        s.zeroed = ctx.enter_context(nc.semaphore("zeroed"))
        s.wloaded = ctx.enter_context(nc.semaphore("wloaded"))
        s.dloaded = ctx.enter_context(nc.semaphore("dloaded"))
        s.ident_ready = ctx.enter_context(nc.semaphore("ident_ready"))
        s.sty_done = ctx.enter_context(nc.semaphore("sty_done"))
        s.sty_ready = ctx.enter_context(nc.semaphore("sty_ready"))
        s.sq_done = ctx.enter_context(nc.semaphore("sq_done"))
        s.dem_done = ctx.enter_context(nc.semaphore("dem_done"))
        s.dem_root = ctx.enter_context(nc.semaphore("dem_root"))
        s.tab_done = ctx.enter_context(nc.semaphore("tab_done"))
        with nc.Block() as block:
            @block.sync
            def _(sp):
                for b in range(GB):
                    rows = slice(b * S, (b + 1) * S)
                    sp.dma_start(demw[rows, :, :, :], d["demod_w"]).then_inc(s.dloaded, 16)
                    sp.dma_start(modb[rows, :], d["mod_b"]).then_inc(s.dloaded, 16)
                    sp.dma_start(bias[rows, :], d["conv_b"]).then_inc(s.dloaded, 16)
                sp.dma_start(styT[:, :], d["style_t"]).then_inc(s.dloaded, 16)
                sp.dma_start(modT[:, :, :], d["mod_wt"]).then_inc(s.dloaded, 16)
                sp.wait_ge(s.zeroed, CONDS)
                for b in range(GB):
                    rows = slice(b * S, (b + 1) * S)
                    for c in range(CONDS):
                        sp.dma_start(k.convw[rows, c, :, rows], d["conv_w"][:, c, :, :]
                                     ).then_inc(s.wloaded, 16)
                sp.wait_ge(s.wloaded, 16 * GB * CONDS)

            @block.gpsimd
            def _(pool):
                for c in range(CONDS):
                    nc.gpsimd.memset(k.convw[:, c, :, :], 0.0).then_inc(s.zeroed, 1)
                nc.gpsimd.memset(k.ident[:, :], 0.0).then_inc(s.ident_ready, 1)
                pool.wait_ge(s.ident_ready, 1)
                nc.gpsimd.affine_select(out=k.ident[:, :], in_=k.ident[:, :],
                                        compare_op=ALU.not_equal, fill=1.0, base=0,
                                        pattern=[[-1, P]], channel_multiplier=1
                                        ).then_inc(s.ident_ready, 1)

            loads = 16 * (3 * GB + 2)

            @block.tensor
            def _(pe):
                pe.wait_ge(s.dloaded, loads)
                for b in range(GB):
                    for l in range(NL):
                        mm = nc.tensor.matmul(ps[b * S:(b + 1) * S, 4, l * groups:(l + 1) * groups],
                                              modT[:, l, :], styT[:, b:GB * groups:GB],
                                              start=True, stop=True)
                mm.then_inc(s.sty_done, 1)
                pe.wait_ge(s.sty_ready, 2)
                pe.wait_ge(s.sq_done, 3)
                for b in range(GB):
                    rows = slice(b * S, (b + 1) * S)
                    for l in range(NL):
                        mm = nc.tensor.matmul(ps[rows, b, l * groups:(l + 1) * groups],
                                              demsq[rows, l, :], stysq[rows, l, :],
                                              start=True, stop=True)
                mm.then_inc(s.dem_done, 1)

            @block.scalar
            def _(act):
                act.wait_ge(s.sq_done, 4)
                act.wait_ge(s.dem_done, 1)
                for b in range(GB):
                    rows = slice(b * S, (b + 1) * S)
                    nc.scalar.activation(dem[rows, :, :, :].rearrange("p c l g -> p (c l g)"),
                                         ps[rows, b, 0:NL * groups], ACT.Sqrt,
                                         bias=eps[rows, :], scale=CONV_SCALE ** 2
                                         ).then_inc(s.dem_root, 1)

            @block.vector
            def _(dve):
                dve.wait_ge(s.dloaded, loads)
                sq = demw[:, :, :, :].rearrange("p l t o -> p (l t o)")
                nc.vector.tensor_tensor(sq, sq, sq, ALU.mult).then_inc(s.sq_done, 1)
                dve.wait_ge(s.sq_done, 1)
                nc.vector.tensor_tensor(demsq[:, :, :], demw[:, :, 0, :], demw[:, :, 1, :],
                                        ALU.add).then_inc(s.sq_done, 1)
                dve.wait_ge(s.sq_done, 2)
                nc.vector.tensor_tensor(demsq[:, :, :], demsq[:, :, :], demw[:, :, 2, :],
                                        ALU.add).then_inc(s.sq_done, 1)
                nc.vector.memset(eps[:, :], CONV_EPS).then_inc(s.sq_done, 1)
                dve.wait_ge(s.sty_done, 1)
                styf = sty[:, :, :, :].rearrange("p c l g -> p (c l) g")
                nc.vector.tensor_tensor(
                    styf, ps[:, 4, 0:NL * groups].rearrange("p (l g) -> p l g", l=NL),
                    modb[:, :].unsqueeze(2).broadcast_to([P, NL, groups]),
                    ALU.add).then_inc(s.sty_ready, 1)
                dve.wait_ge(s.sty_ready, 1)
                nc.vector.tensor_tensor(stysq[:, :, :], styf, styf, ALU.mult
                                        ).then_inc(s.sty_ready, 1)
                dve.wait_ge(s.dem_root, GB)
                dall = dem[:, :, :, :].rearrange("p c l g -> p (c l g)")
                nc.vector.reciprocal(dall, dall).then_inc(s.tab_done, 1)
                dve.wait_ge(s.tab_done, 1)
                nc.vector.tensor_scalar(dall, dall, CONV_SCALE, None, ALU.mult
                                        ).then_inc(s.tab_done, 1)
                dve.wait_ge(s.tab_done, 2)
                tab = [k.table[:, :, :, j] for j in range(NCOEF)]
                bl = [bias[:, l:CONDS * LAYERS:LAYERS].unsqueeze(2).broadcast_to([P, CONDS, groups])
                      for l in range(LAYERS)]
                st = [sty[:, :, l, :] for l in range(LAYERS)]
                dm = [dem[:, :, l, :] for l in range(LAYERS)]
                nc.vector.tensor_copy(tab[0], st[0]).then_inc(s.tab_done, 1)
                nc.vector.tensor_tensor(tab[1], dm[0], dm[1], ALU.mult).then_inc(s.tab_done, 1)
                nc.vector.tensor_tensor(tab[2], bl[0], dm[1], ALU.mult).then_inc(s.tab_done, 1)
                nc.vector.scalar_tensor_tensor(out=tab[3], in0=st[1], scalar=0.25, in1=st[2],
                                               op0=ALU.mult, op1=ALU.mult).then_inc(s.tab_done, 1)
                nc.vector.scalar_tensor_tensor(out=tab[4], in0=st[2], scalar=0.25, in1=bl[1],
                                               op0=ALU.mult, op1=ALU.mult).then_inc(s.tab_done, 1)
                nc.vector.scalar_tensor_tensor(out=tab[5], in0=dm[2], scalar=0.125, in1=st[3],
                                               op0=ALU.mult, op1=ALU.mult).then_inc(s.tab_done, 1)
                nc.vector.scalar_tensor_tensor(out=tab[6], in0=st[3], scalar=0.125, in1=bl[2],
                                               op0=ALU.mult, op1=ALU.mult).then_inc(s.tab_done, 1)
                nc.vector.tensor_copy(tab[7], dm[3]).then_inc(s.tab_done, 1)
                nc.vector.tensor_copy(tab[8], bl[3]).then_inc(s.tab_done, 1)
                dve.wait_ge(s.tab_done, 11)


def phase_attention(nc, k, d, groups, base):
    order = ("C0", "C3a", "B3", "B0", "C3b", "B1", "C1", "C2", "B2", "C4")
    late = ("B3",)
    with ExitStack() as ctx:
        def sb(name, shape):
            return ctx.enter_context(nc.sbuf_tensor(name, shape, F32))

        conv_tiles(nc, ctx, k, "a0")
        w = sb("wqkv", [P, 3, KC, D])
        bqkv = sb("bqkv", [P, 3, D])
        yTv = sb("yTv", [P, KC, P])
        qz = sb("qz", [P, 2, H // 2, 2, HD])
        kd = sb("kd", [P, H, 2, HD])
        v = sb("v", [P, H, HD])
        qT = sb("qT", [P, S, H])
        kT = sb("kT", [P, S, H])
        vT = sb("vT", [P, S, HD + 1])
        e = sb("e", [P, GB * 8, H])
        eT = sb("eT", [P, GB * 8, H])
        top = sb("top", [P, GB * 8])
        rs = sb("rs", [P, GB * 8])
        ctxh = sb("ctxh", [P, GB * 8, HD])
        ctxt = sb("ctxt", [P, H // 2, 2, HD])
        s = Named()
        s.wqkv_loaded = ctx.enter_context(nc.semaphore("wqkv_loaded"))
        s.fixed = ctx.enter_context(nc.semaphore("fixed"))
        s.yTv_ready = ctx.enter_context(nc.semaphore("yTv_ready"))
        s.proj_done = ctx.enter_context(nc.semaphore("proj_done"))
        s.qkv_ready = ctx.enter_context(nc.semaphore("qkv_ready"))
        s.qkvT_ready = ctx.enter_context(nc.semaphore("qkvT_ready"))
        s.scores_done = ctx.enter_context(nc.semaphore("scores_done"))
        s.max_done = ctx.enter_context(nc.semaphore("max_done"))
        s.e_ready = ctx.enter_context(nc.semaphore("e_ready"))
        s.exp_done = ctx.enter_context(nc.semaphore("exp_done"))
        s.eT_ready = ctx.enter_context(nc.semaphore("eT_ready"))
        s.pv_done = ctx.enter_context(nc.semaphore("pv_done"))
        s.ctx_ready = ctx.enter_context(nc.semaphore("ctx_ready"))
        C8 = 8
        scores = k.pb[:, 0:4, 0:C8 * H].rearrange("p b (n t) -> p b n t", n=C8)
        heads = k.pb[:, 0:4, 0:C8 * (HD + 1)].rearrange("p b (n d) -> p b n d", n=C8)

        with nc.Block() as block:
            @block.sync
            def _(sp):
                sp.dma_start(w[:, :, :, :], d["w_qkv"].rearrange("j (c p) n -> p j c n", p=P)
                             ).then_inc(s.wqkv_loaded, 16)
                for j in range(3):
                    sp.dma_start(bqkv[:, j, :], d["b_qkv"][j:j + 1, :].broadcast_to([P, D])
                                 ).then_inc(s.wqkv_loaded, 16)

                loads_and_stores(sp, k, groups, base, True)

            @block.gpsimd
            def _(pool):
                def step(st):
                    on, g, n, m, p = st.part(True)
                    if on:
                        pool.wait_ge(s.ctx_ready, 3 * g + 3)
                        pool.wait_ge(k.res_loaded[p], 16 * m + 16)
                        pool.wait_ge(k.stored[p], 16 * m)
                        nc.gpsimd.tensor_tensor(
                            k.xout[:, p, :], ctxt[:, :, :, :].rearrange("p c h d -> p (c h d)"),
                            k.xres[:, p, :], ALU.add).then_inc(k.out_ready, 1)
                steps(pool, groups, base, step)

            @block.scalar
            def _(act):
                act.wait_ge(k.edges_zero, 12 * (1 + k.cond))

                def step(st):
                    for slot in order:
                        conv_act(act, nc, k, slot, st)
                        on, g, n, m, p = st.part(slot in late)
                        if not on:
                            continue
                        if slot == "B1":
                            act.wait_ge(s.proj_done, 3 * g)
                            act.wait_ge(k.yT_ready, n + 1)
                            for c in range(KC):
                                nc.scalar.copy(
                                    yTv[:, c, :].rearrange("p (g q n) -> p g q n", q=GB, g=GB),
                                    k.yT[:, c, :].rearrange("p (q g n) -> p g q n", q=GB, g=GB)
                                    ).then_inc(s.yTv_ready, 1)
                        if slot == "B2":
                            act.wait_ge(s.e_ready, g + 1)
                            nc.scalar.activation(e[:, :, :], e[:, :, :], ACT.Exp,
                                                 scale=float(HD) ** -0.5).then_inc(s.exp_done, 1)
                steps(act, groups, base, step)

            @block.tensor
            def _(pe):
                pe.wait_ge(s.wqkv_loaded, 64)

                def step(st):
                    for slot in order:
                        conv_tensor(pe, nc, k, slot, st)
                        on, g, n, m, p = st.part(slot in late)
                        if not on:
                            continue
                        if slot == "B0":
                            turn_y(pe, nc, k, st)
                        if slot == "B1":
                            pe.wait_ge(k.yT_ready, n + 1)
                            pe.wait_ge(s.ctx_ready, 3 * g)
                            dense(nc, k.pb[:, 0, :], k.yT, w[:, 0, :, :]).then_inc(s.proj_done, 1)
                            dense(nc, k.pb[:, 1, :], k.yT, w[:, 1, :, :]).then_inc(s.proj_done, 1)
                            pe.wait_ge(s.yTv_ready, KC * (g + 1))
                            dense(nc, k.pb[:, 2, :], yTv, w[:, 2, :, :]).then_inc(s.proj_done, 1)
                        if slot == "B2":
                            pe.wait_ge(s.fixed, 2)
                            pe.wait_ge(s.qkvT_ready, 3 * g + 3)
                            pe.nop(nofuse=True)
                            for i in range(C8):
                                for q in range(GB):
                                    for c in range(GB):
                                        rows = slice(q * S, (q + 1) * S)
                                        mm = nc.tensor.matmul(
                                            k.pb[c * S:(c + 1) * S, q, i * H:(i + 1) * H],
                                            qT[rows, c * C8 + i, :], kT[rows, c * C8 + i, :],
                                            start=True, stop=True)
                            mm.then_inc(s.scores_done, 1)
                        if slot == "B3":
                            pe.wait_ge(s.fixed, 2)
                            pe.wait_ge(s.eT_ready, g + 1)
                            pe.nop(nofuse=True)
                            for i in range(C8):
                                for c in range(GB):
                                    for q in range(GB):
                                        rows = slice(c * S, (c + 1) * S)
                                        mm = nc.tensor.matmul(
                                            k.pb[q * S:(q + 1) * S, c,
                                                 i * (HD + 1):(i + 1) * (HD + 1)],
                                            eT[rows, q * C8 + i, :], vT[rows, q * C8 + i, :],
                                            start=True, stop=True)
                            mm.then_inc(s.pv_done, 1)
                steps(pe, groups, base, step)

            @block.vector
            def _(dve):
                zero_edges(nc, k)
                nc.vector.memset(qz[:, :, :, :, :].rearrange("p a c h d -> p (a c h d)"), 0.0
                                 ).then_inc(s.fixed, 1)
                nc.vector.memset(vT[:, :, HD:HD + 1], 1.0).then_inc(s.fixed, 1)
                dve.wait_ge(s.fixed, 2)
                dve.wait_ge(k.edges_zero, 12 * (1 + k.cond))
                dve.wait_ge(s.wqkv_loaded, 64)

                def step(st):
                    for slot in order:
                        conv_vector(dve, nc, k, slot, st)
                        on, g, n, m, p = st.part(slot in late)
                        if not on:
                            continue
                        if slot == "B0":
                            copy_yT(dve, nc, k, n)
                        if slot == "B1":
                            dve.wait_ge(s.proj_done, 3 * g + 1)
                            qp = k.pb[:, 0, :].rearrange("p (c h d) -> p c h d", h=2, d=HD)
                            qb = bqkv[:, 0, :].rearrange("p (c h d) -> p c h d", h=2, d=HD)
                            for h in range(2):
                                nc.vector.tensor_tensor(qz[:, h, :, h, :], qp[:, :, h, :],
                                                        qb[:, :, h, :], ALU.add
                                                        ).then_inc(s.qkv_ready, 1)
                            dve.wait_ge(s.proj_done, 3 * g + 2)
                            kp = k.pb[:, 1, :].rearrange("p (t d) -> p t d", d=HD)
                            kb = bqkv[:, 1, :].rearrange("p (t d) -> p t d", d=HD)
                            for h in range(2):
                                nc.vector.tensor_tensor(kd[:, :, h, :], kp, kb, ALU.add
                                                        ).then_inc(s.qkv_ready, 1)
                            dve.wait_ge(s.proj_done, 3 * g + 3)
                            nc.vector.tensor_tensor(v[:, :, :].rearrange("p t d -> p (t d)"),
                                                    k.pb[:, 2, :], bqkv[:, 2, :], ALU.add
                                                    ).then_inc(s.qkv_ready, 1)
                            dve.wait_ge(s.qkv_ready, 5 * g + 2)
                            nc.vector.transpose(qT[:, :, :].rearrange("p n m -> p m n"),
                                                qz[:, :, :, :, :].rearrange(
                                                    "p a c h d -> p (a c) (h d)")
                                                ).then_inc(s.qkvT_ready, 1)
                            dve.wait_ge(s.qkv_ready, 5 * g + 4)
                            nc.vector.transpose(kT[:, :, :].rearrange("p n m -> p m n"),
                                                kd[:, :, :, :].rearrange("p t h d -> p t (h d)")
                                                ).then_inc(s.qkvT_ready, 1)
                            dve.wait_ge(s.qkv_ready, 5 * g + 5)
                            nc.vector.transpose(vT[:, :, 0:HD].rearrange("p n d -> p d n"),
                                                v[:, :, :].rearrange("p t d -> p d t")
                                                ).then_inc(s.qkvT_ready, 1)
                        if slot == "B2":
                            dve.wait_ge(s.scores_done, g + 1)
                            top4 = top[:, :].rearrange("p (b n) -> p b n", b=GB)
                            nc.vector.tensor_reduce(top4, scores, AX.X, ALU.max
                                                    ).then_inc(s.max_done, 1)
                            dve.wait_ge(s.max_done, g + 1)
                            nc.vector.tensor_tensor(
                                e[:, :, :].rearrange("p (b n) t -> p b n t", b=GB), scores,
                                top4.unsqueeze(3).broadcast_to([P, GB, C8, H]),
                                ALU.subtract).then_inc(s.e_ready, 1)
                            dve.wait_ge(s.exp_done, g + 1)
                            nc.vector.transpose(eT[:, :, :], e[:, :, :]).then_inc(s.eT_ready, 1)
                        if slot == "B3":
                            dve.wait_ge(s.pv_done, g + 1)
                            rs4 = rs[:, :].rearrange("p (b n) -> p b n", b=GB)
                            nc.vector.reciprocal(rs4, heads[:, :, :, HD]).then_inc(s.ctx_ready, 1)
                            dve.wait_ge(s.ctx_ready, 3 * g + 1)
                            nc.vector.tensor_tensor(
                                ctxh[:, :, :].rearrange("p (b n) d -> p b n d", b=GB),
                                heads[:, :, :, 0:HD],
                                rs4.unsqueeze(3).broadcast_to([P, GB, C8, HD]),
                                ALU.mult).then_inc(s.ctx_ready, 1)
                            dve.wait_ge(s.ctx_ready, 3 * g + 2)
                            dve.wait_ge(k.out_ready, n)
                            nc.vector.transpose(
                                ctxt[:, :, :, :].rearrange("p c h d -> p d h c"),
                                ctxh[:, :, :].rearrange("p n d -> p d n")
                                ).then_inc(s.ctx_ready, 1)
                steps(dve, groups, base, step)


def phase_experts(nc, k, d, groups, base):
    order = ("C0", "C3a", "B0", "C3b", "B1", "C1", "C2", "B2", "C4", "B3")
    late = ()
    with ExitStack() as ctx:
        def sb(name, shape):
            return ctx.enter_context(nc.sbuf_tensor(name, shape, F32))

        conv_tiles(nc, ctx, k, "f0")
        wbase = sb("wbase", [P, KC, D])
        wag = sb("wag", [P, KC, AG])
        wb = sb("wb", [EX * RK, D])
        bbase = sb("bbase", [P, D])
        nbthr = sb("nbthr", [P, 1])
        gates = sb("gates", [P, EX])
        wts = sb("wts", [P, EX])
        sc = sb("sc", [P, 12])
        ntop, gsum, grec, ez, thr, wsum, wrec, empty = (sc[:, j:j + 1] for j in range(8))
        ag = sb("ag", [P, AG])
        hw = sb("hw", [P, EX, RK])
        hwT = sb("hwT", [EX * RK, P])
        xb = sb("xb", [P, D])
        s = Named()
        s.wf0_loaded = ctx.enter_context(nc.semaphore("wf0_loaded"))
        s.f0_fixed = ctx.enter_context(nc.semaphore("f0_fixed"))
        s.ag_done = ctx.enter_context(nc.semaphore("ag_done"))
        s.ag_ready = ctx.enter_context(nc.semaphore("ag_ready"))
        s.ntop_ready = ctx.enter_context(nc.semaphore("ntop_ready"))
        s.gate_exp = ctx.enter_context(nc.semaphore("gate_exp"))
        s.gate_steps = ctx.enter_context(nc.semaphore("gate_steps"))
        s.hw_turned = ctx.enter_context(nc.semaphore("hw_turned"))
        s.hwT_ready = ctx.enter_context(nc.semaphore("hwT_ready"))
        s.f0_done = ctx.enter_context(nc.semaphore("f0_done"))
        s.xb_ready = ctx.enter_context(nc.semaphore("xb_ready"))
        STEPS = 12

        with nc.Block() as block:
            @block.sync
            def _(sp):
                sp.dma_start(wbase[:, :, :], d["w_base"].rearrange("(c p) n -> p c n", p=P)
                             ).then_inc(s.wf0_loaded, 16)
                sp.dma_start(wag[:, :, :], d["w_ag"].rearrange("(c p) n -> p c n", p=P)
                             ).then_inc(s.wf0_loaded, 16)
                sp.dma_start(wb[:, :], d["w_b"]).then_inc(s.wf0_loaded, 16)
                sp.dma_start(bbase[:, :], d["b_base"].broadcast_to([P, D])
                             ).then_inc(s.wf0_loaded, 16)
                sp.dma_start(nbthr[:, :], d["b_thr"].broadcast_to([P, 1])
                             ).then_inc(s.wf0_loaded, 16)

                loads_and_stores(sp, k, groups, base, False)

            @block.gpsimd
            def _(pool):
                pool.wait_ge(s.wf0_loaded, 80)

                def step(st):
                    on, g, n, m, p = st.part(False)
                    if on:
                        pool.wait_ge(k.res_loaded[p], 16 * m + 16)
                        pool.wait_ge(k.out_ready, n)
                        nc.gpsimd.tensor_tensor(xb[:, :], k.xres[:, p, :], bbase[:, :], ALU.add
                                                ).then_inc(s.xb_ready, 1)
                steps(pool, groups, base, step)

            @block.scalar
            def _(act):
                act.wait_ge(k.edges_zero, 12 * (1 + k.cond))
                act.wait_ge(s.f0_fixed, 1)

                def step(st):
                    for slot in order:
                        conv_act(act, nc, k, slot, st)
                        on, g, n, m, p = st.part(slot in late)
                        if not on:
                            continue
                        if slot == "B1":
                            act.wait_ge(s.ag_done, g + 1)
                            act.wait_ge(s.gate_steps, STEPS * g)
                            nc.scalar.copy(ag[:, :], k.pb[:, 1, 0:AG]).then_inc(s.ag_ready, 1)
                            act.wait_ge(s.ag_ready, g + 1)
                            nc.scalar.activation(ez, ag[:, AG - 1:AG], ACT.Exp,
                                                 bias=nbthr[:, :], scale=-1.0
                                                 ).then_inc(s.gate_exp, 1)
                            act.wait_ge(s.ntop_ready, 2 * g + 2)
                            nc.scalar.activation(gates[:, :], ag[:, EX * RK:AG - 1], ACT.Exp,
                                                 bias=ntop, accum_out=gsum).then_inc(s.gate_exp, 1)
                        if slot == "B2":
                            act.wait_ge(s.hw_turned, g + 1)
                            nc.scalar.copy(hwT[:, :], k.pb[:, 2, 0:P]).then_inc(s.hwT_ready, 1)
                steps(act, groups, base, step)

            @block.tensor
            def _(pe):
                pe.wait_ge(s.wf0_loaded, 80)

                def step(st):
                    for slot in order:
                        conv_tensor(pe, nc, k, slot, st)
                        on, g, n, m, p = st.part(slot in late)
                        if not on:
                            continue
                        if slot == "B0":
                            turn_y(pe, nc, k, st)
                        if slot == "B1":
                            pe.wait_ge(k.yT_ready, n + 1)
                            pe.wait_ge(s.gate_steps, STEPS * g)
                            dense(nc, k.pb[:, 1, 0:AG], k.yT, wag, AG).then_inc(s.ag_done, 1)
                            pe.wait_ge(k.out_ready, n)
                            dense(nc, k.pb[:, 0, :], k.yT, wbase, D, last=False)
                        if slot == "B2":
                            pe.wait_ge(s.gate_steps, STEPS * g + STEPS)
                            nc.tensor.transpose(k.pb[:, 2, 0:P],
                                                hw[:, :, :].rearrange("p e r -> p (e r)"),
                                                k.ident[:, :]).then_inc(s.hw_turned, 1)
                        if slot == "B3":
                            pe.wait_ge(s.hwT_ready, g + 1)
                            nc.tensor.matmul(k.pb[:, 0, :], hwT[:, :], wb[:, :], start=False,
                                             stop=True).then_inc(s.f0_done, 1)
                steps(pe, groups, base, step)

            @block.vector
            def _(dve):
                zero_edges(nc, k)
                dve.wait_ge(s.wf0_loaded, 80)
                nc.vector.tensor_scalar(nbthr[:, :], nbthr[:, :], -1.0, None, ALU.mult
                                        ).then_inc(s.f0_fixed, 1)
                dve.wait_ge(s.f0_fixed, 1)
                dve.wait_ge(k.edges_zero, 12 * (1 + k.cond))

                def step(st):
                    for slot in order:
                        conv_vector(dve, nc, k, slot, st)
                        on, g, n, m, p = st.part(slot in late)
                        if not on:
                            continue
                        if slot == "B0":
                            copy_yT(dve, nc, k, n)
                        if slot == "B1":
                            v = nc.vector
                            dve.wait_ge(s.ag_ready, g + 1)
                            v.tensor_reduce(ntop, ag[:, EX * RK:AG - 1], AX.X, ALU.max
                                            ).then_inc(s.ntop_ready, 1)
                            dve.wait_ge(s.ntop_ready, 2 * g + 1)
                            v.tensor_scalar(ntop, ntop, -1.0, None, ALU.mult
                                            ).then_inc(s.ntop_ready, 1)
                            dve.wait_ge(s.gate_exp, 2 * g + 1)
                            v.tensor_scalar(thr, ez, 1.0, None, ALU.add).then_inc(s.gate_steps, 1)
                            dve.wait_ge(s.gate_steps, STEPS * g + 1)
                            v.reciprocal(thr, thr).then_inc(s.gate_steps, 1)
                            dve.wait_ge(s.gate_steps, STEPS * g + 2)
                            v.tensor_scalar(thr, thr, MAX_THRESHOLD, None, ALU.mult
                                            ).then_inc(s.gate_steps, 1)
                            dve.wait_ge(s.gate_exp, 2 * g + 2)
                            v.reciprocal(grec, gsum).then_inc(s.gate_steps, 1)
                            dve.wait_ge(s.gate_steps, STEPS * g + 4)
                            v.tensor_scalar(wts[:, :], gates[:, :], grec, thr, ALU.mult,
                                            ALU.subtract).then_inc(s.gate_steps, 1)
                            dve.wait_ge(s.gate_steps, STEPS * g + 5)
                            v.tensor_scalar(wts[:, :], wts[:, :], 0.0, None, ALU.max
                                            ).then_inc(s.gate_steps, 1)
                            dve.wait_ge(s.gate_steps, STEPS * g + 6)
                            v.reduce_sum(wsum, wts[:, :], AX.X).then_inc(s.gate_steps, 1)
                            dve.wait_ge(s.gate_steps, STEPS * g + 7)
                            v.tensor_scalar(empty, wsum, 0.0, None, ALU.is_equal
                                            ).then_inc(s.gate_steps, 1)
                            dve.wait_ge(s.gate_steps, STEPS * g + 8)
                            v.tensor_tensor(wsum, wsum, empty, ALU.add).then_inc(s.gate_steps, 1)
                            dve.wait_ge(s.gate_steps, STEPS * g + 9)
                            v.reciprocal(wrec, wsum).then_inc(s.gate_steps, 1)
                            dve.wait_ge(s.gate_steps, STEPS * g + 10)
                            v.tensor_scalar(wts[:, :], wts[:, :], wrec, LORA_SCALE, ALU.mult,
                                            ALU.mult).then_inc(s.gate_steps, 1)
                            dve.wait_ge(s.gate_steps, STEPS * g + 11)
                            v.tensor_tensor(hw[:, :, :],
                                            ag[:, 0:EX * RK].rearrange("p (e r) -> p e r", e=EX),
                                            wts[:, :].unsqueeze(2).broadcast_to([P, EX, RK]),
                                            ALU.mult).then_inc(s.gate_steps, 1)
                        if slot == "B3":
                            dve.wait_ge(s.f0_done, g + 1)
                            dve.wait_ge(s.xb_ready, g + 1)
                            dve.wait_ge(k.stored[p], 16 * m)
                            nc.vector.tensor_tensor(k.xout[:, p, :], k.pb[:, 0, :], xb[:, :],
                                                    ALU.add).then_inc(k.out_ready, 1)
                steps(dve, groups, base, step)


def prepare_latent(nc, k, d, wq, wvo, kvln, masks):
    with ExitStack() as ctx:
        def sb(name, shape):
            return ctx.enter_context(nc.sbuf_tensor(name, shape, F32))

        wqn = sb("wqn", [NOPE, H, QR])
        wk = sb("wk", [NOPE, H, CR])
        wv = sb("wv", [VD, H, CR])
        wo = sb("wo", [VD, 2, H // 4, D])
        qln = sb("qln", [P, 2])
        s = Named()
        s.wqk_loaded = ctx.enter_context(nc.semaphore("wqk_loaded"))
        s.wv_loaded = ctx.enter_context(nc.semaphore("wv_loaded"))
        s.wpe_loaded = ctx.enter_context(nc.semaphore("wpe_loaded"))
        s.qk_done = ctx.enter_context(nc.semaphore("qk_done"))
        s.qk_ready = ctx.enter_context(nc.semaphore("qk_ready"))
        s.vo_done = ctx.enter_context(nc.semaphore("vo_done"))
        s.vo_ready = ctx.enter_context(nc.semaphore("vo_ready"))
        s.mask_done = ctx.enter_context(nc.semaphore("mask_done"))
        wo_loaded = [ctx.enter_context(nc.semaphore(f"wo_loaded_{b}")) for b in range(2)]
        HB = 512 // CR
        QH = H // 4
        chunks = ((0, P), (P, QR))
        banks = [k.pc[:, 0, :], k.pc[:, 1, :]]
        vbanks = [k.pb[:, 0, :], k.pb[:, 1, :]]
        with nc.Block() as block:
            @block.sync
            def _(sp):
                sp.dma_start(wqn[:, :, :], d["w_q_nope"]).then_inc(s.wqk_loaded, 16)
                sp.dma_start(wk[:, :, :], d["w_k"]).then_inc(s.wqk_loaded, 16)
                for c, (lo, hi) in enumerate(chunks):
                    sp.dma_start(wq[0:hi - lo, c, :, CR:], d["w_q_pe"][lo:hi, :, :]
                                 ).then_inc(s.wpe_loaded, 16)
                    sp.dma_start(qln[0:hi - lo, c:c + 1], d["q_ln"][lo:hi, :]
                                 ).then_inc(s.wpe_loaded, 16)
                sp.dma_start(kvln[:, :], d["kv_ln"].broadcast_to([P, CR])).then_inc(s.wpe_loaded, 16)
                sp.dma_start(wv[:, :, :], d["w_v"]).then_inc(s.wv_loaded, 16)
                for q in range(4):
                    if q >= 2:
                        sp.wait_ge(s.vo_done, (q - 1) * QH // 2)
                    sp.dma_start(wo[:, q % 2, :, :],
                                 d["w_o"][q * QH:(q + 1) * QH, :, :].rearrange("h v n -> v h n")
                                 ).then_inc(wo_loaded[q % 2], 16)

            @block.gpsimd
            def _(pool):
                nc.gpsimd.memset(masks[:, :], 0.0).then_inc(s.mask_done, 1)
                pool.wait_ge(s.mask_done, 1)
                for b in range(GB):
                    rows = slice(b * S, (b + 1) * S)
                    nc.gpsimd.affine_select(out=masks[rows, :], in_=masks[rows, :],
                                            compare_op=ALU.is_ge, fill=MASKED, base=0,
                                            pattern=[[-1, S]], channel_multiplier=1
                                            ).then_inc(s.mask_done, 1)

            @block.tensor
            def _(pe):
                pe.wait_ge(s.wqk_loaded, 32)
                for m in range(H // HB * 2):
                    hb, c = divmod(m, 2)
                    lo, hi = chunks[c]
                    if m >= 2:
                        pe.wait_ge(s.qk_ready, m - 1)
                    for j in range(HB):
                        mm = nc.tensor.matmul(banks[m % 2][0:hi - lo, j * CR:(j + 1) * CR],
                                              wqn[:, hb * HB + j, lo:hi], wk[:, hb * HB + j, :],
                                              start=True, stop=True)
                    mm.then_inc(s.qk_done, 1)
                pe.wait_ge(s.wv_loaded, 16)
                for m in range(H // 2):
                    q = 2 * m // QH
                    pe.wait_ge(wo_loaded[q % 2], 16 * (q // 2 + 1))
                    if m >= 2:
                        pe.wait_ge(s.vo_ready, m - 1)
                    for j in range(2):
                        mm = nc.tensor.matmul(vbanks[m % 2][j * CR:(j + 1) * CR, :],
                                              wv[:, 2 * m + j, :], wo[:, q % 2, (2 * m + j) % QH, :],
                                              start=True, stop=True)
                    mm.then_inc(s.vo_done, 1)

            @block.scalar
            def _(act):
                for m in range(H // 2):
                    act.wait_ge(s.vo_done, m + 1)
                    nc.scalar.copy(wvo[:, m, :], vbanks[m % 2]).then_inc(s.vo_ready, 1)

            @block.vector
            def _(dve):
                dve.wait_ge(s.wpe_loaded, 80)
                for m in range(H // HB * 2):
                    hb, c = divmod(m, 2)
                    rows = chunks[c][1] - chunks[c][0]
                    dve.wait_ge(s.qk_done, m + 1)
                    nc.vector.tensor_scalar(
                        wq[0:rows, c, hb * HB:(hb + 1) * HB, 0:CR],
                        banks[m % 2][0:rows, :].rearrange("p (h n) -> p h n", n=CR),
                        qln[0:rows, c:c + 1], None, ALU.mult).then_inc(s.qk_ready, 1)
                    nc.vector.tensor_scalar(
                        wq[0:rows, c, hb * HB:(hb + 1) * HB, CR:],
                        wq[0:rows, c, hb * HB:(hb + 1) * HB, CR:],
                        qln[0:rows, c:c + 1], None, ALU.mult)


def phase_latent(nc, k, d, groups, base):
    NB = 8
    LAG = 2
    order = ("C0", "B0", "C3a", "B1", "C3b", "C1", "B2", "Q0", "Q1", "Q2", "C2", "Q3", "Q4", "Q5",
             "Q6", "Q7", "Q8", "Q9", "B3", "B5", "C4", "B4")
    late = ("B5",)
    with ExitStack() as outer:
        def keep(name, shape):
            return outer.enter_context(nc.sbuf_tensor(name, shape, F32))

        wq = keep("wq", [P, 2, H, CR + RO])
        wvo = keep("wvo", [P, H // 2, D])
        kvln = keep("kvln", [P, CR])
        masks = keep("masks", [P, S])
        prepare_latent(nc, k, d, wq, wvo, kvln, masks)

        ctx = outer
        sb = keep
        conv_tiles(nc, ctx, k, "a1")
        wa = sb("wa", [P, KC, QR + CR + RO])
        cos = sb("cos", [P, RO])
        sin = sb("sin", [P, RO])
        a = sb("a", [P, QR + CR + RO])
        junk = sb("junk", [P, QR])
        ms = sb("ms", [P, 2])
        rms = sb("rms", [P, 2])
        qn = sb("qn", [P, QR])
        kf = sb("kf", [P, CR + RO])
        t1 = sb("t1", [P, RO])
        t2 = sb("t2", [P, RO])
        qnT = sb("qnT", [P, 2, P])
        kfT = sb("kfT", [P, P])
        qs = sb("qs", [P, 3, 4, CR + RO])
        r1 = sb("r1", [P, 4, RO])
        r2 = sb("r2", [P, 4, RO])
        qT = sb("mqT", [P, H, P])
        sc = sb("scores", [P, H, S])
        pr = sb("probs", [P, H, S])
        prT = sb("probsT", [P, H, S])
        top = sb("mtop", [P, H])
        den = sb("mden", [P, H])
        oT = sb("oT", [P, H // 2, GB, S])
        s = Named()
        s.wa_loaded = ctx.enter_context(nc.semaphore("wa_loaded"))
        s.eps_set = ctx.enter_context(nc.semaphore("eps_set"))
        s.a_done = ctx.enter_context(nc.semaphore("a_done"))
        s.a_ready = ctx.enter_context(nc.semaphore("a_ready"))
        s.ms_ready = ctx.enter_context(nc.semaphore("ms_ready"))
        s.root_ready = ctx.enter_context(nc.semaphore("root_ready"))
        s.norm_steps = ctx.enter_context(nc.semaphore("norm_steps"))
        s.kq_turned = ctx.enter_context(nc.semaphore("kq_turned"))
        s.kqT_ready = ctx.enter_context(nc.semaphore("kqT_ready"))
        s.q_done = ctx.enter_context(nc.semaphore("q_done"))
        s.q_copied = ctx.enter_context(nc.semaphore("q_copied"))
        s.rope_steps = ctx.enter_context(nc.semaphore("rope_steps"))
        s.q_turned = ctx.enter_context(nc.semaphore("q_turned"))
        s.qT_ready = ctx.enter_context(nc.semaphore("qT_ready"))
        s.sT_done = ctx.enter_context(nc.semaphore("sT_done"))
        s.s_ready = ctx.enter_context(nc.semaphore("s_ready"))
        s.masked = ctx.enter_context(nc.semaphore("masked"))
        s.soft_steps = ctx.enter_context(nc.semaphore("soft_steps"))
        s.p_exp = ctx.enter_context(nc.semaphore("p_exp"))
        s.p_ready = ctx.enter_context(nc.semaphore("p_ready"))
        s.prT_ready = ctx.enter_context(nc.semaphore("prT_ready"))
        s.pv2_done = ctx.enter_context(nc.semaphore("pv2_done"))
        s.oT_ready = ctx.enter_context(nc.semaphore("oT_ready"))
        s.a1_done = ctx.enter_context(nc.semaphore("a1_done"))
        eps = sb("rmseps", [P, 1])
        NS = 9
        half = RO // 2

        def rotated(x):
            return x[..., half:], x[..., 0:half]

        with nc.Block() as block:
            @block.sync
            def _(sp):
                sp.dma_start(wa[:, :, :], d["w_a"].rearrange("(c p) n -> p c n", p=P)
                             ).then_inc(s.wa_loaded, 16)
                sp.dma_start(cos[:, :], d["rope_cos"]).then_inc(s.wa_loaded, 16)
                sp.dma_start(sin[:, :], d["rope_sin"]).then_inc(s.wa_loaded, 16)

                loads_and_stores(sp, k, groups, base, True)

            @block.gpsimd
            def _(pool):
                def step(st):
                    g = st.g
                    on, g, n, m, p = st.part(False)
                    if on:
                        pool.wait_ge(s.s_ready, g + 1)
                        nc.gpsimd.tensor_tensor(sc[:, :, :], sc[:, :, :],
                                                masks[:, :].unsqueeze(1).broadcast_to([P, H, S]),
                                                ALU.add).then_inc(s.masked, 1)
                        pool.wait_ge(s.soft_steps, 4 * g + 4)
                        nc.gpsimd.tensor_tensor(pr[:, :, :], pr[:, :, :],
                                                den[:, :].unsqueeze(2).broadcast_to([P, H, S]),
                                                ALU.mult).then_inc(s.p_ready, 1)
                steps(pool, groups, base, step)

            @block.scalar
            def _(act):
                act.wait_ge(k.edges_zero, 12 * (1 + k.cond))
                act.wait_ge(s.eps_set, 1)

                def step(st):
                    for slot in order:
                        conv_act(act, nc, k, slot, st)
                        on, g, n, m, p = st.part(slot in late)
                        if not on:
                            continue
                        if slot == "B1":
                            act.wait_ge(s.a_done, g + 1)
                            act.wait_ge(s.norm_steps, NS * g)
                            nc.scalar.copy(a[:, :], k.pb[:, 0, 0:QR + CR + RO]
                                           ).then_inc(s.a_ready, 1)
                            act.wait_ge(s.ms_ready, 2 * g + 2)
                            for j, width in enumerate((QR, CR)):
                                nc.scalar.activation(rms[:, j:j + 1], ms[:, j:j + 1], ACT.Sqrt,
                                                     bias=eps[:, :], scale=1.0 / width
                                                     ).then_inc(s.root_ready, 1)
                        if slot == "B2":
                            act.wait_ge(s.kq_turned, 3 * g + 3)
                            nc.scalar.copy(qnT[:, 0, :], k.pb[:, 4, 0:P]).then_inc(s.kqT_ready, 1)
                            nc.scalar.copy(qnT[0:QR - P, 1, :], k.pb[0:QR - P, 4, P:2 * P]
                                           ).then_inc(s.kqT_ready, 1)
                            nc.scalar.copy(kfT[:, :], k.pb[:, 4, 2 * P:3 * P]
                                           ).then_inc(s.kqT_ready, 1)
                        if slot[0] == "Q":
                            j = int(slot[1])
                            if j < NB:
                                act.wait_ge(s.q_done, NB * g + j + 1)
                                if j >= 3:
                                    act.wait_ge(s.q_turned, NB * g + j - 2)
                                nc.scalar.copy(qs[:, j % 3, :, :],
                                               k.pb[:, j % 2, :].rearrange("p (h n) -> p h n", h=4)
                                               ).then_inc(s.q_copied, 1)
                            if j >= LAG:
                                i = j - LAG
                                act.wait_ge(s.q_turned, NB * g + i + 1)
                                nc.scalar.copy(qT[:, 4 * i:4 * i + 4, :],
                                               k.pb[:, 2 + i % 2, :].rearrange(
                                                   "p (h n) -> p h n", h=4)).then_inc(s.qT_ready, 1)
                        if slot == "B3":
                            act.wait_ge(s.soft_steps, 4 * g + 2)
                            nc.scalar.activation(pr[:, :, :], pr[:, :, :], ACT.Exp,
                                                 scale=MLA_SCALE).then_inc(s.p_exp, 1)
                        if slot == "B4":
                            for b in range(0, GB, 2):
                                act.wait_ge(s.pv2_done, GB * g + b + 1)
                                nc.scalar.copy(oT[:, :, b, :],
                                               k.pb[:, b, :].rearrange("p (h s) -> p h s", s=S)
                                               ).then_inc(s.oT_ready, 1)
                steps(act, groups, base, step)

            @block.tensor
            def _(pe):
                pe.wait_ge(s.wa_loaded, 48)

                def step(st):
                    for slot in order:
                        conv_tensor(pe, nc, k, slot, st)
                        on, g, n, m, p = st.part(slot in late)
                        if not on:
                            continue
                        if slot == "B0":
                            if not is_first(n):
                                pe.wait_ge(k.out_ready, n - 1)
                            turn_y(pe, nc, k, st)
                        if slot == "B1":
                            pe.wait_ge(k.yT_ready, n + 1)
                            pe.wait_ge(s.oT_ready, GB * g)
                            dense(nc, k.pb[:, 0, 0:QR + CR + RO], k.yT, wa, QR + CR + RO
                                  ).then_inc(s.a_done, 1)
                        if slot == "B2":
                            pe.wait_ge(s.norm_steps, NS * g + NS)
                            nc.tensor.transpose(k.pb[:, 4, 0:P], qn[:, 0:P], k.ident[:, :]
                                                ).then_inc(s.kq_turned, 1)
                            nc.tensor.transpose(k.pb[0:QR - P, 4, P:2 * P], qn[:, P:QR],
                                                k.ident[:, :]).then_inc(s.kq_turned, 1)
                            nc.tensor.transpose(k.pb[:, 4, 2 * P:3 * P], kf[:, :], k.ident[:, :]
                                                ).then_inc(s.kq_turned, 1)
                        if slot[0] == "Q":
                            j = int(slot[1])
                            if j == 0:
                                pe.wait_ge(s.kqT_ready, 3 * g + 3)
                            if 2 <= j < NB:
                                pe.wait_ge(s.q_copied, NB * g + j - 1)
                            if j < NB:
                                for c, rows in enumerate((P, QR - P)):
                                    mm = nc.tensor.matmul(
                                        k.pb[:, j % 2, :], qnT[0:rows, c, :],
                                        wq[0:rows, c, 4 * j:4 * j + 4, :].rearrange(
                                            "p h n -> p (h n)"),
                                        start=(c == 0), stop=(c == 1))
                                mm.then_inc(s.q_done, 1)
                            if j >= LAG:
                                i = j - LAG
                                pe.wait_ge(s.rope_steps, 5 * (NB * g + i + 1))
                                if i >= 2:
                                    pe.wait_ge(s.qT_ready, NB * g + i - 1)
                                for h in range(4):
                                    mm = nc.tensor.transpose(
                                        k.pb[:, 2 + i % 2, h * P:(h + 1) * P], qs[:, i % 3, h, :],
                                        k.ident[:, :])
                                mm.then_inc(s.q_turned, 1)
                        if slot == "B3":
                            pe.wait_ge(s.qT_ready, NB * g + NB)
                            for m in range(2):
                                for b in range(GB):
                                    cols = slice(b * S, (b + 1) * S)
                                    mm = nc.tensor.matmul(
                                        k.pb[cols, m, :], kfT[:, cols],
                                        qT[:, m * H // 2:(m + 1) * H // 2, cols],
                                        start=True, stop=True)
                                mm.then_inc(s.sT_done, 1)
                        if slot == "B4":
                            pe.wait_ge(s.prT_ready, g + 1)
                            for b in range(GB):
                                rows = slice(b * S, (b + 1) * S)
                                for hh in range(2):
                                    mm = nc.tensor.matmul(
                                        k.pb[hh * CR:(hh + 1) * CR, b, :], kf[rows, 0:CR],
                                        prT[rows, hh:H:2, :], start=True, stop=True)
                                mm.then_inc(s.pv2_done, 1)
                        if slot == "B5":
                            pe.wait_ge(s.oT_ready, GB * g + GB)
                            for m in range(H // 2):
                                mm = nc.tensor.matmul(
                                    k.pb[:, 4, :], oT[:, m, :, :].rearrange("p b s -> p (b s)"),
                                    wvo[:, m, :], start=(m == 0), stop=(m == H // 2 - 1))
                            mm.then_inc(s.a1_done, 1)
                steps(pe, groups, base, step)

            @block.vector
            def _(dve):
                zero_edges(nc, k)
                nc.vector.memset(eps[:, :], RMS_EPS).then_inc(s.eps_set, 1)
                dve.wait_ge(s.wa_loaded, 48)
                dve.wait_ge(k.edges_zero, 12 * (1 + k.cond))

                def step(st):
                    v = nc.vector
                    for slot in order:
                        conv_vector(dve, nc, k, slot, st)
                        on, g, n, m, p = st.part(slot in late)
                        if not on:
                            continue
                        if slot == "B0":
                            copy_yT(dve, nc, k, n)
                        if slot == "B1":
                            dve.wait_ge(s.a_ready, g + 1)
                            dve.wait_ge(s.norm_steps, NS * g)
                            v.tensor_tensor_reduce(out=junk[:, :], in0=a[:, 0:QR], in1=a[:, 0:QR],
                                                   scale=1.0, scalar=0.0, op0=ALU.mult,
                                                   op1=ALU.add, accum_out=ms[:, 0:1]
                                                   ).then_inc(s.ms_ready, 1)
                            dve.wait_ge(s.ms_ready, 2 * g + 1)
                            v.tensor_tensor_reduce(out=junk[:, 0:CR], in0=a[:, QR:QR + CR],
                                                   in1=a[:, QR:QR + CR], scale=1.0, scalar=0.0,
                                                   op0=ALU.mult, op1=ALU.add,
                                                   accum_out=ms[:, 1:2]).then_inc(s.ms_ready, 1)
                            pe_ = a[:, QR + CR:]
                            v.tensor_tensor(t1[:, :], pe_, cos[:, :], ALU.mult
                                            ).then_inc(s.norm_steps, 1)
                            hi, lo = rotated(pe_)
                            v.tensor_tensor(t2[:, 0:half], hi, sin[:, 0:half], ALU.mult
                                            ).then_inc(s.norm_steps, 1)
                            v.tensor_tensor(t2[:, half:], lo, sin[:, half:], ALU.mult
                                            ).then_inc(s.norm_steps, 1)
                            dve.wait_ge(s.norm_steps, NS * g + 3)
                            v.tensor_tensor(kf[:, CR:], t1[:, :], t2[:, :], ALU.add
                                            ).then_inc(s.norm_steps, 1)
                            dve.wait_ge(s.root_ready, 2 * g + 2)
                            v.reciprocal(rms[:, :], rms[:, :]).then_inc(s.norm_steps, 1)
                            dve.wait_ge(s.norm_steps, NS * g + 5)
                            v.tensor_scalar(qn[:, :], a[:, 0:QR], rms[:, 0:1], None, ALU.mult
                                            ).then_inc(s.norm_steps, 1)
                            v.tensor_scalar(kf[:, 0:CR], a[:, QR:QR + CR], rms[:, 1:2], None,
                                            ALU.mult).then_inc(s.norm_steps, 1)
                            dve.wait_ge(s.norm_steps, NS * g + 7)
                            v.tensor_tensor(kf[:, 0:CR], kf[:, 0:CR], kvln[:, :], ALU.mult
                                            ).then_inc(s.norm_steps, 2)
                        if slot[0] == "Q" and int(slot[1]) < NB:
                            j = int(slot[1])
                            dve.wait_ge(s.q_copied, NB * g + j + 1)
                            at = 5 * (NB * g + j)
                            dve.wait_ge(s.rope_steps, at)
                            pe_ = qs[:, j % 3, :, CR:]
                            c4 = cos[:, :].unsqueeze(1).broadcast_to([P, 4, RO])
                            v.tensor_tensor(r1[:, :, :], pe_, c4, ALU.mult
                                            ).then_inc(s.rope_steps, 1)
                            for lo in (0, half):
                                part = slice(lo, lo + half)
                                other = slice(half - lo, RO - lo)
                                v.tensor_tensor(
                                    r2[:, :, part], pe_[:, :, other],
                                    sin[:, part].unsqueeze(1).broadcast_to([P, 4, half]), ALU.mult
                                    ).then_inc(s.rope_steps, 1)
                            dve.wait_ge(s.rope_steps, at + 3)
                            v.tensor_tensor(qs[:, j % 3, :, CR:], r1[:, :, :], r2[:, :, :], ALU.add
                                            ).then_inc(s.rope_steps, 2)
                        if slot == "B3":
                            for m in range(2):
                                dve.wait_ge(s.sT_done, 2 * g + m + 1)
                                mm = v.transpose(sc[:, m * H // 2:(m + 1) * H // 2, :],
                                                 k.pb[:, m, :].rearrange("p (h s) -> p h s", s=S))
                            mm.then_inc(s.s_ready, 1)
                            dve.wait_ge(s.masked, g + 1)
                            v.tensor_reduce(top[:, :], sc[:, :, :], AX.X, ALU.max
                                            ).then_inc(s.soft_steps, 1)
                            dve.wait_ge(s.soft_steps, 4 * g + 1)
                            v.tensor_tensor(pr[:, :, :], sc[:, :, :],
                                            top[:, :].unsqueeze(2).broadcast_to([P, H, S]),
                                            ALU.subtract).then_inc(s.soft_steps, 1)
                            dve.wait_ge(s.p_exp, g + 1)
                            v.reduce_sum(den[:, :], pr[:, :, :], AX.X).then_inc(s.soft_steps, 1)
                            dve.wait_ge(s.soft_steps, 4 * g + 3)
                            v.reciprocal(den[:, :], den[:, :]).then_inc(s.soft_steps, 1)
                            dve.wait_ge(s.p_ready, g + 1)
                            v.transpose(prT[:, :, :], pr[:, :, :]).then_inc(s.prT_ready, 1)
                        if slot == "B4":
                            for b in range(1, GB, 2):
                                dve.wait_ge(s.pv2_done, GB * g + b + 1)
                                v.tensor_copy(oT[:, :, b, :],
                                              k.pb[:, b, :].rearrange("p (h s) -> p h s", s=S)
                                              ).then_inc(s.oT_ready, 1)
                        if slot == "B5":
                            dve.wait_ge(s.a1_done, g + 1)
                            dve.wait_ge(k.res_loaded[p], 16 * m + 16)
                            dve.wait_ge(k.stored[p], 16 * m)
                            v.tensor_tensor(k.xout[:, p, :], k.pb[:, 4, :], k.xres[:, p, :],
                                            ALU.add).then_inc(k.out_ready, 1)
                steps(dve, groups, base, step)


def phase_signs(nc, k, d, groups, base):
    order = ("C0", "C3a", "B0", "C3b", "B1", "C1", "B2", "C2", "B3", "C4", "B4", "B5")
    late = ()
    with ExitStack() as ctx:
        def sb(name, shape, dt=F32):
            return ctx.enter_context(nc.sbuf_tensor(name, shape, dt))

        conv_tiles(nc, ctx, k, "f1")
        raw = sb("raw", [P, 3, KC, D // 4], mybir.dt.int32)
        w = sb("wsign", [P, 3, KC, D])
        fac = sb("fac", [P, KC])
        two = sb("two", [P, KC])
        scales = sb("scales", [P, 3])
        hid = sb("hid", [P, D])
        hT = sb("hT", [P, KC, P])
        s = Named()
        s.signs_loaded = ctx.enter_context(nc.semaphore("signs_loaded"))
        s.fac_ready = ctx.enter_context(nc.semaphore("fac_ready"))
        s.w_ready = ctx.enter_context(nc.semaphore("w_ready"))
        s.dense_done = ctx.enter_context(nc.semaphore("dense_done"))
        s.hid_ready = ctx.enter_context(nc.semaphore("hid_ready"))
        s.hid_turned = ctx.enter_context(nc.semaphore("hid_turned"))
        s.hT_ready = ctx.enter_context(nc.semaphore("hT_ready"))
        NW = 2 + 3 * KC + 1

        with nc.Block() as block:
            @block.sync
            def _(sp):
                sp.dma_start(raw[:, :, :, :], d["k_signs"].rearrange("j (c p) n -> p j c n", p=P)
                             ).then_inc(s.signs_loaded, 16)
                sp.dma_start(scales[:, :], d["s_scales"].broadcast_to([P, 3])
                             ).then_inc(s.signs_loaded, 16)

                loads_and_stores(sp, k, groups, base, False)

            @block.gpsimd
            def _(pool):
                nc.gpsimd.memset(fac[:, :], 1.0).then_inc(s.fac_ready, 1)
                pool.wait_ge(s.fac_ready, 1)
                nc.gpsimd.affine_select(out=fac[:, :], in_=fac[:, :], compare_op=ALU.is_ge,
                                        fill=INH, base=EXC - 1, pattern=[[-P, KC]],
                                        channel_multiplier=-1).then_inc(s.fac_ready, 1)

            @block.scalar
            def _(act):
                act.wait_ge(k.edges_zero, 12 * (1 + k.cond))
                act.wait_ge(s.w_ready, NW)

                def step(st):
                    for slot in order:
                        conv_act(act, nc, k, slot, st)
                        on, g, n, m, p = st.part(slot in late)
                        if not on:
                            continue
                        if slot in ("B1", "B3"):
                            layer = 0 if slot == "B1" else 1
                            act.wait_ge(s.dense_done, 3 * g + layer + 1)
                            act.wait_ge(s.hid_turned, 2 * g + layer)
                            nc.scalar.activation(hid[:, :], k.pb[:, layer, :], ACT.Relu,
                                                 scale=scales[:, layer:layer + 1]
                                                 ).then_inc(s.hid_ready, 1)
                steps(act, groups, base, step)

            @block.tensor
            def _(pe):
                pe.wait_ge(s.w_ready, NW)

                def step(st):
                    for slot in order:
                        conv_tensor(pe, nc, k, slot, st)
                        on, g, n, m, p = st.part(slot in late)
                        if not on:
                            continue
                        if slot == "B0":
                            turn_y(pe, nc, k, st)
                        if slot == "B1":
                            pe.wait_ge(k.yT_ready, n + 1)
                            dense(nc, k.pb[:, 0, :], k.yT, w[:, 0, :, :]).then_inc(s.dense_done, 1)
                        if slot in ("B2", "B4"):
                            layer = 0 if slot == "B2" else 1
                            pe.wait_ge(s.hid_ready, 2 * g + layer + 1)
                            for c in range(KC):
                                mm = nc.tensor.transpose(k.pb[:, 3, c * P:(c + 1) * P],
                                                         hid[:, c * P:(c + 1) * P], k.ident[:, :])
                            mm.then_inc(s.hid_turned, 1)
                        if slot in ("B3", "B5"):
                            layer = 1 if slot == "B3" else 2
                            pe.wait_ge(s.hT_ready, 2 * g + layer)
                            pe.wait_ge(k.out_ready, n)
                            dense(nc, k.pb[:, layer, :], hT, w[:, layer, :, :]
                                  ).then_inc(s.dense_done, 1)
                steps(pe, groups, base, step)

            @block.vector
            def _(dve):
                zero_edges(nc, k)
                dve.wait_ge(s.signs_loaded, 32)
                dve.wait_ge(s.fac_ready, 2)
                nc.vector.tensor_scalar(two[:, :], fac[:, :], 2.0, None, ALU.mult
                                        ).then_inc(s.w_ready, 1)
                nc.vector.tensor_scalar(scales[:, 0:2], scales[:, 0:2], 2.0, None, ALU.mult
                                        ).then_inc(s.w_ready, 1)
                dve.wait_ge(s.w_ready, 2)
                for j in range(3):
                    for c in range(KC):
                        signs = raw[:, j, c, :].bitcast(U8)
                        if j == 0:
                            nc.vector.tensor_scalar(w[:, j, c, :], signs, 2.0, -1.0, ALU.mult,
                                                    ALU.add).then_inc(s.w_ready, 1)
                        else:
                            nc.vector.tensor_scalar(w[:, j, c, :], signs, two[:, c:c + 1],
                                                    fac[:, c:c + 1], ALU.mult, ALU.subtract
                                                    ).then_inc(s.w_ready, 1)
                dve.wait_ge(k.edges_zero, 12 * (1 + k.cond))
                dve.wait_ge(s.w_ready, NW - 1)
                nc.vector.memset(two[:, :], 0.0).then_inc(s.w_ready, 1)

                def step(st):
                    for slot in order:
                        conv_vector(dve, nc, k, slot, st)
                        on, g, n, m, p = st.part(slot in late)
                        if not on:
                            continue
                        if slot == "B0":
                            copy_yT(dve, nc, k, n)
                        if slot in ("B2", "B4"):
                            layer = 0 if slot == "B2" else 1
                            dve.wait_ge(s.hid_turned, 2 * g + layer + 1)
                            dve.wait_ge(s.dense_done, 3 * g + layer + 1)
                            nc.vector.tensor_copy(hT[:, :, :].rearrange("p c t -> p (c t)"),
                                                  k.pb[:, 3, :]).then_inc(s.hT_ready, 1)
                        if slot == "B5":
                            dve.wait_ge(s.dense_done, 3 * g + 3)
                            dve.wait_ge(k.res_loaded[p], 16 * m + 16)
                            dve.wait_ge(k.stored[p], 16 * m)
                            nc.vector.scalar_tensor_tensor(
                                out=k.xout[:, p, :], in0=k.pb[:, 2, :], scalar=scales[:, 2:3],
                                in1=k.xres[:, p, :], op0=ALU.mult, op1=ALU.add
                                ).then_inc(k.out_ready, 1)
                steps(dve, groups, base, step)


PHASES = [phase_attention, phase_experts, phase_latent, phase_signs]


def program(nc, d, out, groups):
    with ExitStack() as ctx:
        k = Named()
        k.prescaled = ctx.enter_context(nc.semaphore("prescaled"))
        k.coef_ready = ctx.enter_context(nc.semaphore("coef_ready"))
        k.conv1_done = ctx.enter_context(nc.semaphore("conv1_done"))
        k.x2_ready = ctx.enter_context(nc.semaphore("x2_ready"))
        k.conv2_done = ctx.enter_context(nc.semaphore("conv2_done"))
        k.y2_ready = ctx.enter_context(nc.semaphore("y2_ready"))
        k.blur1_done = ctx.enter_context(nc.semaphore("blur1_done"))
        k.conv3_done = ctx.enter_context(nc.semaphore("conv3_done"))
        k.y3_ready = ctx.enter_context(nc.semaphore("y3_ready"))
        k.blur2_done = ctx.enter_context(nc.semaphore("blur2_done"))
        k.conv4_done = ctx.enter_context(nc.semaphore("conv4_done"))
        k.y_ready = ctx.enter_context(nc.semaphore("y_ready"))
        k.y_turned = ctx.enter_context(nc.semaphore("y_turned"))
        k.yT_ready = ctx.enter_context(nc.semaphore("yT_ready"))
        k.out_ready = ctx.enter_context(nc.semaphore("out_ready"))
        k.edges_zero = ctx.enter_context(nc.semaphore("edges_zero"))
        k.x_loaded, k.res_loaded, k.stored = (
            [ctx.enter_context(nc.semaphore(f"{name}_{par}")) for par in range(2)]
            for name in ("x_loaded", "res_loaded", "stored"))
        k.convw = ctx.enter_context(nc.sbuf_tensor("convw", [P, CONDS, LAYERS * TAPS, P], F32))
        k.table = ctx.enter_context(nc.sbuf_tensor("table", [P, CONDS, groups, NCOEF], F32))
        k.ident = ctx.enter_context(nc.sbuf_tensor("ident", [P, P], F32))
        prepare(nc, k, d, groups)
        k.pc = ctx.enter_context(nc.psum_tensor("pc", [P, 3, 512], F32))
        k.pb = ctx.enter_context(nc.psum_tensor("pb", [P, 5, 512], F32))
        k.src = d["x"]
        for n, phase in enumerate(PHASES):
            k.cond = n
            k.dst = out if n == len(PHASES) - 1 else \
                nc.dram_tensor(f"x_after_{n}", [groups * P, D], F32, kind="Internal").ap()
            phase(nc, k, d, groups, n * groups)
            k.src = k.dst


def kernel(**inputs):
    import concourse.bacc as bacc
    from concourse.bass_utils import run_bass_kernel_spmd

    a = {n: np.asarray(v) for n, v in inputs.items()}
    batches = a["x"].shape[0]
    conds = ("L0_cond", "L0_cond2", "L1_cond", "L1_cond2")
    cw = np.stack([a[c + "_weights"] for c in conds])
    lhs = np.stack([cw[:, l] if l == 1 else cw[:, l].transpose(0, 2, 1, 3)
                    for l in range(LAYERS)], 1)
    qb = a["L1_attn_Wq_b"].reshape(QR, H, NOPE + RO)
    kvb = a["L1_attn_Wkv_b"].reshape(CR, H, NOPE + VD)
    split = np.concatenate([np.arange(0, RO, 2), np.arange(1, RO, 2)])
    inv = np.float32(1.0) / np.float32(10000.0) ** (np.arange(0, RO, 2, dtype=np.float32) / RO)
    angle = np.outer(np.arange(S, dtype=np.float32), inv).astype(np.float32)
    cos, sin = np.cos(angle), np.sin(angle)
    host = {
        "x": a["x"].reshape(batches * S, D),
        "style_t": a["cond_512"].T,
        "conv_w": lhs.transpose(2, 0, 1, 4, 3).reshape(S, CONDS, LAYERS * TAPS, S),
        "demod_w": cw.transpose(3, 0, 1, 4, 2).reshape(S, CONDS * LAYERS, TAPS, S),
        "mod_wt": np.stack([a[c + "_mod_w"] for c in conds]).reshape(-1, S, STYLE).transpose(2, 0, 1),
        "mod_b": np.stack([a[c + "_mod_b"] for c in conds]).reshape(-1, S).T,
        "conv_b": np.stack([a[c + "_biases"] for c in conds]).reshape(-1, S).T,
        "w_qkv": np.stack([a["L0_attn_w" + j].T for j in "qkv"]),
        "b_qkv": np.stack([a["L0_attn_b" + j] for j in "qkv"]),
        "w_base": a["L0_ffn_W_base"].T,
        "b_base": a["L0_ffn_b_base"].reshape(1, D),
        "w_ag": np.concatenate([a["L0_ffn_A_w"].reshape(EX * RK, D), a["L0_ffn_W_gate"],
                                a["L0_ffn_W_thr"].reshape(1, D)]).T,
        "b_thr": a["L0_ffn_b_thr"].reshape(1, 1),
        "w_b": a["L0_ffn_B_w"].transpose(0, 2, 1).reshape(EX * RK, D),
        "w_a": np.concatenate([a["L1_attn_Wq_a"], a["L1_attn_Wkv_a"][:, :CR],
                               a["L1_attn_Wkv_a"][:, CR:][:, split]], 1),
        "q_ln": a["L1_attn_q_a_ln_w"].reshape(QR, 1),
        "kv_ln": a["L1_attn_kv_a_ln_w"].reshape(1, CR),
        "w_q_nope": qb[:, :, :NOPE].transpose(2, 1, 0),
        "w_q_pe": qb[:, :, NOPE:][:, :, split],
        "w_k": kvb[:, :, :NOPE].transpose(2, 1, 0),
        "w_v": kvb[:, :, NOPE:].transpose(2, 1, 0),
        "w_o": a["L1_attn_Wo"].reshape(H, VD, D),
        "rope_cos": np.tile(np.concatenate([cos, cos], 1), (GB, 1)),
        "rope_sin": np.tile(np.concatenate([-sin, sin], 1), (GB, 1)),
        "k_signs": np.stack([np.ascontiguousarray(a["L1_ffn_k" + j]).view(np.int32) for j in "012"]),
        "s_scales": np.stack([a["L1_ffn_s" + j] for j in "012"]).reshape(1, 3),
    }
    nc = bacc.Bacc("TRN2", target_bir_lowering=False, num_devices=1)
    arrays, dram = {}, {}
    for name, v in host.items():
        v = np.ascontiguousarray(v)
        arrays[name] = v
        dram[name] = nc.dram_tensor(name, v.shape, mybir.dt.from_np(v.dtype),
                                    kind="ExternalInput").ap()
    out = nc.dram_tensor("out", [batches * S, D], F32, kind="ExternalOutput").ap()
    program(nc, dram, out, batches // GB)
    r = run_bass_kernel_spmd(nc, [arrays], core_ids=[0])
    return r.results[0]["out"].reshape(batches, S, D)
```

```python
from contextlib import ExitStack

import numpy as np
import concourse.bass as bass
from concourse import mybir

F32 = mybir.dt.float32
F32R = mybir.dt.float32r
U8 = mybir.dt.uint8
ALU = mybir.AluOpType
ACT = mybir.ActivationFunctionType
AX = mybir.AxisListType

P = 128
D = 512
S = 32
GB = P // S
KC = D // P
STYLE = 64
LAYERS, TAPS = 4, 3
CONDS = 4
CONV_SCALE = 1.0 / float(np.sqrt(S * TAPS ** 2))
CONV_EPS = 1e-8
UP = 2 * D
NCOEF = 9
NCOEF_A = 5

SPLIT = ((0, 0), (1, 0), (0, 1))

H = 32
HD = 16
QR, CR, RO = 192, 64, 64
NOPE, VD = 128, 128
RMS_EPS = 1e-6
MLA_SCALE = float(NOPE + RO) ** -0.5
MASKED = -1e30

EX, RK = 8, 16
AG = EX * RK + EX + 1
MAX_THRESHOLD = 0.125
LORA_SCALE = 2.0
EXC = round(D * 0.8)
INH = -4.0


class Named:
    pass


def is_first(count):
    return isinstance(count, int) and count == 0


class Step:

    def __init__(self, t, half, par, groups, before):
        fixed = isinstance(t, int)
        self.conv_a = not fixed or t < groups
        self.conv_b = not fixed or 1 <= t <= groups
        self.blk = not fixed or 2 <= t <= groups + 1
        self.late = not fixed or 3 <= t
        self.t, self.half, self.par = t, half, par
        self.ga, self.gb, self.g, self.gl = t, t - 1, t - 2, t - 3
        self.na, self.nb, self.n, self.nl = (before + x for x in (t, t - 1, t - 2, t - 3))
        self.ma, self.m, self.ml = (before // 2 + x for x in (half, half - 1, half - 2 + par))
        self.pa, self.pb, self.p, self.pl = par, 1 - par, par, 1 - par

    def part(self, late):
        if late:
            return self.late, self.gl, self.nl, self.ml, self.pl
        return self.blk, self.g, self.n, self.m, self.p


def steps(eng, groups, base, body):
    first = 2 if base else 3
    assert groups % 2 == 0 and groups // 2 > first
    for t in range(2 * first):
        body(Step(t, t // 2, t % 2, groups, base))
    with eng.Fori(first, groups // 2) as i:
        body(Step(2 * i, i, 0, groups, base))
        body(Step(2 * i + 1, i, 1, groups, base))
    for t in range(groups, groups + 3):
        body(Step(t, t // 2, t % 2, groups, base))



def conv_load(sp, k, st):
    if not is_first(st.na):
        sp.wait_ge(k.prescaled, st.na - 1)
    sp.dma_start(k.xin[:, st.pa, :], k.src[bass.ds(st.ga * P, P), :]
                 ).then_inc(k.x_loaded[st.pa], 16)


def conv_act(act, nc, k, slot, st):
    if slot == "X3H" and st.conv_a:
        act.wait_ge(k.blur1_done, 3 * st.na + 3)
        act.wait_ge(k.conv3_done, 2 * st.na)
        nc.scalar.copy(k.x3[:, 0, 1:1 + UP], k.blur_a[:, 0:UP]).then_inc(k.x3_high, 1)
    n, coef = st.na, k.coef[:, st.pa, :]
    if slot == "C0" and st.conv_a:
        act.wait_ge(k.x_loaded[st.pa], 16 * st.ma + 16)
        act.wait_ge(k.coef_ready, n + 1)
        act.wait_ge(k.conv1_done, n)
        for x1, ready in ((k.x1[:, 0, 1:1 + D], k.x1_high), (k.x12_full[:, :], k.prescaled)):
            nc.scalar.activation(x1, k.xin[:, st.pa, :], ACT.Copy, scale=coef[:, 0:1]
                                 ).then_inc(ready, 1)
    if slot == "C1" and st.conv_a:
        act.wait_ge(k.conv1_done, n + 1)
        act.wait_ge(k.conv2_done, 3 * n)
        for x2, ready in ((k.x2[:, 0, 1:1 + D], k.x2_high), (k.x12_full[:, :], k.x2_ready)):
            nc.scalar.activation(x2, k.pc[:, 0, :], ACT.Identity, bias=coef[:, 2:3],
                                 scale=coef[:, 1:2]).then_inc(ready, 1)
    if slot == "C2e" and st.conv_a:
        act.wait_ge(k.blur1_done, 3 * n)
        for m, (src, lo, cnt) in enumerate(((1, 1, D), (2, 2, D), (0, UP + 1, 1))):
            act.wait_ge(k.conv2_done, 3 * n + m + 1)
            nc.scalar.activation(k.y2[:, lo:lo + 2 * cnt - 1:2], k.pc[:, src, 0:cnt], ACT.Identity,
                                 bias=coef[:, 4:5], scale=coef[:, 3:4]).then_inc(k.y2_ready, 1)
    n, coef = st.nb, k.coef[:, st.pb, :]
    if slot in ("C3a", "C3b") and st.conv_b:
        m = 0 if slot == "C3a" else 1
        act.wait_ge(k.blur2_done, 3 * n)
        act.wait_ge(k.coef_b_ready, n + 1)
        act.wait_ge(k.conv3_done, 2 * n + m + 1)
        nc.scalar.activation(k.y3[:, 2 + m * D:2 + (m + 1) * D], k.pc[:, 1 + m, :],
                             ACT.Identity, bias=coef[:, 6:7],
                             scale=coef[:, 5:6]).then_inc(k.y3_ready, 1)
    if slot == "X4H" and st.conv_b:
        act.wait_ge(k.blur2_done, 3 * n + 3)
        act.wait_ge(k.conv4_done, n)
        nc.scalar.copy(k.x4[:, 0, 0:UP + 1], k.x4_full[:, 0:UP + 1]).then_inc(k.x4_high, 1)
    if slot == "C4" and st.conv_b:
        act.wait_ge(k.conv4_done, n + 1)
        if not is_first(n):
            act.wait_ge(k.y_turned, n - 1)
        nc.scalar.activation(k.y[:, st.pb, :], k.pc[:, 0, :], ACT.Identity,
                             bias=coef[:, 8:9], scale=coef[:, 7:8]).then_inc(k.y_ready, 1)


def conv_vector(dve, nc, k, slot, st):
    n = st.na
    if slot == "X3L" and st.conv_a:
        dve.wait_ge(k.x3_high, st.na + 1)
        nc.vector.tensor_tensor(k.x3[:, 1, 1:1 + UP], k.blur_a[:, 0:UP],
                                k.x3[:, 0, 1:1 + UP].bitcast(F32), ALU.subtract
                                ).then_inc(k.x3_low, 1)
    if slot == "CB" and st.conv_a:
        dve.wait_ge(k.y2_ready, 3 * n + 3)
        nc.vector.tensor_tensor(k.blur_a[:, 0:UP + 2], k.y2[:, 0:UP + 2], k.y2[:, 1:UP + 3],
                                ALU.add).then_inc(k.blur1_done, 1)
        dve.wait_ge(k.blur1_done, 3 * n + 1)
        nc.vector.tensor_tensor(k.blur_b[:, 0:UP + 1], k.blur_a[:, 0:UP + 1],
                                k.blur_a[:, 1:UP + 2], ALU.add).then_inc(k.blur1_done, 1)
        dve.wait_ge(k.blur1_done, 3 * n + 2)
        nc.vector.tensor_tensor(k.blur_a[:, 0:UP], k.blur_b[:, 0:UP], k.blur_b[:, 1:UP + 1],
                                ALU.add).then_inc(k.blur1_done, 1)
    n = st.nb
    if slot == "C3c" and st.conv_b:
        dve.wait_ge(k.y3_ready, 2 * n + 2)
        dve.wait_ge(k.x3_low, n + 1)
        nc.vector.tensor_tensor(k.blur_a[:, 0:UP + 3], k.y3[:, 0:UP + 3], k.y3[:, 1:UP + 4],
                                ALU.add).then_inc(k.blur2_done, 1)
        dve.wait_ge(k.blur2_done, 3 * n + 1)
        nc.vector.tensor_tensor(k.blur_b[:, 0:UP + 2], k.blur_a[:, 0:UP + 2],
                                k.blur_a[:, 1:UP + 3], ALU.add).then_inc(k.blur2_done, 1)
        dve.wait_ge(k.blur2_done, 3 * n + 2)
        dve.wait_ge(k.x4_low, n)
        nc.vector.tensor_tensor(k.x4_full[:, 0:UP + 1], k.blur_b[:, 0:UP + 1],
                                k.blur_b[:, 1:UP + 2], ALU.add).then_inc(k.blur2_done, 1)


def conv_pool(pool, nc, k, slot, st):
    n = st.na
    def coefficients(first, last, group, par, ready):
        row = k.table[:, k.cond, bass.ds(group, 1), first:last].rearrange("p a c -> p (a c)")
        nc.gpsimd.tensor_tensor(k.coef[:, par, first:last], row, k.ones[:, first:last], ALU.mult
                                ).then_inc(ready, 1)

    if slot == "C0" and st.conv_a:
        if not is_first(n):
            pool.wait_ge(k.y2_ready, 3 * n - 3)
        coefficients(0, NCOEF_A, st.ga, st.pa, k.coef_ready)
        pool.wait_ge(k.prescaled, n + 1)
        nc.gpsimd.tensor_tensor(k.x1[:, 1, 1:1 + D], k.x12_full[:, :],
                                k.x1[:, 0, 1:1 + D].bitcast(F32), ALU.subtract
                                ).then_inc(k.x1_low, 1)
    if slot == "C1" and st.conv_a:
        pool.wait_ge(k.x2_ready, n + 1)
        nc.gpsimd.tensor_tensor(k.x2[:, 1, 1:1 + D], k.x12_full[:, :],
                                k.x2[:, 0, 1:1 + D].bitcast(F32), ALU.subtract
                                ).then_inc(k.x2_low, 1)
    n = st.nb
    if slot == "C0" and st.conv_b:
        if not is_first(n):
            pool.wait_ge(k.y_ready, n - 1)
        coefficients(NCOEF_A, NCOEF, st.gb, st.pb, k.coef_b_ready)
    if slot == "X4L" and st.conv_b:
        pool.wait_ge(k.x4_high, n + 1)
        nc.gpsimd.tensor_tensor(k.x4[:, 1, 0:UP + 1], k.x4_full[:, 0:UP + 1],
                                k.x4[:, 0, 0:UP + 1].bitcast(F32), ALU.subtract
                                ).then_inc(k.x4_low, 1)


def conv_tensor(pe, nc, k, slot, st):
    def products(out, layer, pieces, low, count):
        for m, (wpart, xpart) in enumerate(SPLIT):
            if xpart == 1:
                pe.wait_ge(low, count)
            for i, (tap, x) in enumerate(pieces):
                mm = nc.tensor.matmul(out, k.convw[:, wpart, layer * TAPS + tap, :], x(xpart),
                                      start=(m + i == 0),
                                      stop=(m == len(SPLIT) - 1 and i == len(pieces) - 1))
        return mm

    def shifted(x, at, cnt, stride=1):
        return lambda part: x[:, part, at:at + (cnt - 1) * stride + 1:stride]

    n = st.na
    if slot == "C1" and st.conv_a:
        pe.wait_ge(k.x1_high, n + 1)
        if not is_first(n):
            pe.wait_ge(k.y_ready, n - 1)
        products(k.pc[:, 0, :], 0, [(tap, shifted(k.x1, tap, D)) for tap in range(TAPS)],
                 k.x1_low, n + 1).then_inc(k.conv1_done, 1)
    if slot == "C2" and st.conv_a:
        pe.wait_ge(k.x2_high, n + 1)
        if not is_first(n):
            pe.wait_ge(k.y3_ready, 2 * n - 1)
        products(k.pc[:, 1, :], 1, [(0, shifted(k.x2, 1, D)), (2, shifted(k.x2, 0, D))],
                 k.x2_low, n + 1).then_inc(k.conv2_done, 1)
        pe.wait_ge(k.y3_ready, 2 * n)
        products(k.pc[:, 2, :], 1, [(1, shifted(k.x2, 1, D))],
                 k.x2_low, n + 1).then_inc(k.conv2_done, 1)
        products(k.pc[:, 0, 0:2], 1, [(2, shifted(k.x2, D, 2))],
                 k.x2_low, n + 1).then_inc(k.conv2_done, 1)
    n = st.nb
    if slot in ("C3a", "C3b") and st.conv_b:
        m = 0 if slot == "C3a" else 1
        pe.wait_ge(k.x3_high, n + 1)
        products(k.pc[:, 1 + m, :], 2,
                 [(tap, shifted(k.x3, m * D + tap, D)) for tap in range(TAPS)],
                 k.x3_low, n + 1).then_inc(k.conv3_done, 1)
    if slot == "C4" and st.conv_b:
        if st.conv_a:
            pe.wait_ge(k.y2_ready, 3 * n + 6)
        pe.wait_ge(k.x4_high, n + 1)
        products(k.pc[:, 0, :], 3, [(tap, shifted(k.x4, tap, D, 2)) for tap in range(TAPS)],
                 k.x4_low, n + 1).then_inc(k.conv4_done, 1)



def residual_load(sp, k, g, m, par):
    sp.wait_ge(k.stored[par], 16 * m)
    sp.dma_start(k.xres[:, par, :], k.src[bass.ds(g * P, P), :]).then_inc(k.res_loaded[par], 16)


def store(sp, k, g, n, par):
    sp.wait_ge(k.out_ready, n + 1)
    sp.dma_start(k.dst[bass.ds(g * P, P), :], k.xres[:, par, :]).then_inc(k.stored[par], 16)


def loads_and_stores(sp, k, groups, base):
    def step(st):
        if st.conv_a:
            conv_load(sp, k, st)
        if not isinstance(st.t, int) or st.t >= 4:
            store(sp, k, st.gl - 1, st.nl - 1, st.pa)
        if st.late:
            residual_load(sp, k, st.gl, st.ml, st.pl)
    steps(sp, groups, base, step)
    store(sp, k, groups - 1, base + groups - 1, 1)
    for par in range(2):
        sp.wait_ge(k.stored[par], 8 * (base + groups))


def turn_y(pe, nc, k, st):
    pe.wait_ge(k.y_ready, st.n + 1)
    for c in range(KC):
        mm = nc.tensor.transpose(k.pb[:, 4, c * P:(c + 1) * P], k.y[:, st.p, c * P:(c + 1) * P],
                                 k.ident[:, :])
    mm.then_inc(k.y_turned, 1)


def copy_yT(dve, nc, k, n):
    dve.wait_ge(k.y_turned, n + 1)
    nc.vector.tensor_copy(k.yT[:, :, :].rearrange("p c t -> p (c t)"),
                          k.pb[:, 4, :]).then_inc(k.yT_ready, 1)


def yT_high(act, nc, k, n):
    act.wait_ge(k.y_turned, n + 1)
    nc.scalar.copy(k.yTs[:, 0, :, :].rearrange("p c t -> p (c t)"),
                   k.pb[:, 4, :]).then_inc(k.yT_top, 1)


def yT_low(dve, nc, k, n, nf):
    dve.wait_ge(k.yT_top, nf + 1)
    nc.vector.tensor_tensor(k.yTs[:, 1, :, :].rearrange("p c t -> p (c t)"), k.pb[:, 4, :],
                            k.yTs[:, 0, :, :].rearrange("p c t -> p (c t)").bitcast(F32),
                            ALU.subtract).then_inc(k.yT_ready, 1)


def dense(nc, out, xT, w, cols=D, last=True):
    for c in range(KC):
        mm = nc.tensor.matmul(out, xT[:, c, :], w[:, c, 0:cols], start=(c == 0),
                              stop=last and c == KC - 1)
    return mm


def dense_split(nc, out, xT, w, parts, low=None, start=True, last=True):
    for m, (wpart, xpart) in enumerate(parts):
        if xpart == 1 and low is not None:
            low()
        for c in range(KC):
            mm = nc.tensor.matmul(out, xT[:, xpart, c, :], w[:, wpart, c, :],
                                  start=start and m + c == 0,
                                  stop=last and m == len(parts) - 1 and c == KC - 1)
    return mm



def conv_tiles(nc, ctx, k, tag, split_yT):
    def sb(name, shape, dt=F32):
        return ctx.enter_context(nc.sbuf_tensor(f"{name}_{tag}", shape, dt))

    k.xin = sb("xin", [P, 2, D])
    k.coef = sb("coef", [P, 2, NCOEF])
    k.x1 = sb("x1", [P, 2, D + 2], F32R)
    k.x4_full = sb("x4_full", [P, UP + 2])
    k.x12_full = sb("x12_full", [P, D])
    k.x2 = sb("x2", [P, 2, D + 2], F32R)
    k.y2 = sb("y2", [P, UP + 3])
    k.x3 = sb("x3", [P, 2, UP + 2], F32R)
    k.y3 = sb("y3", [P, UP + 4])
    k.x4 = sb("x4", [P, 2, UP + 2], F32R)
    blur = sb("blur", [P, 2, UP + 4])
    k.blur_a, k.blur_b = blur[:, 0, :], blur[:, 1, :]
    k.convw_full = blur[:, :, :].rearrange("p a n -> p (a n)")[:, 0:LAYERS * TAPS * P].rearrange(
        "p (t o) -> p t o", o=P)
    k.y = sb("y", [P, 2, D])
    if split_yT:
        k.yTs = sb("yTs", [P, 2, KC, P], F32R)
    else:
        k.yT = sb("yT", [P, KC, P])
    k.xres = sb("xres", [P, 2, D])


EDGES = 11


def zero_edges(nc, k):
    nc.vector.memset(k.convw_full, 0.0).then_inc(k.convw_zero, 1)
    for tile, cols in ((k.x1, (0, D + 1)), (k.x2, (0, D + 1)), (k.x3, (0, UP + 1))):
        for c in cols:
            nc.vector.memset(tile[:, :, c:c + 1].bitcast(F32), 0.0).then_inc(k.edges_zero, 1)
    for tile, cols in ((k.y2, (0, UP + 2)), (k.y3, (0, 1, UP + 2, UP + 3))):
        for c in cols:
            nc.vector.memset(tile[:, c:c + 1], 0.0).then_inc(k.edges_zero, 1)


def load_conv_weights(sp, k, d):
    sp.wait_ge(k.convw_zero, k.cond + 1)
    for b in range(GB):
        rows = slice(b * S, (b + 1) * S)
        sp.dma_start(k.convw_full[rows, :, rows], d["conv_w"][:, k.cond, :, :]
                     ).then_inc(k.convw_loaded, 16)


def conv_weights_high(act, nc, k):
    act.wait_ge(k.convw_loaded, 16 * GB * (k.cond + 1))
    nc.scalar.copy(k.convw[:, 0, :, :], k.convw_full).then_inc(k.convw_split, 1)


def conv_weights_low(dve, nc, k):
    dve.wait_ge(k.convw_split, 2 * k.cond + 1)
    nc.vector.tensor_tensor(k.convw[:, 1, :, :], k.convw_full,
                            k.convw[:, 0, :, :].bitcast(F32), ALU.subtract
                            ).then_inc(k.convw_split, 1)
    dve.wait_ge(k.convw_split, 2 * k.cond + 2)


def prepare(nc, k, d, groups):
    with ExitStack() as ctx:
        def sb(name, shape):
            return ctx.enter_context(nc.sbuf_tensor(name, shape, F32))

        NL = CONDS * LAYERS
        demw = sb("demw", [P, NL, TAPS, S])
        styT = sb("styT", [STYLE, groups * GB])
        modT = sb("modT", [STYLE, NL, S])
        modb = sb("modb", [P, NL])
        bias = sb("bias", [P, NL])
        demsq = sb("demsq", [P, NL, S])
        sty = sb("sty", [P, CONDS, LAYERS, groups])
        stysq = sb("stysq", [P, NL, groups])
        dem = sb("dem", [P, CONDS, LAYERS, groups])
        eps = sb("eps", [P, 1])
        ps = ctx.enter_context(nc.psum_tensor("ps_prep", [P, 5, 512], F32))
        NB = min(NL, 512 // groups)
        assert NB == NL
        s = Named()
        s.dloaded = ctx.enter_context(nc.semaphore("dloaded"))
        s.ident_ready = ctx.enter_context(nc.semaphore("ident_ready"))
        s.sty_done = ctx.enter_context(nc.semaphore("sty_done"))
        s.sty_ready = ctx.enter_context(nc.semaphore("sty_ready"))
        s.sq_done = ctx.enter_context(nc.semaphore("sq_done"))
        s.dem_done = ctx.enter_context(nc.semaphore("dem_done"))
        s.dem_root = ctx.enter_context(nc.semaphore("dem_root"))
        s.tab_done = ctx.enter_context(nc.semaphore("tab_done"))
        with nc.Block() as block:
            @block.sync
            def _(sp):
                for b in range(GB):
                    rows = slice(b * S, (b + 1) * S)
                    sp.dma_start(demw[rows, :, :, :], d["demod_w"]).then_inc(s.dloaded, 16)
                    sp.dma_start(modb[rows, :], d["mod_b"]).then_inc(s.dloaded, 16)
                    sp.dma_start(bias[rows, :], d["conv_b"]).then_inc(s.dloaded, 16)
                sp.dma_start(styT[:, :], d["style_t"]).then_inc(s.dloaded, 16)
                sp.dma_start(modT[:, :, :], d["mod_wt"]).then_inc(s.dloaded, 16)

            @block.gpsimd
            def _(pool):
                nc.gpsimd.memset(k.ones[:, :], 1.0)
                nc.gpsimd.memset(k.ident[:, :], 0.0).then_inc(s.ident_ready, 1)
                pool.wait_ge(s.ident_ready, 1)
                nc.gpsimd.affine_select(out=k.ident[:, :], in_=k.ident[:, :],
                                        compare_op=ALU.not_equal, fill=1.0, base=0,
                                        pattern=[[-1, P]], channel_multiplier=1
                                        ).then_inc(s.ident_ready, 1)

            loads = 16 * (3 * GB + 2)

            @block.tensor
            def _(pe):
                pe.wait_ge(s.dloaded, loads)
                for b in range(GB):
                    for l in range(NL):
                        mm = nc.tensor.matmul(ps[b * S:(b + 1) * S, 4, l * groups:(l + 1) * groups],
                                              modT[:, l, :], styT[:, b:GB * groups:GB],
                                              start=True, stop=True)
                mm.then_inc(s.sty_done, 1)
                pe.wait_ge(s.sty_ready, 2)
                pe.wait_ge(s.sq_done, 3)
                for b in range(GB):
                    rows = slice(b * S, (b + 1) * S)
                    for l in range(NL):
                        mm = nc.tensor.matmul(ps[rows, b, l * groups:(l + 1) * groups],
                                              demsq[rows, l, :], stysq[rows, l, :],
                                              start=True, stop=True)
                mm.then_inc(s.dem_done, 1)

            @block.scalar
            def _(act):
                act.wait_ge(s.sq_done, 4)
                act.wait_ge(s.dem_done, 1)
                for b in range(GB):
                    rows = slice(b * S, (b + 1) * S)
                    nc.scalar.activation(dem[rows, :, :, :].rearrange("p c l g -> p (c l g)"),
                                         ps[rows, b, 0:NL * groups], ACT.Sqrt,
                                         bias=eps[rows, :], scale=CONV_SCALE ** 2
                                         ).then_inc(s.dem_root, 1)

            @block.vector
            def _(dve):
                dve.wait_ge(s.dloaded, loads)
                sq = demw[:, :, :, :].rearrange("p l t o -> p (l t o)")
                nc.vector.tensor_tensor(sq, sq, sq, ALU.mult).then_inc(s.sq_done, 1)
                dve.wait_ge(s.sq_done, 1)
                nc.vector.tensor_tensor(demsq[:, :, :], demw[:, :, 0, :], demw[:, :, 1, :],
                                        ALU.add).then_inc(s.sq_done, 1)
                dve.wait_ge(s.sq_done, 2)
                nc.vector.tensor_tensor(demsq[:, :, :], demsq[:, :, :], demw[:, :, 2, :],
                                        ALU.add).then_inc(s.sq_done, 1)
                nc.vector.memset(eps[:, :], CONV_EPS).then_inc(s.sq_done, 1)
                dve.wait_ge(s.sty_done, 1)
                styf = sty[:, :, :, :].rearrange("p c l g -> p (c l) g")
                nc.vector.tensor_tensor(
                    styf, ps[:, 4, 0:NL * groups].rearrange("p (l g) -> p l g", l=NL),
                    modb[:, :].unsqueeze(2).broadcast_to([P, NL, groups]),
                    ALU.add).then_inc(s.sty_ready, 1)
                dve.wait_ge(s.sty_ready, 1)
                nc.vector.tensor_tensor(stysq[:, :, :], styf, styf, ALU.mult
                                        ).then_inc(s.sty_ready, 1)
                dve.wait_ge(s.dem_root, GB)
                dall = dem[:, :, :, :].rearrange("p c l g -> p (c l g)")
                nc.vector.reciprocal(dall, dall).then_inc(s.tab_done, 1)
                dve.wait_ge(s.tab_done, 1)
                nc.vector.tensor_scalar(dall, dall, CONV_SCALE, None, ALU.mult
                                        ).then_inc(s.tab_done, 1)
                dve.wait_ge(s.tab_done, 2)
                tab = [k.table[:, :, :, j] for j in range(NCOEF)]
                bl = [bias[:, l:CONDS * LAYERS:LAYERS].unsqueeze(2).broadcast_to([P, CONDS, groups])
                      for l in range(LAYERS)]
                st = [sty[:, :, l, :] for l in range(LAYERS)]
                dm = [dem[:, :, l, :] for l in range(LAYERS)]
                nc.vector.tensor_copy(tab[0], st[0]).then_inc(s.tab_done, 1)
                nc.vector.tensor_tensor(tab[1], dm[0], dm[1], ALU.mult).then_inc(s.tab_done, 1)
                nc.vector.tensor_tensor(tab[2], bl[0], dm[1], ALU.mult).then_inc(s.tab_done, 1)
                nc.vector.scalar_tensor_tensor(out=tab[3], in0=st[1], scalar=0.25, in1=st[2],
                                               op0=ALU.mult, op1=ALU.mult).then_inc(s.tab_done, 1)
                nc.vector.scalar_tensor_tensor(out=tab[4], in0=st[2], scalar=0.25, in1=bl[1],
                                               op0=ALU.mult, op1=ALU.mult).then_inc(s.tab_done, 1)
                nc.vector.scalar_tensor_tensor(out=tab[5], in0=dm[2], scalar=0.125, in1=st[3],
                                               op0=ALU.mult, op1=ALU.mult).then_inc(s.tab_done, 1)
                nc.vector.scalar_tensor_tensor(out=tab[6], in0=st[3], scalar=0.125, in1=bl[2],
                                               op0=ALU.mult, op1=ALU.mult).then_inc(s.tab_done, 1)
                nc.vector.tensor_copy(tab[7], dm[3]).then_inc(s.tab_done, 1)
                nc.vector.tensor_copy(tab[8], bl[3]).then_inc(s.tab_done, 1)
                dve.wait_ge(s.tab_done, 11)


def phase_attention(nc, k, d, groups, base):
    order = ("C0", "C1", "B2a", "C3a", "B2", "B0", "C3b", "C3c", "C2", "C2e", "CB", "X4H", "X4L",
             "BY", "B3", "C4", "X3H", "X3L", "B1", "BV")
    late = ("B2a", "B2", "B3")
    with ExitStack() as ctx:
        def sb(name, shape, dt=F32):
            return ctx.enter_context(nc.sbuf_tensor(name, shape, dt))

        conv_tiles(nc, ctx, k, "a0", True)
        w_full = sb("wqkv", [P, KC, D])
        w = sb("wqkv_parts", [P, 3, 2, KC, D], F32R)
        bqkv = sb("bqkv", [P, 3, D])
        yTv = sb("yTv", [P, 2, KC, P], F32R)
        qz = sb("qz", [P, 2, H // 2, 2, HD])
        kd = sb("kd", [P, H, 2, HD])
        v = sb("v", [P, H, HD])
        qT = sb("qT", [P, S, H])
        kT = sb("kT", [P, S, H])
        vT = sb("vT", [P, S, HD + 1])
        e = sb("e", [P, GB * 8, H])
        eT = sb("eT", [P, GB * 8, H])
        top = sb("top", [P, GB * 8])
        rs = sb("rs", [P, GB * 8])
        ctxh = sb("ctxh", [P, GB * 8, HD])
        ctxt = sb("ctxt", [P, H // 2, 2, HD])
        s = Named()
        s.wqkv_loaded = ctx.enter_context(nc.semaphore("wqkv_loaded"))
        s.bqkv_loaded = ctx.enter_context(nc.semaphore("bqkv_loaded"))
        s.w_split = ctx.enter_context(nc.semaphore("w_split_a0"))
        s.fixed = ctx.enter_context(nc.semaphore("fixed"))
        s.yTv_ready = ctx.enter_context(nc.semaphore("yTv_ready"))
        s.proj_done = ctx.enter_context(nc.semaphore("proj_done"))
        s.qkv_ready = ctx.enter_context(nc.semaphore("qkv_ready"))
        s.qkvT_ready = ctx.enter_context(nc.semaphore("qkvT_ready"))
        s.scores_done = ctx.enter_context(nc.semaphore("scores_done"))
        s.max_done = ctx.enter_context(nc.semaphore("max_done"))
        s.e_ready = ctx.enter_context(nc.semaphore("e_ready"))
        s.exp_done = ctx.enter_context(nc.semaphore("exp_done"))
        s.eT_ready = ctx.enter_context(nc.semaphore("eT_ready"))
        s.pv_done = ctx.enter_context(nc.semaphore("pv_done"))
        s.ctx_ready = ctx.enter_context(nc.semaphore("ctx_ready"))
        C8 = 8
        scores = k.pb[:, 0:4, 0:C8 * H].rearrange("p b (n t) -> p b n t", n=C8)
        heads = k.pb[:, 0:4, 0:C8 * (HD + 1)].rearrange("p b (n d) -> p b n d", n=C8)

        with nc.Block() as block:
            @block.sync
            def _(sp):
                load_conv_weights(sp, k, d)
                for j in range(3):
                    sp.dma_start(bqkv[:, j, :], d["b_qkv"][j:j + 1, :].broadcast_to([P, D])
                                 ).then_inc(s.bqkv_loaded, 16)
                for j in range(3):
                    if j:
                        sp.wait_ge(s.w_split, 2 * j)
                    sp.dma_start(w_full[:, :, :], d["w_qkv"][j].rearrange("(c p) n -> p c n", p=P)
                                 ).then_inc(s.wqkv_loaded, 16)

                loads_and_stores(sp, k, groups, base)

            @block.gpsimd
            def _(pool):
                def step(st):
                    for slot in order:
                        conv_pool(pool, nc, k, slot, st)
                        on, g, n, m, p = st.part(slot in late)
                        if not on or slot != "B3":
                            continue
                        pool.wait_ge(s.ctx_ready, 3 * g + 3)
                        pool.wait_ge(k.res_loaded[p], 16 * m + 16)
                        nc.gpsimd.tensor_tensor(
                            k.xres[:, p, :], ctxt[:, :, :, :].rearrange("p c h d -> p (c h d)"),
                            k.xres[:, p, :], ALU.add).then_inc(k.out_ready, 1)
                steps(pool, groups, base, step)

            @block.scalar
            def _(act):
                act.wait_ge(k.edges_zero, EDGES * (1 + k.cond))
                conv_weights_high(act, nc, k)
                for j in range(3):
                    act.wait_ge(s.wqkv_loaded, 16 * (j + 1))
                    nc.scalar.copy(w[:, j, 0, :, :], w_full[:, :, :]).then_inc(s.w_split, 1)

                def step(st):
                    for slot in order:
                        conv_act(act, nc, k, slot, st)
                        on, g, n, m, p = st.part(slot in late)
                        if not on:
                            continue
                        if slot == "BY":
                            act.wait_ge(k.yT_top, g + 1)
                            act.wait_ge(s.proj_done, 3 * g)
                            for part in range(2):
                                if part == 1:
                                    act.wait_ge(k.yT_ready, n + 1)
                                for c in range(KC):
                                    nc.scalar.copy(
                                        yTv[:, part, c, :].rearrange(
                                            "p (g q n) -> p g q n", q=GB, g=GB),
                                        k.yTs[:, part, c, :].rearrange(
                                            "p (q g n) -> p g q n", q=GB, g=GB)
                                        ).then_inc(s.yTv_ready, 1)
                        if slot == "B0":
                            yT_high(act, nc, k, n)
                        if slot == "B2":
                            act.wait_ge(s.e_ready, g + 1)
                            nc.scalar.activation(e[:, :, :], e[:, :, :], ACT.Exp,
                                                 scale=float(HD) ** -0.5).then_inc(s.exp_done, 1)
                steps(act, groups, base, step)

            @block.tensor
            def _(pe):
                pe.wait_ge(s.w_split, 6)
                pe.wait_ge(k.convw_split, 2 * k.cond + 2)

                def step(st):
                    for slot in order:
                        conv_tensor(pe, nc, k, slot, st)
                        on, g, n, m, p = st.part(slot in late)
                        if not on:
                            continue
                        if slot == "B0":
                            pe.wait_ge(s.qkv_ready, 5 * g)
                            turn_y(pe, nc, k, st)
                        if slot == "B1":
                            pe.wait_ge(k.yT_top, g + 1)
                            pe.wait_ge(s.ctx_ready, 3 * g)
                            for j in range(2):
                                dense_split(nc, k.pb[:, j, :], k.yTs, w[:, j, :, :, :], SPLIT,
                                            lambda: pe.wait_ge(k.yT_ready, n + 1)
                                            ).then_inc(s.proj_done, 1)
                            pe.wait_ge(s.yTv_ready, 2 * KC * (g + 1))
                            dense_split(nc, k.pb[:, 4, :], yTv, w[:, 2, :, :, :], SPLIT
                                        ).then_inc(s.proj_done, 1)
                        if slot in ("B2a", "B2"):
                            pe.wait_ge(s.fixed, 2)
                            pe.wait_ge(s.qkvT_ready, 3 * g + 2)
                            pe.nop(nofuse=True)
                            for i in range(C8 // 2) if slot == "B2a" else range(C8 // 2, C8):
                                for q in range(GB):
                                    for c in range(GB):
                                        rows = slice(q * S, (q + 1) * S)
                                        mm = nc.tensor.matmul(
                                            k.pb[c * S:(c + 1) * S, q, i * H:(i + 1) * H],
                                            qT[rows, c * C8 + i, :], kT[rows, c * C8 + i, :],
                                            start=True, stop=True)
                            if slot == "B2":
                                mm.then_inc(s.scores_done, 1)
                        if slot == "B3":
                            pe.wait_ge(s.fixed, 2)
                            pe.wait_ge(s.qkvT_ready, 3 * g + 3)
                            pe.wait_ge(s.eT_ready, g + 1)
                            pe.nop(nofuse=True)
                            for i in range(C8):
                                for c in range(GB):
                                    for q in range(GB):
                                        rows = slice(c * S, (c + 1) * S)
                                        mm = nc.tensor.matmul(
                                            k.pb[q * S:(q + 1) * S, c,
                                                 i * (HD + 1):(i + 1) * (HD + 1)],
                                            eT[rows, q * C8 + i, :], vT[rows, q * C8 + i, :],
                                            start=True, stop=True)
                            mm.then_inc(s.pv_done, 1)
                steps(pe, groups, base, step)

            @block.vector
            def _(dve):
                zero_edges(nc, k)
                nc.vector.memset(qz[:, :, :, :, :].rearrange("p a c h d -> p (a c h d)"), 0.0
                                 ).then_inc(s.fixed, 1)
                nc.vector.memset(vT[:, :, HD:HD + 1], 1.0).then_inc(s.fixed, 1)
                dve.wait_ge(s.fixed, 2)
                dve.wait_ge(k.edges_zero, EDGES * (1 + k.cond))
                conv_weights_low(dve, nc, k)
                for j in range(3):
                    dve.wait_ge(s.w_split, 2 * j + 1)
                    nc.vector.tensor_tensor(w[:, j, 1, :, :], w_full[:, :, :],
                                            w[:, j, 0, :, :].bitcast(F32), ALU.subtract
                                            ).then_inc(s.w_split, 1)
                dve.wait_ge(s.bqkv_loaded, 48)

                def step(st):
                    for slot in order:
                        conv_vector(dve, nc, k, slot, st)
                        on, g, n, m, p = st.part(slot in late)
                        if not on:
                            continue
                        if slot == "B0":
                            yT_low(dve, nc, k, n, g)
                        if slot == "B1":
                            dve.wait_ge(s.proj_done, 3 * g + 1)
                            qp = k.pb[:, 0, :].rearrange("p (c h d) -> p c h d", h=2, d=HD)
                            qb = bqkv[:, 0, :].rearrange("p (c h d) -> p c h d", h=2, d=HD)
                            for h in range(2):
                                nc.vector.tensor_tensor(qz[:, h, :, h, :], qp[:, :, h, :],
                                                        qb[:, :, h, :], ALU.add
                                                        ).then_inc(s.qkv_ready, 1)
                            dve.wait_ge(s.proj_done, 3 * g + 2)
                            kp = k.pb[:, 1, :].rearrange("p (t d) -> p t d", d=HD)
                            kb = bqkv[:, 1, :].rearrange("p (t d) -> p t d", d=HD)
                            for h in range(2):
                                nc.vector.tensor_tensor(kd[:, :, h, :], kp, kb, ALU.add
                                                        ).then_inc(s.qkv_ready, 1)
                            dve.wait_ge(s.qkv_ready, 5 * g + 2)
                            nc.vector.transpose(qT[:, :, :].rearrange("p n m -> p m n"),
                                                qz[:, :, :, :, :].rearrange(
                                                    "p a c h d -> p (a c) (h d)")
                                                ).then_inc(s.qkvT_ready, 1)
                            dve.wait_ge(s.qkv_ready, 5 * g + 4)
                            nc.vector.transpose(kT[:, :, :].rearrange("p n m -> p m n"),
                                                kd[:, :, :, :].rearrange("p t h d -> p t (h d)")
                                                ).then_inc(s.qkvT_ready, 1)
                        if slot == "BV":
                            dve.wait_ge(s.proj_done, 3 * g + 3)
                            nc.vector.tensor_tensor(v[:, :, :].rearrange("p t d -> p (t d)"),
                                                    k.pb[:, 4, :], bqkv[:, 2, :], ALU.add
                                                    ).then_inc(s.qkv_ready, 1)
                            dve.wait_ge(s.qkv_ready, 5 * g + 5)
                            nc.vector.transpose(vT[:, :, 0:HD].rearrange("p n d -> p d n"),
                                                v[:, :, :].rearrange("p t d -> p d t")
                                                ).then_inc(s.qkvT_ready, 1)
                        if slot == "B2":
                            dve.wait_ge(s.scores_done, g + 1)
                            top4 = top[:, :].rearrange("p (b n) -> p b n", b=GB)
                            nc.vector.tensor_reduce(top4, scores, AX.X, ALU.max
                                                    ).then_inc(s.max_done, 1)
                            dve.wait_ge(s.max_done, g + 1)
                            nc.vector.tensor_tensor(
                                e[:, :, :].rearrange("p (b n) t -> p b n t", b=GB), scores,
                                top4.unsqueeze(3).broadcast_to([P, GB, C8, H]),
                                ALU.subtract).then_inc(s.e_ready, 1)
                            dve.wait_ge(s.exp_done, g + 1)
                            nc.vector.transpose(eT[:, :, :], e[:, :, :]).then_inc(s.eT_ready, 1)
                        if slot == "B3":
                            dve.wait_ge(s.pv_done, g + 1)
                            rs4 = rs[:, :].rearrange("p (b n) -> p b n", b=GB)
                            nc.vector.reciprocal(rs4, heads[:, :, :, HD]).then_inc(s.ctx_ready, 1)
                            dve.wait_ge(s.ctx_ready, 3 * g + 1)
                            nc.vector.tensor_tensor(
                                ctxh[:, :, :].rearrange("p (b n) d -> p b n d", b=GB),
                                heads[:, :, :, 0:HD],
                                rs4.unsqueeze(3).broadcast_to([P, GB, C8, HD]),
                                ALU.mult).then_inc(s.ctx_ready, 1)
                            dve.wait_ge(s.ctx_ready, 3 * g + 2)
                            dve.wait_ge(k.out_ready, n)
                            nc.vector.transpose(
                                ctxt[:, :, :, :].rearrange("p c h d -> p d h c"),
                                ctxh[:, :, :].rearrange("p n d -> p d n")
                                ).then_inc(s.ctx_ready, 1)
                steps(dve, groups, base, step)


def phase_experts(nc, k, d, groups, base):
    order = ("C0", "G0", "G1", "C3a", "C1", "B0", "C3b", "C3c", "B2", "C2", "C2e", "CB", "X4H",
             "X4L", "B1", "X3H", "C4", "X3L", "B3")
    late = ("G0", "G1", "B2", "B3")
    with ExitStack() as ctx:
        def sb(name, shape, dt=F32):
            return ctx.enter_context(nc.sbuf_tensor(name, shape, dt))

        conv_tiles(nc, ctx, k, "f0", True)
        w_full = sb("w_full", [P, KC, D + AG + 1])
        w = sb("w_parts", [P, 2, KC, D + AG + 1], F32R)
        wb_full = sb("wb_full", [EX * RK, D])
        wb = sb("wb_parts", [P, 2, D], F32R)
        bbase = sb("bbase", [P, D])
        nbthr = sb("nbthr", [P, 1])
        gates = sb("gates", [P, EX])
        wts = sb("wts", [P, EX])
        sc = sb("sc", [P, 12])
        ntop, gsum, grec, ez, thr, wsum, wrec, empty = (sc[:, j:j + 1] for j in range(8))
        ag = sb("ag", [P, AG])
        hw = sb("hw", [P, EX, RK])
        hwT = sb("hwT", [P, 2, P], F32R)
        xb = sb("xb", [P, D])
        s = Named()
        s.wf0_loaded = ctx.enter_context(nc.semaphore("wf0_loaded"))
        s.f0_fixed = ctx.enter_context(nc.semaphore("f0_fixed"))
        s.ag_done = ctx.enter_context(nc.semaphore("ag_done"))
        s.ag_ready = ctx.enter_context(nc.semaphore("ag_ready"))
        s.ntop_ready = ctx.enter_context(nc.semaphore("ntop_ready"))
        s.gate_exp = ctx.enter_context(nc.semaphore("gate_exp"))
        s.gate_steps = ctx.enter_context(nc.semaphore("gate_steps"))
        s.hw_turned = ctx.enter_context(nc.semaphore("hw_turned"))
        s.hwT_high = ctx.enter_context(nc.semaphore("hwT_high"))
        s.hwT_ready = ctx.enter_context(nc.semaphore("hwT_ready"))
        s.w_split = ctx.enter_context(nc.semaphore("w_split"))
        s.f0_done = ctx.enter_context(nc.semaphore("f0_done"))
        s.xb_ready = ctx.enter_context(nc.semaphore("xb_ready"))
        STEPS = 12

        with nc.Block() as block:
            @block.sync
            def _(sp):
                load_conv_weights(sp, k, d)
                sp.dma_start(w_full[:, :, 0:D], d["w_base"].rearrange("(c p) n -> p c n", p=P)
                             ).then_inc(s.wf0_loaded, 16)
                sp.dma_start(w_full[:, :, D:D + AG], d["w_ag"].rearrange("(c p) n -> p c n", p=P)
                             ).then_inc(s.wf0_loaded, 16)
                sp.dma_start(wb_full[:, :], d["w_b"]).then_inc(s.wf0_loaded, 16)
                sp.dma_start(bbase[:, :], d["b_base"].broadcast_to([P, D])
                             ).then_inc(s.wf0_loaded, 16)
                sp.dma_start(nbthr[:, :], d["b_thr"].broadcast_to([P, 1])
                             ).then_inc(s.wf0_loaded, 16)

                loads_and_stores(sp, k, groups, base)

            @block.gpsimd
            def _(pool):
                pool.wait_ge(s.wf0_loaded, 80)

                def step(st):
                    for slot in order:
                        conv_pool(pool, nc, k, slot, st)
                        on, g, n, m, p = st.part(slot in late)
                        if not on or slot != "B3":
                            continue
                        pool.wait_ge(k.res_loaded[p], 16 * m + 16)
                        pool.wait_ge(k.out_ready, n)
                        nc.gpsimd.tensor_tensor(xb[:, :], k.xres[:, p, :], bbase[:, :], ALU.add
                                                ).then_inc(s.xb_ready, 1)
                steps(pool, groups, base, step)

            @block.scalar
            def _(act):
                act.wait_ge(k.edges_zero, EDGES * (1 + k.cond))
                conv_weights_high(act, nc, k)
                act.wait_ge(s.f0_fixed, 2)
                nc.scalar.copy(w[:, 0, :, :], w_full[:, :, :]).then_inc(s.w_split, 1)
                nc.scalar.copy(wb[:, 0, :], wb_full[:, :]).then_inc(s.w_split, 1)

                def step(st):
                    for slot in order:
                        conv_act(act, nc, k, slot, st)
                        on, g, n, m, p = st.part(slot in late)
                        if not on:
                            continue
                        if slot == "B0":
                            yT_high(act, nc, k, n)
                        if slot == "B1":
                            act.wait_ge(s.ag_done, g + 1)
                            act.wait_ge(s.gate_steps, STEPS * g)
                            nc.scalar.copy(ag[:, :], k.pb[:, 1, 0:AG]).then_inc(s.ag_ready, 1)
                            act.wait_ge(s.ag_ready, g + 1)
                            nc.scalar.activation(ez, ag[:, AG - 1:AG], ACT.Exp,
                                                 bias=nbthr[:, :], scale=-1.0
                                                 ).then_inc(s.gate_exp, 1)
                        if slot == "G1":
                            act.wait_ge(s.ntop_ready, 2 * g + 2)
                            nc.scalar.activation(gates[:, :], ag[:, EX * RK:AG - 1], ACT.Exp,
                                                 bias=ntop, accum_out=gsum).then_inc(s.gate_exp, 1)
                        if slot == "B2":
                            act.wait_ge(s.hw_turned, g + 1)
                            act.wait_ge(s.f0_done, g)
                            nc.scalar.copy(hwT[:, 0, :], k.pb[:, 2, 0:P]).then_inc(s.hwT_high, 1)
                steps(act, groups, base, step)

            @block.tensor
            def _(pe):
                pe.wait_ge(s.w_split, 4)
                pe.wait_ge(k.convw_split, 2 * k.cond + 2)

                def step(st):
                    for slot in order:
                        conv_tensor(pe, nc, k, slot, st)
                        on, g, n, m, p = st.part(slot in late)
                        if not on:
                            continue
                        if slot == "B0":
                            turn_y(pe, nc, k, st)
                        if slot == "B1":
                            pe.wait_ge(k.yT_top, groups + g + 1)
                            pe.wait_ge(s.gate_steps, STEPS * g)
                            dense_split(nc, k.pb[:, 1, 0:AG + 1], k.yTs, w[:, :, :, D:], SPLIT,
                                        lambda: pe.wait_ge(k.yT_ready, n + 1)
                                        ).then_inc(s.ag_done, 1)
                            pe.wait_ge(k.out_ready, n - 1)
                            dense_split(nc, k.pb[:, 3 * p, :], k.yTs, w[:, :, :, 0:D], SPLIT, last=False)
                        if slot == "B2":
                            pe.wait_ge(s.gate_steps, STEPS * g + STEPS)
                            pe.wait_ge(s.hwT_ready, g)
                            nc.tensor.transpose(k.pb[:, 2, 0:P],
                                                hw[:, :, :].rearrange("p e r -> p (e r)"),
                                                k.ident[:, :]).then_inc(s.hw_turned, 1)
                        if slot == "B3":
                            pe.wait_ge(s.hwT_ready, g + 1)
                            for wpart, xpart in SPLIT:
                                mm = nc.tensor.matmul(k.pb[:, 3 * p, :], hwT[:, xpart, :],
                                                      wb[:, wpart, :], start=False,
                                                      stop=(wpart, xpart) == SPLIT[-1])
                            mm.then_inc(s.f0_done, 1)
                steps(pe, groups, base, step)

            @block.vector
            def _(dve):
                zero_edges(nc, k)
                nc.vector.memset(w_full[:, :, D + AG:], 0.0).then_inc(s.f0_fixed, 1)
                dve.wait_ge(s.wf0_loaded, 80)
                nc.vector.tensor_scalar(nbthr[:, :], nbthr[:, :], -1.0, None, ALU.mult
                                        ).then_inc(s.f0_fixed, 1)
                dve.wait_ge(s.w_split, 2)
                nc.vector.tensor_tensor(w[:, 1, :, :], w_full[:, :, :],
                                        w[:, 0, :, :].bitcast(F32), ALU.subtract
                                        ).then_inc(s.w_split, 1)
                nc.vector.tensor_tensor(wb[:, 1, :], wb_full[:, :], wb[:, 0, :].bitcast(F32),
                                        ALU.subtract).then_inc(s.w_split, 1)
                dve.wait_ge(k.edges_zero, EDGES * (1 + k.cond))
                conv_weights_low(dve, nc, k)

                def step(st):
                    for slot in order:
                        conv_vector(dve, nc, k, slot, st)
                        on, g, n, m, p = st.part(slot in late)
                        if not on:
                            continue
                        if slot == "B0":
                            yT_low(dve, nc, k, n, groups + g)
                        v = nc.vector
                        if slot == "G0":
                            dve.wait_ge(s.ag_ready, g + 1)
                            v.tensor_reduce(ntop, ag[:, EX * RK:AG - 1], AX.X, ALU.max
                                            ).then_inc(s.ntop_ready, 1)
                            dve.wait_ge(s.ntop_ready, 2 * g + 1)
                            v.tensor_scalar(ntop, ntop, -1.0, None, ALU.mult
                                            ).then_inc(s.ntop_ready, 1)
                        if slot == "G1":
                            dve.wait_ge(s.gate_exp, 2 * g + 1)
                            v.tensor_scalar(thr, ez, 1.0, None, ALU.add).then_inc(s.gate_steps, 1)
                            dve.wait_ge(s.gate_steps, STEPS * g + 1)
                            v.reciprocal(thr, thr).then_inc(s.gate_steps, 1)
                            dve.wait_ge(s.gate_steps, STEPS * g + 2)
                            v.tensor_scalar(thr, thr, MAX_THRESHOLD, None, ALU.mult
                                            ).then_inc(s.gate_steps, 1)
                            dve.wait_ge(s.gate_exp, 2 * g + 2)
                            v.reciprocal(grec, gsum).then_inc(s.gate_steps, 1)
                            dve.wait_ge(s.gate_steps, STEPS * g + 4)
                            v.tensor_scalar(wts[:, :], gates[:, :], grec, thr, ALU.mult,
                                            ALU.subtract).then_inc(s.gate_steps, 1)
                            dve.wait_ge(s.gate_steps, STEPS * g + 5)
                            v.tensor_scalar(wts[:, :], wts[:, :], 0.0, None, ALU.max
                                            ).then_inc(s.gate_steps, 1)
                            dve.wait_ge(s.gate_steps, STEPS * g + 6)
                            v.reduce_sum(wsum, wts[:, :], AX.X).then_inc(s.gate_steps, 1)
                            dve.wait_ge(s.gate_steps, STEPS * g + 7)
                            v.tensor_scalar(empty, wsum, 0.0, None, ALU.is_equal
                                            ).then_inc(s.gate_steps, 1)
                            dve.wait_ge(s.gate_steps, STEPS * g + 8)
                            v.tensor_tensor(wsum, wsum, empty, ALU.add).then_inc(s.gate_steps, 1)
                            dve.wait_ge(s.gate_steps, STEPS * g + 9)
                            v.reciprocal(wrec, wsum).then_inc(s.gate_steps, 1)
                            dve.wait_ge(s.gate_steps, STEPS * g + 10)
                            v.tensor_scalar(wts[:, :], wts[:, :], wrec, LORA_SCALE, ALU.mult,
                                            ALU.mult).then_inc(s.gate_steps, 1)
                            dve.wait_ge(s.gate_steps, STEPS * g + 11)
                            dve.wait_ge(s.hw_turned, g)
                            v.tensor_tensor(hw[:, :, :],
                                            ag[:, 0:EX * RK].rearrange("p (e r) -> p e r", e=EX),
                                            wts[:, :].unsqueeze(2).broadcast_to([P, EX, RK]),
                                            ALU.mult).then_inc(s.gate_steps, 1)
                        if slot == "B2":
                            dve.wait_ge(s.hwT_high, g + 1)
                            nc.vector.tensor_tensor(hwT[:, 1, :], k.pb[:, 2, 0:P],
                                                    hwT[:, 0, :].bitcast(F32), ALU.subtract
                                                    ).then_inc(s.hwT_ready, 1)
                        if slot == "B3":
                            dve.wait_ge(s.f0_done, g + 1)
                            dve.wait_ge(s.xb_ready, g + 1)
                            nc.vector.tensor_tensor(k.xres[:, p, :], k.pb[:, 3 * p, :], xb[:, :],
                                                    ALU.add).then_inc(k.out_ready, 1)
                steps(dve, groups, base, step)


def prepare_latent(nc, k, d, wq1, wq2, wvo, kvln, masks):
    with ExitStack() as ctx:
        def sb(name, shape):
            return ctx.enter_context(nc.sbuf_tensor(name, shape, F32))

        wqn = sb("wqn", [NOPE, H, QR])
        wk = sb("wk", [NOPE, H, CR])
        wv = sb("wv", [VD, H, CR])
        wo = sb("wo", [VD, 2, H // 4, D])
        wpe = sb("wpe", [P, 2, H, RO])
        qln = sb("qln", [P, 2])
        s = Named()
        s.wqk_loaded = ctx.enter_context(nc.semaphore("wqk_loaded"))
        s.wv_loaded = ctx.enter_context(nc.semaphore("wv_loaded"))
        s.wpe_loaded = ctx.enter_context(nc.semaphore("wpe_loaded"))
        s.qk_done = ctx.enter_context(nc.semaphore("qk_done"))
        s.qk_high = ctx.enter_context(nc.semaphore("qk_high"))
        s.qk_ready = ctx.enter_context(nc.semaphore("qk_ready"))
        s.vo_done = ctx.enter_context(nc.semaphore("vo_done"))
        s.vo_ready = ctx.enter_context(nc.semaphore("vo_ready"))
        s.mask_done = ctx.enter_context(nc.semaphore("mask_done"))
        wo_loaded = [ctx.enter_context(nc.semaphore(f"wo_loaded_{b}")) for b in range(2)]
        HB = 512 // CR
        QH = H // 4
        chunks = ((0, P), (P, QR))
        banks = [k.pc[:, 0, :], k.pc[:, 1, :]]
        vbanks = [k.pb[:, 0, :], k.pb[:, 1, :]]
        with nc.Block() as block:
            @block.sync
            def _(sp):
                sp.dma_start(wqn[:, :, :], d["w_q_nope"]).then_inc(s.wqk_loaded, 16)
                sp.dma_start(wk[:, :, :], d["w_k"]).then_inc(s.wqk_loaded, 16)
                for at, c, (lo, hi) in ((0, 0, chunks[0]), (0, 1, chunks[1]), (QR - P, 1, chunks[1])):
                    sp.dma_start(wpe[at:at + hi - lo, c, :, :], d["w_q_pe"][lo:hi, :, :]
                                 ).then_inc(s.wpe_loaded, 16)
                    sp.dma_start(qln[at:at + hi - lo, c:c + 1], d["q_ln"][lo:hi, :]
                                 ).then_inc(s.wpe_loaded, 16)
                sp.dma_start(kvln[:, :], d["kv_ln"].broadcast_to([P, CR])).then_inc(s.wpe_loaded, 16)
                sp.dma_start(wv[:, :, :], d["w_v"]).then_inc(s.wv_loaded, 16)
                for q in range(4):
                    if q >= 2:
                        sp.wait_ge(s.vo_done, (q - 1) * QH // 2)
                    sp.dma_start(wo[:, q % 2, :, :],
                                 d["w_o"][q * QH:(q + 1) * QH, :, :].rearrange("h v n -> v h n")
                                 ).then_inc(wo_loaded[q % 2], 16)

            @block.gpsimd
            def _(pool):
                nc.gpsimd.memset(masks[:, :], 0.0).then_inc(s.mask_done, 1)
                pool.wait_ge(s.mask_done, 1)
                for b in range(GB):
                    rows = slice(b * S, (b + 1) * S)
                    nc.gpsimd.affine_select(out=masks[rows, :], in_=masks[rows, :],
                                            compare_op=ALU.is_ge, fill=MASKED, base=0,
                                            pattern=[[-1, S]], channel_multiplier=1
                                            ).then_inc(s.mask_done, 1)

            @block.tensor
            def _(pe):
                pe.wait_ge(s.wqk_loaded, 32)
                for m in range(H // HB * 2):
                    hb, c = divmod(m, 2)
                    lo, hi = chunks[c]
                    if m >= 2:
                        pe.wait_ge(s.qk_ready, m - 1)
                    for j in range(HB):
                        for at in (0,) if c == 0 else (0, QR - P):
                            mm = nc.tensor.matmul(
                                banks[m % 2][at:at + hi - lo, j * CR:(j + 1) * CR],
                                wqn[:, hb * HB + j, lo:hi], wk[:, hb * HB + j, :],
                                start=True, stop=True)
                    mm.then_inc(s.qk_done, 1)
                pe.wait_ge(s.wv_loaded, 16)
                for m in range(H // 2):
                    q = 2 * m // QH
                    pe.wait_ge(wo_loaded[q % 2], 16 * (q // 2 + 1))
                    if m >= 2:
                        pe.wait_ge(s.vo_ready, m - 1)
                    for j in range(2):
                        mm = nc.tensor.matmul(vbanks[m % 2][j * CR:(j + 1) * CR, :],
                                              wv[:, 2 * m + j, :], wo[:, q % 2, (2 * m + j) % QH, :],
                                              start=True, stop=True)
                    mm.then_inc(s.vo_done, 1)

            def pieces():
                for c in range(2):
                    yield wpe[:, c, :, :], c, slice(0, H), slice(CR, CR + RO)
                for m in range(H // HB * 2):
                    hb, c = divmod(m, 2)
                    yield (banks[m % 2].rearrange("p (h n) -> p h n", n=CR), c,
                           slice(hb * HB, (hb + 1) * HB), slice(0, CR))

            @block.scalar
            def _(act):
                act.wait_ge(s.wpe_loaded, 112)
                for m, (src, c, heads, cols) in enumerate(pieces()):
                    if m >= 2:
                        act.wait_ge(s.qk_done, m - 1)
                    dst = wq1[:, 0, heads, cols] if c == 0 else wq2[:, heads, cols]
                    nc.scalar.activation(dst, src, ACT.Copy, scale=qln[:, c:c + 1]
                                         ).then_inc(s.qk_high, 1)
                for m in range(H // 2):
                    act.wait_ge(s.vo_done, m + 1)
                    nc.scalar.copy(wvo[:, m, :], vbanks[m % 2]).then_inc(s.vo_ready, 1)

            @block.vector
            def _(dve):
                dve.wait_ge(s.wpe_loaded, 112)
                for m, (src, c, heads, cols) in enumerate(pieces()):
                    dve.wait_ge(s.qk_high, m + 1)
                    if c == 0:
                        rows, dst, high = slice(0, P), wq1[:, 1, heads, cols], wq1[:, 0, heads, cols]
                    else:
                        rows = slice(QR - P, P)
                        dst = high = wq2[rows, heads, cols]
                    mm = nc.vector.scalar_tensor_tensor(
                        out=dst, in0=src[rows], scalar=qln[rows, c:c + 1], in1=high.bitcast(F32),
                        op0=ALU.mult, op1=ALU.subtract)
                    if m >= 2:
                        mm.then_inc(s.qk_ready, 1)


def phase_latent(nc, k, d, groups, base):
    NB = 8
    LAG = 2
    order = ("C0", "B0", "C3a", "B1", "C1", "BL", "C3b", "B2", "Q0", "Q1", "Q2", "Q3", "Q4", "Q5",
             "Q6", "Q7", "C3c", "Q8", "C2", "Q9", "X4H", "B3", "X4L", "C2e", "CB", "X3H", "X3L",
             "B5", "C4", "B4")
    late = ("B5",)
    with ExitStack() as outer:
        def keep(name, shape, dt=F32):
            return outer.enter_context(nc.sbuf_tensor(name, shape, dt))

        wq1 = keep("wq1", [P, 2, H, CR + RO], F32R)
        wq2 = keep("wq2", [P, H, CR + RO], F32R)
        wvo = keep("wvo", [P, H // 2, D])
        kvln = keep("kvln", [P, CR])
        masks = keep("masks", [P, S])
        prepare_latent(nc, k, d, wq1, wq2, wvo, kvln, masks)

        ctx = outer
        sb = keep
        conv_tiles(nc, ctx, k, "a1", False)
        wa = sb("wa", [P, KC, QR + CR + RO])
        cos = sb("cos", [P, RO])
        sin = sb("sin", [P, RO])
        a = sb("a", [P, QR + CR + RO])
        junk = sb("junk", [P, QR])
        ms = sb("ms", [P, 2])
        rms = sb("rms", [P, 2])
        R2 = QR - P
        qn = sb("qn", [P, P + 2 * R2])
        kf = sb("kf", [P, CR + RO])
        t1 = sb("t1", [P, RO])
        t2 = sb("t2", [P, RO])
        qnT1 = sb("qnT1", [P, 2, P], F32R)
        qnT2 = sb("qnT2", [P, 2, P], F32R)
        kfT = sb("kfT", [P, P])
        qs = sb("qs", [P, 3, 4, CR + RO])
        r1 = sb("r1", [P, 4, RO])
        r2 = sb("r2", [P, 4, RO])
        qT = sb("mqT", [P, H // 2, P])
        sc = sb("scores", [P, H, S])
        pr = sb("probs", [P, H, S])
        prT = sb("probsT", [P, H, S])
        top = sb("mtop", [P, H])
        den = sb("mden", [P, H])
        oT = sb("oT", [P, H // 2, GB, S])
        s = Named()
        s.wa_loaded = ctx.enter_context(nc.semaphore("wa_loaded"))
        s.eps_set = ctx.enter_context(nc.semaphore("eps_set"))
        s.a_done = ctx.enter_context(nc.semaphore("a_done"))
        s.a_ready = ctx.enter_context(nc.semaphore("a_ready"))
        s.ms_ready = ctx.enter_context(nc.semaphore("ms_ready"))
        s.root_ready = ctx.enter_context(nc.semaphore("root_ready"))
        s.norm_steps = ctx.enter_context(nc.semaphore("norm_steps"))
        s.kq_turned = ctx.enter_context(nc.semaphore("kq_turned"))
        s.kqT_ready = ctx.enter_context(nc.semaphore("kqT_ready"))
        s.q_done = ctx.enter_context(nc.semaphore("q_done"))
        s.q_copied = ctx.enter_context(nc.semaphore("q_copied"))
        s.rope_steps = ctx.enter_context(nc.semaphore("rope_steps"))
        s.q_turned = ctx.enter_context(nc.semaphore("q_turned"))
        s.qT_ready = ctx.enter_context(nc.semaphore("qT_ready"))
        s.qnT_low = ctx.enter_context(nc.semaphore("qnT_low"))
        s.s_half = ctx.enter_context(nc.semaphore("s_half"))
        s.sT_done = ctx.enter_context(nc.semaphore("sT_done"))
        s.masked = ctx.enter_context(nc.semaphore("masked"))
        s.soft_steps = ctx.enter_context(nc.semaphore("soft_steps"))
        s.p_exp = ctx.enter_context(nc.semaphore("p_exp"))
        s.p_ready = ctx.enter_context(nc.semaphore("p_ready"))
        s.prT_ready = ctx.enter_context(nc.semaphore("prT_ready"))
        s.pv2_done = ctx.enter_context(nc.semaphore("pv2_done"))
        s.oT_ready = ctx.enter_context(nc.semaphore("oT_ready"))
        s.a1_done = ctx.enter_context(nc.semaphore("a1_done"))
        eps = sb("rmseps", [P, 1])
        NS = 9
        half = RO // 2

        def rotated(x):
            return x[..., half:], x[..., 0:half]

        with nc.Block() as block:
            @block.sync
            def _(sp):
                load_conv_weights(sp, k, d)
                sp.dma_start(wa[:, :, :], d["w_a"].rearrange("(c p) n -> p c n", p=P)
                             ).then_inc(s.wa_loaded, 16)
                sp.dma_start(cos[:, :], d["rope_cos"]).then_inc(s.wa_loaded, 16)
                sp.dma_start(sin[:, :], d["rope_sin"]).then_inc(s.wa_loaded, 16)

                loads_and_stores(sp, k, groups, base)

            @block.gpsimd
            def _(pool):
                def step(st):
                    for slot in order:
                        conv_pool(pool, nc, k, slot, st)
                        on, g, n, m, p = st.part(slot in late)
                        if not on or slot != "B3":
                            continue
                        pool.wait_ge(s.s_half, 2 * g + 2)
                        nc.gpsimd.tensor_tensor(sc[:, :, :], sc[:, :, :],
                                                masks[:, :].unsqueeze(1).broadcast_to([P, H, S]),
                                                ALU.add).then_inc(s.masked, 1)
                        pool.wait_ge(s.soft_steps, 4 * g + 4)
                        nc.gpsimd.tensor_tensor(pr[:, :, :], pr[:, :, :],
                                                den[:, :].unsqueeze(2).broadcast_to([P, H, S]),
                                                ALU.mult).then_inc(s.p_ready, 1)
                steps(pool, groups, base, step)

            @block.scalar
            def _(act):
                act.wait_ge(k.edges_zero, EDGES * (1 + k.cond))
                conv_weights_high(act, nc, k)
                act.wait_ge(s.eps_set, 1)

                def step(st):
                    for slot in order:
                        conv_act(act, nc, k, slot, st)
                        on, g, n, m, p = st.part(slot in late)
                        if not on:
                            continue
                        if slot == "B1":
                            act.wait_ge(s.a_done, g + 1)
                            act.wait_ge(s.norm_steps, NS * g)
                            nc.scalar.copy(a[:, :], k.pb[:, 0, 0:QR + CR + RO]
                                           ).then_inc(s.a_ready, 1)
                            act.wait_ge(s.ms_ready, 2 * g + 2)
                            for j, width in enumerate((QR, CR)):
                                nc.scalar.activation(rms[:, j:j + 1], ms[:, j:j + 1], ACT.Sqrt,
                                                     bias=eps[:, :], scale=1.0 / width
                                                     ).then_inc(s.root_ready, 1)
                        if slot == "B2":
                            act.wait_ge(s.kq_turned, 3 * g + 3)
                            nc.scalar.copy(qnT1[:, 0, :], k.pb[:, 4, 0:P]).then_inc(s.kqT_ready, 1)
                            nc.scalar.copy(qnT2[:, 0, :], k.pb[:, 4, P:2 * P]
                                           ).then_inc(s.kqT_ready, 1)
                            nc.scalar.copy(kfT[:, :], k.pb[:, 4, 2 * P:3 * P]
                                           ).then_inc(s.kqT_ready, 1)
                        if slot[0] == "Q":
                            j = int(slot[1])
                            if j < NB:
                                act.wait_ge(s.q_done, NB * g + j + 1)
                                if j >= 3:
                                    act.wait_ge(s.q_turned, NB * g + j - 2)
                                nc.scalar.copy(qs[:, j % 3, :, :],
                                               k.pb[:, j % 2, :].rearrange("p (h n) -> p h n", h=4)
                                               ).then_inc(s.q_copied, 1)
                            if j >= LAG:
                                i = j - LAG
                                act.wait_ge(s.q_turned, NB * g + i + 1)
                                act.wait_ge(s.sT_done, 2 * g + i // 4)
                                at = 4 * i % (H // 2)
                                nc.scalar.copy(qT[:, at:at + 4, :],
                                               k.pb[:, 2 + i % 2, :].rearrange(
                                                   "p (h n) -> p h n", h=4)).then_inc(s.qT_ready, 1)
                        if slot == "B3":
                            act.wait_ge(s.soft_steps, 4 * g + 2)
                            nc.scalar.activation(pr[:, :, :], pr[:, :, :], ACT.Exp,
                                                 scale=MLA_SCALE).then_inc(s.p_exp, 1)
                        if slot == "B4":
                            for b in range(0, GB, 2):
                                act.wait_ge(s.pv2_done, GB * g + b + 1)
                                nc.scalar.copy(oT[:, :, b, :],
                                               k.pb[:, b, :].rearrange("p (h s) -> p h s", s=S)
                                               ).then_inc(s.oT_ready, 1)
                steps(act, groups, base, step)

            @block.tensor
            def _(pe):
                pe.wait_ge(s.wa_loaded, 48)

                def scores_half(g, m, bank):
                    pe.wait_ge(s.qT_ready, NB * g + NB // 2 * (m + 1))
                    for b in range(GB):
                        cols = slice(b * S, (b + 1) * S)
                        mm = nc.tensor.matmul(k.pb[cols, bank, :], kfT[:, cols], qT[:, :, cols],
                                              start=True, stop=True)
                    mm.then_inc(s.sT_done, 1)

                pe.wait_ge(k.convw_split, 2 * k.cond + 2)

                def step(st):
                    for slot in order:
                        conv_tensor(pe, nc, k, slot, st)
                        on, g, n, m, p = st.part(slot in late)
                        if not on:
                            continue
                        if slot == "B0":
                            if not is_first(n):
                                pe.wait_ge(k.out_ready, n - 1)
                            turn_y(pe, nc, k, st)
                        if slot == "B1":
                            pe.wait_ge(k.yT_ready, n + 1)
                            pe.wait_ge(s.oT_ready, GB * g)
                            dense(nc, k.pb[:, 0, 0:QR + CR + RO], k.yT, wa, QR + CR + RO
                                  ).then_inc(s.a_done, 1)
                        if slot == "B2":
                            pe.wait_ge(s.norm_steps, NS * g + NS)
                            nc.tensor.transpose(k.pb[:, 4, 0:P], qn[:, 0:P], k.ident[:, :]
                                                ).then_inc(s.kq_turned, 1)
                            nc.tensor.transpose(k.pb[:, 4, P:2 * P], qn[:, P:], k.ident[:, :]
                                                ).then_inc(s.kq_turned, 1)
                            nc.tensor.transpose(k.pb[:, 4, 2 * P:3 * P], kf[:, :], k.ident[:, :]
                                                ).then_inc(s.kq_turned, 1)
                        if slot[0] == "Q":
                            j = int(slot[1])
                            if j == 0:
                                pe.wait_ge(s.kqT_ready, 3 * g + 3)
                            if 2 <= j < NB:
                                pe.wait_ge(s.q_copied, NB * g + j - 1)
                            if j < NB:
                                heads = slice(4 * j, 4 * j + 4)
                                low = slice(0, R2)
                                factors = (
                                    (qnT1[:, 0, :], wq1[:, 0, heads, :]),
                                    (qnT1[:, 0, :], wq1[:, 1, heads, :]),
                                    (qnT2[:, 0, :], wq2[:, heads, :]),
                                    (qnT1[:, 1, :], wq1[:, 0, heads, :]),
                                    (qnT2[low, 1, :], wq2[low, heads, :]))
                                for part, (lhsT, rhs) in enumerate(factors):
                                    if j == 0 and part == 3:
                                        pe.wait_ge(s.qnT_low, 2 * g + 2)
                                    mm = nc.tensor.matmul(k.pb[:, j % 2, :], lhsT,
                                                          rhs.rearrange("p h n -> p (h n)"),
                                                          start=part == 0,
                                                          stop=part == len(factors) - 1)
                                mm.then_inc(s.q_done, 1)
                            if j == LAG + 4:
                                scores_half(g, 0, 4)
                            if j >= LAG:
                                i = j - LAG
                                pe.wait_ge(s.rope_steps, 5 * (NB * g + i + 1))
                                if i >= 2:
                                    pe.wait_ge(s.qT_ready, NB * g + i - 1)
                                for h in range(4):
                                    mm = nc.tensor.transpose(
                                        k.pb[:, 2 + i % 2, h * P:(h + 1) * P], qs[:, i % 3, h, :],
                                        k.ident[:, :])
                                mm.then_inc(s.q_turned, 1)
                        if slot == "B3":
                            scores_half(g, 1, 1)
                            pe.wait_ge(s.s_half, 2 * g + 1)
                        if slot == "B4":
                            pe.wait_ge(s.prT_ready, g + 1)
                            for b in range(GB):
                                rows = slice(b * S, (b + 1) * S)
                                for hh in range(2):
                                    mm = nc.tensor.matmul(
                                        k.pb[hh * CR:(hh + 1) * CR, b, :], kf[rows, 0:CR],
                                        prT[rows, hh:H:2, :], start=True, stop=True)
                                mm.then_inc(s.pv2_done, 1)
                        if slot == "B5":
                            pe.wait_ge(s.oT_ready, GB * g + GB)
                            for m in range(H // 2):
                                mm = nc.tensor.matmul(
                                    k.pb[:, 4, :], oT[:, m, :, :].rearrange("p b s -> p (b s)"),
                                    wvo[:, m, :], start=(m == 0), stop=(m == H // 2 - 1))
                            mm.then_inc(s.a1_done, 1)
                steps(pe, groups, base, step)

            @block.vector
            def _(dve):
                zero_edges(nc, k)
                nc.vector.memset(eps[:, :], RMS_EPS).then_inc(s.eps_set, 1)
                dve.wait_ge(s.wa_loaded, 48)
                dve.wait_ge(k.edges_zero, EDGES * (1 + k.cond))
                conv_weights_low(dve, nc, k)

                def scores_turned(g, m, bank):
                    dve.wait_ge(s.sT_done, 2 * g + m + 1)
                    nc.vector.transpose(sc[:, m * H // 2:(m + 1) * H // 2, :],
                                        k.pb[:, bank, :].rearrange("p (h s) -> p h s", s=S)
                                        ).then_inc(s.s_half, 1)

                def step(st):
                    v = nc.vector
                    for slot in order:
                        conv_vector(dve, nc, k, slot, st)
                        on, g, n, m, p = st.part(slot in late)
                        if not on:
                            continue
                        if slot == "B0":
                            copy_yT(dve, nc, k, n)
                        if slot == "B1":
                            dve.wait_ge(s.a_ready, g + 1)
                            dve.wait_ge(s.norm_steps, NS * g)
                            v.tensor_tensor_reduce(out=junk[:, :], in0=a[:, 0:QR], in1=a[:, 0:QR],
                                                   scale=1.0, scalar=0.0, op0=ALU.mult,
                                                   op1=ALU.add, accum_out=ms[:, 0:1]
                                                   ).then_inc(s.ms_ready, 1)
                            dve.wait_ge(s.ms_ready, 2 * g + 1)
                            v.tensor_tensor_reduce(out=junk[:, 0:CR], in0=a[:, QR:QR + CR],
                                                   in1=a[:, QR:QR + CR], scale=1.0, scalar=0.0,
                                                   op0=ALU.mult, op1=ALU.add,
                                                   accum_out=ms[:, 1:2]).then_inc(s.ms_ready, 1)
                            pe_ = a[:, QR + CR:]
                            v.tensor_tensor(t1[:, :], pe_, cos[:, :], ALU.mult
                                            ).then_inc(s.norm_steps, 1)
                            hi, lo = rotated(pe_)
                            v.tensor_tensor(t2[:, 0:half], hi, sin[:, 0:half], ALU.mult
                                            ).then_inc(s.norm_steps, 1)
                            v.tensor_tensor(t2[:, half:], lo, sin[:, half:], ALU.mult
                                            ).then_inc(s.norm_steps, 1)
                            dve.wait_ge(s.norm_steps, NS * g + 3)
                            v.tensor_tensor(kf[:, CR:], t1[:, :], t2[:, :], ALU.add
                                            ).then_inc(s.norm_steps, 1)
                            dve.wait_ge(s.root_ready, 2 * g + 2)
                            v.reciprocal(rms[:, :], rms[:, :]).then_inc(s.norm_steps, 1)
                            dve.wait_ge(s.norm_steps, NS * g + 5)
                            v.tensor_scalar(qn[:, 0:QR], a[:, 0:QR], rms[:, 0:1], None, ALU.mult)
                            v.tensor_scalar(qn[:, QR:], a[:, P:QR], rms[:, 0:1], None, ALU.mult
                                            ).then_inc(s.norm_steps, 1)
                            v.tensor_scalar(kf[:, 0:CR], a[:, QR:QR + CR], rms[:, 1:2], None,
                                            ALU.mult).then_inc(s.norm_steps, 1)
                            dve.wait_ge(s.norm_steps, NS * g + 7)
                            v.tensor_tensor(kf[:, 0:CR], kf[:, 0:CR], kvln[:, :], ALU.mult
                                            ).then_inc(s.norm_steps, 2)
                        if slot == "BL":
                            dve.wait_ge(s.kqT_ready, 3 * g + 3)
                            for at, tile, rows in ((0, qnT1, P), (P, qnT2, R2)):
                                v.tensor_tensor(tile[0:rows, 1, :], k.pb[0:rows, 4, at:at + P],
                                                tile[0:rows, 0, :].bitcast(F32), ALU.subtract
                                                ).then_inc(s.qnT_low, 1)
                        if slot == "Q6":
                            scores_turned(g, 0, 4)
                        if slot[0] == "Q" and int(slot[1]) < NB:
                            j = int(slot[1])
                            dve.wait_ge(s.q_copied, NB * g + j + 1)
                            at = 5 * (NB * g + j)
                            dve.wait_ge(s.rope_steps, at)
                            pe_ = qs[:, j % 3, :, CR:]
                            c4 = cos[:, :].unsqueeze(1).broadcast_to([P, 4, RO])
                            v.tensor_tensor(r1[:, :, :], pe_, c4, ALU.mult
                                            ).then_inc(s.rope_steps, 1)
                            for lo in (0, half):
                                part = slice(lo, lo + half)
                                other = slice(half - lo, RO - lo)
                                v.tensor_tensor(
                                    r2[:, :, part], pe_[:, :, other],
                                    sin[:, part].unsqueeze(1).broadcast_to([P, 4, half]), ALU.mult
                                    ).then_inc(s.rope_steps, 1)
                            dve.wait_ge(s.rope_steps, at + 3)
                            v.tensor_tensor(qs[:, j % 3, :, CR:], r1[:, :, :], r2[:, :, :], ALU.add
                                            ).then_inc(s.rope_steps, 2)
                        if slot == "B3":
                            scores_turned(g, 1, 1)
                            dve.wait_ge(s.masked, g + 1)
                            v.tensor_reduce(top[:, :], sc[:, :, :], AX.X, ALU.max
                                            ).then_inc(s.soft_steps, 1)
                            dve.wait_ge(s.soft_steps, 4 * g + 1)
                            v.tensor_tensor(pr[:, :, :], sc[:, :, :],
                                            top[:, :].unsqueeze(2).broadcast_to([P, H, S]),
                                            ALU.subtract).then_inc(s.soft_steps, 1)
                            dve.wait_ge(s.p_exp, g + 1)
                            v.reduce_sum(den[:, :], pr[:, :, :], AX.X).then_inc(s.soft_steps, 1)
                            dve.wait_ge(s.soft_steps, 4 * g + 3)
                            v.reciprocal(den[:, :], den[:, :]).then_inc(s.soft_steps, 1)
                            dve.wait_ge(s.p_ready, g + 1)
                            v.transpose(prT[:, :, :], pr[:, :, :]).then_inc(s.prT_ready, 1)
                        if slot == "B4":
                            for b in range(1, GB, 2):
                                dve.wait_ge(s.pv2_done, GB * g + b + 1)
                                v.tensor_copy(oT[:, :, b, :],
                                              k.pb[:, b, :].rearrange("p (h s) -> p h s", s=S)
                                              ).then_inc(s.oT_ready, 1)
                        if slot == "B5":
                            dve.wait_ge(s.a1_done, g + 1)
                            dve.wait_ge(k.res_loaded[p], 16 * m + 16)
                            v.tensor_tensor(k.xres[:, p, :], k.pb[:, 4, :], k.xres[:, p, :],
                                            ALU.add).then_inc(k.out_ready, 1)
                steps(dve, groups, base, step)


def phase_signs(nc, k, d, groups, base):
    order = ("C0", "C3a", "C1", "B0", "C3b", "C3c", "C2", "C2e", "CB", "B3", "X4H", "X4L", "B1",
             "B4", "X3H", "C4", "X3L", "B5", "B2")
    late = ("B3", "B4", "B5")
    with ExitStack() as ctx:
        def sb(name, shape, dt=F32):
            return ctx.enter_context(nc.sbuf_tensor(name, shape, dt))

        conv_tiles(nc, ctx, k, "f1", True)
        raw = sb("raw", [P, 3, KC, D // 4], mybir.dt.int32)
        w = sb("wsign", [P, 3, 1, KC, D], F32R)
        fac = sb("fac", [P, KC])
        two = sb("two", [P, KC])
        scales = sb("scales", [P, 3])
        hid = sb("hid", [P, D])
        hT = sb("hT", [P, 2, KC, P], F32R)
        signed = ((0, 0), (0, 1))
        s = Named()
        s.signs_loaded = ctx.enter_context(nc.semaphore("signs_loaded"))
        s.fac_ready = ctx.enter_context(nc.semaphore("fac_ready"))
        s.w_ready = ctx.enter_context(nc.semaphore("w_ready"))
        s.dense_done = [ctx.enter_context(nc.semaphore(f"dense_done_{j}")) for j in range(3)]
        s.hid_ready = ctx.enter_context(nc.semaphore("hid_ready"))
        s.hid_turned = ctx.enter_context(nc.semaphore("hid_turned"))
        s.hT_high = ctx.enter_context(nc.semaphore("hT_high"))
        s.hT_ready = ctx.enter_context(nc.semaphore("hT_ready"))
        NW = 2 + 3 * KC + 1

        with nc.Block() as block:
            @block.sync
            def _(sp):
                load_conv_weights(sp, k, d)
                sp.dma_start(raw[:, :, :, :], d["k_signs"].rearrange("j (c p) n -> p j c n", p=P)
                             ).then_inc(s.signs_loaded, 16)
                sp.dma_start(scales[:, :], d["s_scales"].broadcast_to([P, 3])
                             ).then_inc(s.signs_loaded, 16)

                loads_and_stores(sp, k, groups, base)

            @block.gpsimd
            def _(pool):
                nc.gpsimd.memset(fac[:, :], 1.0).then_inc(s.fac_ready, 1)
                pool.wait_ge(s.fac_ready, 1)
                nc.gpsimd.affine_select(out=fac[:, :], in_=fac[:, :], compare_op=ALU.is_ge,
                                        fill=INH, base=EXC - 1, pattern=[[-P, KC]],
                                        channel_multiplier=-1).then_inc(s.fac_ready, 1)
                pool.wait_ge(k.edges_zero, EDGES * (1 + k.cond))

                def step(st):
                    for slot in order:
                        conv_pool(pool, nc, k, slot, st)
                steps(pool, groups, base, step)

            @block.scalar
            def _(act):
                act.wait_ge(k.edges_zero, EDGES * (1 + k.cond))
                conv_weights_high(act, nc, k)
                act.wait_ge(s.w_ready, NW)

                def step(st):
                    for slot in order:
                        conv_act(act, nc, k, slot, st)
                        on, g, n, m, p = st.part(slot in late)
                        if not on:
                            continue
                        if slot == "B0":
                            yT_high(act, nc, k, n)
                        if slot in ("B2", "B4"):
                            layer = 0 if slot == "B2" else 1
                            act.wait_ge(s.hid_turned, 2 * g + layer + 1)
                            act.wait_ge(s.dense_done[2 - layer], g + layer)
                            nc.scalar.copy(hT[:, 0, :, :].rearrange("p c t -> p (c t)"),
                                           k.pb[:, 3, :]).then_inc(s.hT_high, 1)
                        if slot in ("B1", "B3"):
                            layer = 0 if slot == "B1" else 1
                            act.wait_ge(s.dense_done[layer], g + 1)
                            act.wait_ge(s.hid_turned, 2 * g + layer)
                            nc.scalar.activation(hid[:, :], k.pb[:, layer, :], ACT.Relu,
                                                 scale=scales[:, layer:layer + 1]
                                                 ).then_inc(s.hid_ready, 1)
                steps(act, groups, base, step)

            @block.tensor
            def _(pe):
                pe.wait_ge(s.w_ready, NW)
                pe.wait_ge(k.convw_split, 2 * k.cond + 2)

                def step(st):
                    for slot in order:
                        conv_tensor(pe, nc, k, slot, st)
                        on, g, n, m, p = st.part(slot in late)
                        if not on:
                            continue
                        if slot == "B0":
                            turn_y(pe, nc, k, st)
                        if slot == "B1":
                            pe.wait_ge(k.yT_top, 2 * groups + g + 1)
                            dense_split(nc, k.pb[:, 0, :], k.yTs, w[:, 0, :, :, :], signed,
                                        lambda: pe.wait_ge(k.yT_ready, n + 1)
                                        ).then_inc(s.dense_done[0], 1)
                        if slot in ("B2", "B4"):
                            layer = 0 if slot == "B2" else 1
                            pe.wait_ge(s.hid_ready, 2 * g + layer + 1)
                            for c in range(KC):
                                mm = nc.tensor.transpose(k.pb[:, 3, c * P:(c + 1) * P],
                                                         hid[:, c * P:(c + 1) * P], k.ident[:, :])
                            mm.then_inc(s.hid_turned, 1)
                        if slot in ("B3", "B5"):
                            layer = 1 if slot == "B3" else 2
                            pe.wait_ge(s.hT_high, 2 * g + layer)
                            if slot == "B5":
                                pe.wait_ge(k.out_ready, n)
                            dense_split(nc, k.pb[:, layer, :], hT, w[:, layer, :, :, :], signed,
                                        lambda: pe.wait_ge(s.hT_ready, 2 * g + layer)
                                        ).then_inc(s.dense_done[layer], 1)
                steps(pe, groups, base, step)

            @block.vector
            def _(dve):
                zero_edges(nc, k)
                dve.wait_ge(s.signs_loaded, 32)
                dve.wait_ge(s.fac_ready, 2)
                nc.vector.tensor_scalar(two[:, :], fac[:, :], 2.0, None, ALU.mult
                                        ).then_inc(s.w_ready, 1)
                nc.vector.tensor_scalar(scales[:, 0:2], scales[:, 0:2], 2.0, None, ALU.mult
                                        ).then_inc(s.w_ready, 1)
                dve.wait_ge(s.w_ready, 2)
                for j in range(3):
                    for c in range(KC):
                        signs = raw[:, j, c, :].bitcast(U8)
                        if j == 0:
                            nc.vector.tensor_scalar(w[:, j, 0, c, :], signs, 2.0, -1.0, ALU.mult,
                                                    ALU.add).then_inc(s.w_ready, 1)
                        else:
                            nc.vector.tensor_scalar(w[:, j, 0, c, :], signs, two[:, c:c + 1],
                                                    fac[:, c:c + 1], ALU.mult, ALU.subtract
                                                    ).then_inc(s.w_ready, 1)
                dve.wait_ge(k.edges_zero, EDGES * (1 + k.cond))
                conv_weights_low(dve, nc, k)
                dve.wait_ge(s.w_ready, NW - 1)
                nc.vector.memset(two[:, :], 0.0).then_inc(s.w_ready, 1)

                def step(st):
                    for slot in order:
                        conv_vector(dve, nc, k, slot, st)
                        on, g, n, m, p = st.part(slot in late)
                        if not on:
                            continue
                        if slot == "B0":
                            yT_low(dve, nc, k, n, 2 * groups + g)
                        if slot in ("B2", "B4"):
                            layer = 0 if slot == "B2" else 1
                            dve.wait_ge(s.hT_high, 2 * g + layer + 1)
                            nc.vector.tensor_tensor(
                                hT[:, 1, :, :].rearrange("p c t -> p (c t)"), k.pb[:, 3, :],
                                hT[:, 0, :, :].rearrange("p c t -> p (c t)").bitcast(F32),
                                ALU.subtract).then_inc(s.hT_ready, 1)
                        if slot == "B5":
                            dve.wait_ge(s.dense_done[2], g + 1)
                            dve.wait_ge(k.res_loaded[p], 16 * m + 16)
                            nc.vector.scalar_tensor_tensor(
                                out=k.xres[:, p, :], in0=k.pb[:, 2, :], scalar=scales[:, 2:3],
                                in1=k.xres[:, p, :], op0=ALU.mult, op1=ALU.add
                                ).then_inc(k.out_ready, 1)
                steps(dve, groups, base, step)


PHASES = [phase_attention, phase_experts, phase_latent, phase_signs]


def program(nc, d, out, groups):
    with ExitStack() as ctx:
        k = Named()
        k.prescaled = ctx.enter_context(nc.semaphore("prescaled"))
        k.coef_ready = ctx.enter_context(nc.semaphore("coef_ready"))
        k.convw_zero = ctx.enter_context(nc.semaphore("convw_zero"))
        k.convw_loaded = ctx.enter_context(nc.semaphore("convw_loaded"))
        k.convw_split = ctx.enter_context(nc.semaphore("convw_split"))
        k.x1_high = ctx.enter_context(nc.semaphore("x1_high"))
        k.x1_low = ctx.enter_context(nc.semaphore("x1_low"))
        k.x2_high = ctx.enter_context(nc.semaphore("x2_high"))
        k.x2_low = ctx.enter_context(nc.semaphore("x2_low"))
        k.x3_high = ctx.enter_context(nc.semaphore("x3_high"))
        k.x3_low = ctx.enter_context(nc.semaphore("x3_low"))
        k.x4_high = ctx.enter_context(nc.semaphore("x4_high"))
        k.x4_low = ctx.enter_context(nc.semaphore("x4_low"))
        k.yT_top = ctx.enter_context(nc.semaphore("yT_top"))
        k.coef_b_ready = ctx.enter_context(nc.semaphore("coef_b_ready"))
        k.conv1_done = ctx.enter_context(nc.semaphore("conv1_done"))
        k.x2_ready = ctx.enter_context(nc.semaphore("x2_ready"))
        k.conv2_done = ctx.enter_context(nc.semaphore("conv2_done"))
        k.y2_ready = ctx.enter_context(nc.semaphore("y2_ready"))
        k.blur1_done = ctx.enter_context(nc.semaphore("blur1_done"))
        k.conv3_done = ctx.enter_context(nc.semaphore("conv3_done"))
        k.y3_ready = ctx.enter_context(nc.semaphore("y3_ready"))
        k.blur2_done = ctx.enter_context(nc.semaphore("blur2_done"))
        k.conv4_done = ctx.enter_context(nc.semaphore("conv4_done"))
        k.y_ready = ctx.enter_context(nc.semaphore("y_ready"))
        k.y_turned = ctx.enter_context(nc.semaphore("y_turned"))
        k.yT_ready = ctx.enter_context(nc.semaphore("yT_ready"))
        k.out_ready = ctx.enter_context(nc.semaphore("out_ready"))
        k.edges_zero = ctx.enter_context(nc.semaphore("edges_zero"))
        k.x_loaded, k.res_loaded, k.stored = (
            [ctx.enter_context(nc.semaphore(f"{name}_{par}")) for par in range(2)]
            for name in ("x_loaded", "res_loaded", "stored"))
        k.convw = ctx.enter_context(nc.sbuf_tensor("convw", [P, 2, LAYERS * TAPS, P], F32R))
        k.table = ctx.enter_context(nc.sbuf_tensor("table", [P, CONDS, groups, NCOEF], F32))
        k.ones = ctx.enter_context(nc.sbuf_tensor("ones", [P, NCOEF], F32))
        k.ident = ctx.enter_context(nc.sbuf_tensor("ident", [P, P], F32))
        prepare(nc, k, d, groups)
        k.pc = ctx.enter_context(nc.psum_tensor("pc", [P, 3, 512], F32))
        k.pb = ctx.enter_context(nc.psum_tensor("pb", [P, 5, 512], F32))
        k.src = d["x"]
        for n, phase in enumerate(PHASES):
            k.cond = n
            k.dst = out if n == len(PHASES) - 1 else \
                nc.dram_tensor(f"x_after_{n}", [groups * P, D], F32, kind="Internal").ap()
            phase(nc, k, d, groups, n * groups)
            k.src = k.dst


def kernel(**inputs):
    import concourse.bacc as bacc
    from concourse.bass_utils import run_bass_kernel_spmd

    a = {n: np.asarray(v) for n, v in inputs.items()}
    batches = a["x"].shape[0]
    conds = ("L0_cond", "L0_cond2", "L1_cond", "L1_cond2")
    cw = np.stack([a[c + "_weights"] for c in conds])
    lhs = np.stack([cw[:, l] if l == 1 else cw[:, l].transpose(0, 2, 1, 3)
                    for l in range(LAYERS)], 1)
    qb = a["L1_attn_Wq_b"].reshape(QR, H, NOPE + RO)
    kvb = a["L1_attn_Wkv_b"].reshape(CR, H, NOPE + VD)
    split = np.concatenate([np.arange(0, RO, 2), np.arange(1, RO, 2)])
    inv = np.float32(1.0) / np.float32(10000.0) ** (np.arange(0, RO, 2, dtype=np.float32) / RO)
    angle = np.outer(np.arange(S, dtype=np.float32), inv).astype(np.float32)
    cos, sin = np.cos(angle), np.sin(angle)
    host = {
        "x": a["x"].reshape(batches * S, D),
        "style_t": a["cond_512"].T,
        "conv_w": lhs.transpose(2, 0, 1, 4, 3).reshape(S, CONDS, LAYERS * TAPS, S),
        "demod_w": cw.transpose(3, 0, 1, 4, 2).reshape(S, CONDS * LAYERS, TAPS, S),
        "mod_wt": np.stack([a[c + "_mod_w"] for c in conds]).reshape(-1, S, STYLE).transpose(2, 0, 1),
        "mod_b": np.stack([a[c + "_mod_b"] for c in conds]).reshape(-1, S).T,
        "conv_b": np.stack([a[c + "_biases"] for c in conds]).reshape(-1, S).T,
        "w_qkv": np.stack([a["L0_attn_w" + j].T for j in "qkv"]),
        "b_qkv": np.stack([a["L0_attn_b" + j] for j in "qkv"]),
        "w_base": a["L0_ffn_W_base"].T,
        "b_base": a["L0_ffn_b_base"].reshape(1, D),
        "w_ag": np.concatenate([a["L0_ffn_A_w"].reshape(EX * RK, D), a["L0_ffn_W_gate"],
                                a["L0_ffn_W_thr"].reshape(1, D)]).T,
        "b_thr": a["L0_ffn_b_thr"].reshape(1, 1),
        "w_b": a["L0_ffn_B_w"].transpose(0, 2, 1).reshape(EX * RK, D),
        "w_a": np.concatenate([a["L1_attn_Wq_a"], a["L1_attn_Wkv_a"][:, :CR],
                               a["L1_attn_Wkv_a"][:, CR:][:, split]], 1),
        "q_ln": a["L1_attn_q_a_ln_w"].reshape(QR, 1),
        "kv_ln": a["L1_attn_kv_a_ln_w"].reshape(1, CR),
        "w_q_nope": qb[:, :, :NOPE].transpose(2, 1, 0),
        "w_q_pe": qb[:, :, NOPE:][:, :, split],
        "w_k": kvb[:, :, :NOPE].transpose(2, 1, 0),
        "w_v": kvb[:, :, NOPE:].transpose(2, 1, 0),
        "w_o": a["L1_attn_Wo"].reshape(H, VD, D),
        "rope_cos": np.tile(np.concatenate([cos, cos], 1), (GB, 1)),
        "rope_sin": np.tile(np.concatenate([-sin, sin], 1), (GB, 1)),
        "k_signs": np.stack([np.ascontiguousarray(a["L1_ffn_k" + j]).view(np.int32) for j in "012"]),
        "s_scales": np.stack([a["L1_ffn_s" + j] for j in "012"]).reshape(1, 3),
    }
    nc = bacc.Bacc("TRN2", target_bir_lowering=False, num_devices=1)
    arrays, dram = {}, {}
    for name, v in host.items():
        v = np.ascontiguousarray(v)
        arrays[name] = v
        dram[name] = nc.dram_tensor(name, v.shape, mybir.dt.from_np(v.dtype),
                                    kind="ExternalInput").ap()
    out = nc.dram_tensor("out", [batches * S, D], F32, kind="ExternalOutput").ap()
    program(nc, dram, out, batches // GB)
    r = run_bass_kernel_spmd(nc, [arrays], core_ids=[0])
    return r.results[0]["out"].reshape(batches, S, D)
```
